# Optimizing a Trainium2 kernel written in Bass

```python
import numpy as np
import jax
import jax.numpy as jnp

def _softmax(x, axis=-1):
    return jax.nn.softmax(x, axis=axis)

def _gelu(x):
    return jax.nn.gelu(x, approximate=True)

def _silu(x):
    return jax.nn.silu(x)

def _sigmoid(x):
    return jax.nn.sigmoid(x)

def _layernorm(x, axis=-1, eps=1e-05):
    m = jnp.mean(x, axis=axis, keepdims=True)
    v = jnp.var(x, axis=axis, keepdims=True)
    return (x - m) / jnp.sqrt(v + eps)

def _scatter_add(tgt, idx, src, axis=0):
    return tgt.at[idx].add(src)

def _segment_sum(src, seg, n):
    return jax.ops.segment_sum(src, seg, n)
kernel_name = 'mk_seq_preln_d2_jaxref_r4_8c9ef9'

def setup_inputs(seed: int=0):
    np.random.seed(seed)
    _w = jnp.asarray

    def _L0_attn_setup():
        import jax, jax.numpy as jnp
        import numpy as np
        B, L, D, H = (2, 512, 256, 16)
        Dh = D // H
        key = jax.random.key(seed)
        kx, kq, kk, kv, ko = jax.random.split(key, 5)
        scale = 1.0 / np.sqrt(D)
        return {'x': jax.random.normal(kx, (B, L, D), dtype=jnp.float32), 'Wq': jax.random.normal(kq, (D, H, Dh), dtype=jnp.float32) * scale, 'Wk': jax.random.normal(kk, (D, H, Dh), dtype=jnp.float32) * scale, 'Wv': jax.random.normal(kv, (D, H, Dh), dtype=jnp.float32) * scale, 'Wout': jax.random.normal(ko, (H, Dh, D), dtype=jnp.float32) * (1.0 / np.sqrt(D))}
    _L0_attn_in = _L0_attn_setup()

    def _L0_ffn_setup():
        import jax, jax.numpy as jnp
        import numpy as np
        B, S, D, O, E, K = (4, 512, 256, 256, 8, 2)
        key = jax.random.key(seed)
        ks = jax.random.split(key, 5)
        scale_in = 1.0 / np.sqrt(D)
        x = jax.random.normal(ks[0], (B, S, D), dtype=jnp.float32)
        gate_w = jax.random.uniform(ks[1], (E, D), jnp.float32, -scale_in, scale_in)
        gate_b = jax.random.uniform(ks[2], (E,), jnp.float32, -scale_in, scale_in)
        expert_w = jax.random.uniform(ks[3], (E, D, O), jnp.float32, -scale_in, scale_in)
        expert_b = jax.random.uniform(ks[4], (E, O), jnp.float32, -scale_in, scale_in)
        return {'x': x, 'gate_w': gate_w, 'gate_b': gate_b, 'expert_w': expert_w, 'expert_b': expert_b}
    _L0_ffn_in = _L0_ffn_setup()

    def _L1_attn_setup():
        import jax, jax.numpy as jnp
        import numpy as np
        EMBED_DIM = 256
        NUM_HEADS = 16
        HEAD_DIM = EMBED_DIM // NUM_HEADS
        NUM_LANDMARKS = 64
        REG = 1e-06
        BATCH = 2
        SEQ = 2048

        def _sq_dists(X, L):
            Xn = jnp.sum(X * X, axis=-1, keepdims=True)
            Ln = jnp.sum(L * L, axis=-1, keepdims=True)
            XL = jnp.einsum('bhnd,bhkd->bhnk', X, L)
            return jnp.maximum(Xn + jnp.swapaxes(Ln, -2, -1) - 2.0 * XL, 0.0)
        key = jax.random.key(seed)
        ks = jax.random.split(key, 10)
        s = 0.02
        inp = {'query': jax.random.normal(ks[0], (BATCH, SEQ, EMBED_DIM), dtype=jnp.float32), 'Wq': jax.random.normal(ks[1], (EMBED_DIM, EMBED_DIM), dtype=jnp.float32) * s, 'bq': jnp.zeros((EMBED_DIM,), jnp.float32), 'Wk': jax.random.normal(ks[2], (EMBED_DIM, EMBED_DIM), dtype=jnp.float32) * s, 'bk': jnp.zeros((EMBED_DIM,), jnp.float32), 'Wv': jax.random.normal(ks[3], (EMBED_DIM, EMBED_DIM), dtype=jnp.float32) * s, 'bv': jnp.zeros((EMBED_DIM,), jnp.float32), 'Wo': jax.random.normal(ks[4], (EMBED_DIM, EMBED_DIM), dtype=jnp.float32) * s, 'bo': jnp.zeros((EMBED_DIM,), jnp.float32), 'temperature': jnp.asarray(float(HEAD_DIM), jnp.float32), 'landmark_idx': jnp.arange(NUM_LANDMARKS, dtype=jnp.int32) * (SEQ // NUM_LANDMARKS)}
        return inp
    _L1_attn_in = _L1_attn_setup()

    def _L1_ffn_setup():
        import jax, jax.numpy as jnp
        import numpy as np
        key = jax.random.key(seed)
        kx, kw = jax.random.split(key)
        x = jax.random.normal(kx, (32, 1024, 256), dtype=jnp.float32)
        weight = jax.random.normal(kw, (256, 256), dtype=jnp.float32) * 0.01
        return {'x': x, 'weight': weight}
    _L1_ffn_in = _L1_ffn_setup()
    _d = {'L0_attn_x': _L0_attn_in['x'], 'L0_attn_Wq': _L0_attn_in['Wq'], 'L0_attn_Wk': _L0_attn_in['Wk'], 'L0_attn_Wv': _L0_attn_in['Wv'], 'L0_attn_Wout': _L0_attn_in['Wout'], 'L0_ffn_gate_w': _L0_ffn_in['gate_w'], 'L0_ffn_gate_b': _L0_ffn_in['gate_b'], 'L0_ffn_expert_w': _L0_ffn_in['expert_w'], 'L0_ffn_expert_b': _L0_ffn_in['expert_b'], 'L1_attn_Wq': _L1_attn_in['Wq'], 'L1_attn_bq': _L1_attn_in['bq'], 'L1_attn_Wk': _L1_attn_in['Wk'], 'L1_attn_bk': _L1_attn_in['bk'], 'L1_attn_Wv': _L1_attn_in['Wv'], 'L1_attn_bv': _L1_attn_in['bv'], 'L1_attn_Wo': _L1_attn_in['Wo'], 'L1_attn_bo': _L1_attn_in['bo'], 'L1_attn_temperature': _L1_attn_in['temperature'], 'L1_attn_landmark_idx': _L1_attn_in['landmark_idx'], 'L1_ffn_weight': _L1_ffn_in['weight']}
    _x0 = _d['L0_attn_x']
    _d['L0_attn_x'] = jax.random.normal(jax.random.fold_in(jax.random.key(seed), 1), (1, 4096, 256), dtype=_x0.dtype)
    del _x0
    return _d

def reference(L0_attn_x, L0_attn_Wq, L0_attn_Wk, L0_attn_Wv, L0_attn_Wout, L0_ffn_gate_w, L0_ffn_gate_b, L0_ffn_expert_w, L0_ffn_expert_b, L1_attn_Wq, L1_attn_bq, L1_attn_Wk, L1_attn_bk, L1_attn_Wv, L1_attn_bv, L1_attn_Wo, L1_attn_bo, L1_attn_temperature, L1_attn_landmark_idx, L1_ffn_weight):

    def _L0_attn_ref(x, Wq, Wk, Wv, Wout):
        import jax, jax.numpy as jnp
        import numpy as np
        B, L, D, H = (2, 512, 256, 16)
        Dh = D // H
        q = jnp.einsum('bld,dhe->blhe', x, Wq)
        k = jnp.einsum('bld,dhe->blhe', x, Wk)
        v = jnp.einsum('bld,dhe->blhe', x, Wv)
        a = jnp.einsum('bqhd,bkhd->bhqk', q, k) / Dh ** 0.5
        Lq = x.shape[1]
        mask = jnp.tril(jnp.ones((1, 1, Lq, Lq), dtype=jnp.bool_))
        NEG_INF = jnp.finfo(jnp.float32).min
        a = jnp.where(mask, a, NEG_INF)
        a = jax.nn.softmax(a, axis=-1)
        o = jnp.einsum('bhqk,bkhd->bqhd', a, v)
        return jnp.einsum('blhe,hed->bld', o, Wout)

    def _L0_ffn_ref(x, gate_w, gate_b, expert_w, expert_b):
        import jax, jax.numpy as jnp
        import numpy as np
        B, S, D, O, E, K = (4, 512, 256, 256, 8, 2)
        logits = jnp.einsum('bsd,ed->bse', x, gate_w) + gate_b
        if K < E:
            topv, topi = jax.lax.top_k(logits, K)
            keep = jax.nn.one_hot(topi, E, dtype=jnp.float32).sum(axis=-2)
            logits = jnp.where(keep > 0, logits, -jnp.inf)
        gate_score = jax.nn.softmax(logits, axis=-1)
        expert_out = jnp.einsum('bsd,edo->bseo', x, expert_w) + expert_b
        out = jnp.einsum('bseo,bse->bso', expert_out, gate_score)
        return out

    def _L1_attn_ref(query, Wq, bq, Wk, bk, Wv, bv, Wo, bo, temperature, landmark_idx):
        import jax, jax.numpy as jnp
        import numpy as np
        EMBED_DIM = 256
        NUM_HEADS = 16
        HEAD_DIM = EMBED_DIM // NUM_HEADS
        NUM_LANDMARKS = 64
        REG = 1e-06
        BATCH = 2
        SEQ = 2048

        def _sq_dists(X, L):
            Xn = jnp.sum(X * X, axis=-1, keepdims=True)
            Ln = jnp.sum(L * L, axis=-1, keepdims=True)
            XL = jnp.einsum('bhnd,bhkd->bhnk', X, L)
            return jnp.maximum(Xn + jnp.swapaxes(Ln, -2, -1) - 2.0 * XL, 0.0)
        b, n, _ = query.shape
        Q = (query @ Wq.T + bq).reshape(b, n, NUM_HEADS, HEAD_DIM).transpose(0, 2, 1, 3)
        K = (query @ Wk.T + bk).reshape(b, n, NUM_HEADS, HEAD_DIM).transpose(0, 2, 1, 3)
        V = (query @ Wv.T + bv).reshape(b, n, NUM_HEADS, HEAD_DIM).transpose(0, 2, 1, 3)
        landmarks = K[:, :, landmark_idx, :]
        C_Q = _sq_dists(Q, landmarks)
        C_K = _sq_dists(K, landmarks)
        W_sq = C_K[:, :, landmark_idx, :]
        Phi_Q = jnp.exp(-C_Q / temperature)
        Phi_K = jnp.exp(-C_K / temperature)
        W_kernel = jnp.exp(-W_sq / temperature) + REG * jnp.eye(NUM_LANDMARKS, dtype=query.dtype)
        Z = jnp.einsum('bhnk,bhnd->bhkd', Phi_K, V)
        Y = jnp.linalg.solve(W_kernel, Z)
        out_unnorm = jnp.einsum('bhnk,bhkd->bhnd', Phi_Q, Y)
        Phi_K_sum = jnp.sum(Phi_K, axis=-2)[..., None]
        norm = jnp.einsum('bhnk,bhko->bhno', Phi_Q, jnp.linalg.solve(W_kernel, Phi_K_sum))
        norm = jnp.maximum(norm, 1e-10)
        out = out_unnorm / norm
        out = out.transpose(0, 2, 1, 3).reshape(b, n, EMBED_DIM)
        return out @ Wo.T + bo

    def _L1_ffn_ref(x, weight):
        import jax, jax.numpy as jnp
        import numpy as np
        b_weight = jnp.sign(weight)
        return jnp.einsum('bsi,oi->bso', x, b_weight)
    x = L0_attn_x
    x = x + _L0_attn_ref(_layernorm(x, axis=-1), L0_attn_Wq, L0_attn_Wk, L0_attn_Wv, L0_attn_Wout)
    x = x + _L0_ffn_ref(_layernorm(x, axis=-1), L0_ffn_gate_w, L0_ffn_gate_b, L0_ffn_expert_w, L0_ffn_expert_b)
    x = x + _L1_attn_ref(_layernorm(x, axis=-1), L1_attn_Wq, L1_attn_bq, L1_attn_Wk, L1_attn_bk, L1_attn_Wv, L1_attn_bv, L1_attn_Wo, L1_attn_bo, L1_attn_temperature, L1_attn_landmark_idx)
    x = x + _L1_ffn_ref(_layernorm(x, axis=-1), L1_ffn_weight)
    return x

_drawn_inputs = setup_inputs


def setup_inputs(seed=0):
    import zlib

    import numpy as np

    out = dict(_drawn_inputs(seed))
    spreads = {'L1_attn_bq': (0.0, 0.8),
     'L1_attn_bk': (0.0, 0.8),
     'L1_attn_bv': (0.0, 0.285),
     'L1_attn_bo': (0.0, 0.1)}
    factors = {'L1_attn_Wq': 8.0, 'L1_attn_Wk': 8.0, 'L1_attn_Wv': 8.0}
    for name, (base, spread) in spreads.items():
        noise = np.random.default_rng([zlib.crc32(name.encode()), seed]).standard_normal(out[name].shape)
        drawn = base * np.exp(spread * noise) if base else spread * noise
        out[name] = jnp.asarray(drawn.astype(out[name].dtype))
    for name, factor in factors.items():
        out[name] = (out[name] * factor).astype(out[name].dtype)
    return out
```

```python
from contextlib import ExitStack

import concourse.bass as bass
from concourse import mybir

F32 = mybir.dt.float32
BF16 = mybir.dt.bfloat16
I32 = mybir.dt.int32
ALU = mybir.AluOpType
ACT = mybir.ActivationFunctionType
AX = mybir.AxisListType.X

P = 128
N = 4096
D = 256
DC = D // P
H = 16
DH = D // H
T = 512
NT = N // T
SUB = T // P
G = 4
NG = H // G
E = 8
TOP = 2
M = 64
PAIRS = H // 2
LN_EPS = 1e-5
REG = 1e-6
NORM_MIN = 1e-10
MASKED = -3.0e38


def stage_sems(ctx, nc, stage, names):
    return {n: ctx.enter_context(nc.semaphore(f"{stage}_{n}")) for n in names}


def loop_sems(pool, names):
    assert len(names) <= len(pool)
    return dict(zip(names, pool))


def cleared(sems):
    nums = [s.num for s in sems.values()]
    return range(min(nums), max(nums) + 1)


LOOP_SEMS = 52


class Chain:

    def __init__(self, eng, sem):
        self.eng, self.sem, self.n = eng, sem, 0

    def step(self, ins):
        ins.then_inc(self.sem, 1)
        self.n += 1

    def wait(self):
        self.eng.wait_ge(self.sem, self.n)

    def link(self, ins):
        self.step(ins)
        self.wait()


def bc(ap, axis, shape):
    return ap.unsqueeze(axis).broadcast_to(shape)



def ln_stats(dve, ch, x, st, mv, s_var):
    for s in range(SUB):
        ch.step(dve.bn_stats(st[:, s, :], x[:, s, :]))
    ch.wait()
    for s in range(SUB):
        dve.bn_aggr(mv[:, s, :], st[:, s, :]).then_inc(s_var, 1)


def ln_rstd(pool, ch, mv, rstd, neghalf, s_var, n_var, s_rstd):
    pool.wait_ge(s_var, n_var)
    ch.link(pool.tensor_scalar(rstd[:, :], mv[:, :, 1], LN_EPS, None, ALU.add))
    pool.tensor_tensor(rstd[:, :], rstd[:, :], neghalf[:, 0:SUB], ALU.pow).then_inc(s_rstd, 1)


def ln_apply(dve, x, xn, mv, rstd, s_rstd, n_rstd, s_xn):
    dve.wait_ge(s_rstd, n_rstd)
    for s in range(SUB):
        dve.tensor_scalar(xn[:, s, :], x[:, s, :], mv[:, s, 0:1], rstd[:, s:s + 1],
                          ALU.subtract, ALU.mult).then_inc(s_xn, 1)


def transpose_tile(pe, ps, bank, xn, ident, s_xn, n_xn, s_ps):
    for s in range(SUB):
        pe.wait_ge(s_xn, n_xn + s + 1)
        for c in range(DC):
            last = pe.transpose(ps[:, bank + c, s * P:(s + 1) * P], xn[:, s, c * P:(c + 1) * P], ident[:, :])
    last.then_inc(s_ps, 1)



def setup(nc, io, k, ps):
    names = ["w_in", "sgn_in", "gate_in", "small_in", "pool", "dve", "id_ok", "tr_ps", "tr_sb", "sgn"]
    with ExitStack() as ctx:
        sem = stage_sems(ctx, nc, "setup", names)
        raw = ctx.enter_context(nc.sbuf_tensor("raw", [P, 5, DC, D], F32))
        sgn = ctx.enter_context(nc.sbuf_tensor("sgn", [P, DC, D], F32))
        neg = ctx.enter_context(nc.sbuf_tensor("neg", [P, DC, D], F32))
        graw = ctx.enter_context(nc.sbuf_tensor("graw", [E, D], F32))
        zeros = ctx.enter_context(nc.sbuf_tensor("zeros", [P, 8, P], F32))
        idx = ctx.enter_context(nc.sbuf_tensor("idx", [P, M], I32))
        under = ctx.enter_context(nc.sbuf_tensor("under", [P, M], F32))
        m8 = ctx.enter_context(nc.sbuf_tensor("m8", [P, 8], F32))
        i8 = ctx.enter_context(nc.sbuf_tensor("i8", [P, 8, 8], F32))
        weights = [("L1_attn_Wq", k.wq1), ("L1_attn_Wk", k.wk1), ("L1_attn_Wv", k.wv1), ("L1_attn_Wo", k.wo1),
                   ("L1_ffn_weight", k.wf)]
        with nc.Block() as block:
            @block.sync
            def _(sp):
                for i, (name, _) in enumerate(weights):
                    sp.dma_start(raw[:, i], io[name].rearrange("(c p) n -> p c n", p=P)).then_inc(sem["w_in"], 16)
                sp.dma_start(graw[:, :], io["L0_ffn_gate_w"]).then_inc(sem["gate_in"], 16)
                for tile, ap in ((k.bq1, io["L1_attn_bq"]), (k.bk1, io["L1_attn_bk"])):
                    sp.dma_start(tile[:, :], ap.rearrange("(c p) -> p c", p=P),
                                 allow_slow_non_contiguous=True).then_inc(sem["small_in"], 16)
                for tile, ap in ((k.bv1, io["L1_attn_bv"]), (k.bo1, io["L1_attn_bo"]), (k.gate_b, io["L0_ffn_gate_b"]),
                                 (idx, io["L1_attn_landmark_idx"]), (k.negt, io["L1_attn_temperature"])):
                    sp.dma_start(tile[:, :], ap.partition_broadcast(P)).then_inc(sem["small_in"], 16)

            @block.gpsimd
            def _(pool):
                ch = Chain(pool, sem["pool"])
                for tile, v in ((zeros, 0.0), (k.neghalf, -0.5), (k.ones, 1.0), (k.blk2, -2.0), (k.headmask, 1.0),
                                (k.sel, 1.0), (k.quarter, 0.25), (k.half, 0.0)):
                    ch.link(pool.memset(tile[:], v))
                ch.link(pool.memset(k.blk1[:], 0.0))
                ch.wait()
                ch.link(pool.memset(k.half[0:64, 0:1], 1.0))
                ch.link(pool.memset(k.half[64:128, 1:2], 1.0))
                z = zeros[:, 0, :]
                pool.affine_select(out=k.ident[:, :], in_=z, pattern=[[-1, P]], compare_op=ALU.not_equal, fill=1.0,
                                   base=0, channel_multiplier=1).then_inc(sem["id_ok"], 1)
                pool.wait_ge(sem["id_ok"], 1)
                ch.link(pool.affine_select(out=k.identb[:, :], in_=z, pattern=[[-1, P]], compare_op=ALU.not_equal,
                                           fill=1.0, base=0, channel_multiplier=1))
                ch.link(pool.affine_select(out=k.mask_kq[:, :], in_=z, pattern=[[1, P]], compare_op=ALU.is_ge,
                                           fill=MASKED, base=0, channel_multiplier=-1))
                ch.link(pool.affine_select(out=k.mask_qk[:, :], in_=z, pattern=[[-1, P]], compare_op=ALU.is_ge,
                                           fill=MASKED, base=0, channel_multiplier=1))
                for tile, pat, rows in ((k.sel, [[-DH, 32]], 64), (k.blk2, [[-DH, G], [0, M]], 64),
                                        (k.headmask, [[-DH, 8], [0, M]], P)):
                    ch.link(pool.affine_select(out=tile[:], in_=tile[:], pattern=pat, compare_op=ALU.is_ge,
                                               fill=0.0, base=0, channel_multiplier=1))
                    ch.link(pool.affine_select(out=tile[:], in_=tile[:], pattern=[[-s, n] for s, n in pat],
                                               compare_op=ALU.is_ge, fill=0.0, base=DH - 1, channel_multiplier=-1))
                ch.link(pool.affine_select(out=k.blk1[64:96], in_=k.blk1[64:96], pattern=[[-1, G], [0, M]],
                                           compare_op=ALU.not_equal, fill=1.0, base=0, channel_multiplier=1))
                ch.link(pool.affine_select(out=k.regi[:, :], in_=z[0:M, 0:M], pattern=[[-1, M]],
                                           compare_op=ALU.not_equal, fill=REG, base=0, channel_multiplier=1))
                ch.link(pool.affine_select(out=k.before[:, :, :], in_=zeros[:, 0, 0:64].rearrange("p (a b) -> p a b", a=8),
                                           pattern=[[-1, E], [1, E]], compare_op=ALU.is_ge, fill=1.0, base=0,
                                           channel_multiplier=0))
                ch.link(pool.affine_select(out=k.spread[:, :, :], in_=zeros[:, :, :].rearrange("p c (h r) -> p c h r", r=8),
                                           pattern=[[-1, 8], [-8, H], [0, 8]], compare_op=ALU.not_equal, fill=1.0,
                                           base=0, channel_multiplier=1))
                ch.link(pool.affine_select(out=i8[:, :, :], in_=zeros[:, 0, 0:64].rearrange("p (a b) -> p a b", a=8),
                                           pattern=[[-1, 8], [1, 8]], compare_op=ALU.not_equal, fill=1.0, base=0,
                                           channel_multiplier=0))
                ch.link(pool.affine_select(out=k.unit[:, :], in_=zeros[:, 0, 0:2 * M - 1], pattern=[[1, 2 * M - 1]],
                                           compare_op=ALU.not_equal, fill=1.0, base=1 - M, channel_multiplier=0))
                ch.link(pool.iota(k.tok[:, :], pattern=[[P, SUB]], base=0, channel_multiplier=1,
                                  allow_small_or_imprecise_dtypes=True))
                ch.wait()
                pool.engine_nop().then_inc(sem["id_ok"], 1)

            @block.tensor
            def _(pe):
                pe.wait_ge(sem["id_ok"], 1)
                pe.wait_ge(sem["w_in"], 80)
                for i in range(5):
                    src = sgn if i == 4 else raw[:, i]
                    if i == 4:
                        pe.wait_ge(sem["sgn"], 1)
                    if i >= 2:
                        pe.wait_ge(sem["tr_sb"], i - 1)
                    for oc in range(DC):
                        for ic in range(DC):
                            last = pe.transpose(ps[:, 2 * (i % 2) + ic, oc * P:(oc + 1) * P],
                                                src[:, oc, ic * P:(ic + 1) * P], k.ident[:, :])
                    last.then_inc(sem["tr_ps"], 1)
                pe.wait_ge(sem["gate_in"], 16)
                for ic in range(DC):
                    last = pe.transpose(ps[:, 4, ic * E:(ic + 1) * E], graw[:, ic * P:(ic + 1) * P],
                                        k.ident[0:E, 0:E])
                last.then_inc(sem["tr_ps"], 1)

            @block.vector
            def _(dve):
                ch = Chain(dve, sem["dve"])
                dve.wait_ge(sem["w_in"], 80)
                ch.step(dve.tensor_scalar(sgn[:], raw[:, 4], 0.0, None, ALU.is_gt))
                ch.step(dve.tensor_scalar(neg[:], raw[:, 4], 0.0, None, ALU.is_lt))
                ch.wait()
                dve.tensor_tensor(sgn[:], sgn[:], neg[:], ALU.subtract).then_inc(sem["sgn"], 1)
                for i, (_, dst) in enumerate(weights):
                    dve.wait_ge(sem["tr_ps"], i + 1)
                    b = 2 * (i % 2)
                    dve.tensor_copy(dst[:, :, :], ps[:, b:b + DC, 0:D]).then_inc(sem["tr_sb"], 1)
                dve.wait_ge(sem["tr_ps"], 6)
                ch.step(dve.tensor_copy(k.gate_w[:, :, :], ps[:, 4, 0:DC * E].rearrange("p (c e) -> p c e", c=DC)))
                dve.wait_ge(sem["small_in"], 16 * 7)
                ch.link(dve.tensor_copy(k.idx[:, :], idx[:, :]))
                ch.link(dve.tensor_scalar(under[:, :], k.idx[:, :], 0.0, float(N), ALU.is_lt, ALU.mult))
                ch.link(dve.tensor_tensor(k.idx[:, :], k.idx[:, :], under[:, :], ALU.add))
                ch.step(dve.tensor_scalar(k.idx[:, :], k.idx[:, :], 0.0, float(N - 1), ALU.max, ALU.min))
                ch.link(dve.reciprocal(k.negt[:, :], k.negt[:, :]))
                ch.step(dve.tensor_scalar(k.negt[:, :], k.negt[:, :], -1.0, None, ALU.mult))
                dve.wait_ge(sem["id_ok"], 2)
                ch.link(dve.tensor_reduce(m8[:, :], k.spread[:, :, :], AX, ALU.max))
                ch.step(dve.tensor_tensor(k.own[:, :].rearrange("p (a b c) -> p a b c", a=8, b=8),
                                          bc(bc(m8[:, :], 2, [P, 8, 8]), 3, [P, 8, 8, 8]),
                                          bc(i8[:, :, :], 1, [P, 8, 8, 8]), ALU.mult))



def project(nc, io, k, ps, scr):
    names = ["x_in", "w_in", "dve", "pool", "var", "rstd", "xn", "xt_ps", "xt", "qk_ps", "v_ps", "p1", "rest", "p2", "p3",
             "v", "out", "one"]
    with ExitStack() as ctx:
        sb = lambda n, shape, dt=F32: ctx.enter_context(nc.sbuf_tensor(n, shape, dt))
        wsem = stage_sems(ctx, nc, "projw", ["in_", "ones"])
        sem = loop_sems(k.loop_sems, names)
        w = sb("w_qkv", [P, 3, DC, D])
        x = sb("x_a", [P, SUB, D])
        xn = sb("xn_a", [P, SUB, D])
        st = sb("st_a", [P, SUB, 6])
        mv = sb("mv_a", [P, SUB, 2])
        rstd = sb("rstd_a", [P, SUB])
        xt = sb("xt_a", [P, DC, T])
        part = sb("part", [P, 2, 3, DC, T], BF16)
        rest = sb("rest", [P, 4, T])
        v = sb("v_a", [P, SUB, H, 2 * DH])
        with nc.Block() as block:
            @block.sync
            def _(sp):
                for i, name in enumerate(("L0_attn_Wq", "L0_attn_Wk", "L0_attn_Wv")):
                    sp.dma_start(w[:, i], io[name].rearrange("(c p) h e -> p c (h e)", p=P)).then_inc(wsem["in_"], 16)
                sp.wait_ge(wsem["in_"], 48)

            @block.gpsimd
            def _(pool):
                pool.memset(v[:, :, :, DH:2 * DH], 1.0).then_inc(wsem["ones"], 1)
                pool.wait_ge(wsem["ones"], 1)
        with nc.Fori(0, NT) as i:
            with nc.Block() as block:
                @block.sync
                def _(sp):
                    sp.dma_start(x[:], io["L0_attn_x"].rearrange("o (i s p) d -> (o i) p s d", s=SUB, p=P)[i]).then_inc(sem["x_in"], 16)
                    for a, dst in ((0, scr.q), (1, scr.k)):
                        sp.wait_ge(sem["p3"], 2 * (a + 1))
                        sp.wait_ge(sem["p2"], 2 * (a + 1))
                        sp.wait_ge(sem["p1"], 2 * (a + 1))
                        for n in range(3):
                            sp.dma_start(dst.rearrange("a (c p) (i n) -> i a p c n", c=DC, n=T)[i, n],
                                         part[:, a, n]).then_inc(sem["out"], 16)
                    sp.wait_ge(sem["v"], 1)
                    sp.dma_start(scr.v.rearrange("(i s p) n -> i p s n", s=SUB, p=P)[i],
                                 v[:].rearrange("p s h e -> p s (h e)")).then_inc(sem["out"], 16)
                    sp.wait_ge(sem["out"], 16 * 7)

                @block.vector
                def _(dve):
                    ch = Chain(dve, sem["dve"])
                    dve.wait_ge(sem["x_in"], 16)
                    ln_stats(dve, ch, x, st, mv, sem["var"])
                    ln_apply(dve, x, xn, mv, rstd, sem["rstd"], 1, sem["xn"])
                    for o in range(4):
                        a, c = o // DC, o % DC
                        dve.wait_ge(sem["p1"], o + 1)
                        dve.scalar_tensor_tensor(out=rest[:, o, :], in0=ps[:, 2 + o, :], scalar=(DH ** -0.5, 1.0)[a],
                                                 in1=part[:, a, 0, c, :], op0=ALU.mult, op1=ALU.subtract).then_inc(sem["rest"], 1)

                @block.gpsimd
                def _(pool):
                    ch = Chain(pool, sem["pool"])
                    ln_rstd(pool, ch, mv, rstd, k.neghalf, sem["var"], SUB, sem["rstd"])
                    for o in range(4):
                        a, c = o // DC, o % DC
                        pool.wait_ge(sem["rest"], o + 1)
                        pool.tensor_copy(part[:, a, 1, c, :], rest[:, o, :]).then_inc(sem["p2"], 1)
                        pool.wait_ge(sem["p2"], o + 1)
                        pool.tensor_tensor(part[:, a, 2, c, :], rest[:, o, :], part[:, a, 1, c, :],
                                           ALU.subtract).then_inc(sem["p3"], 1)

                @block.tensor
                def _(pe):
                    transpose_tile(pe, ps, 0, xn, k.ident, sem["xn"], 0, sem["xt_ps"])
                    pe.wait_ge(sem["xt"], 1)
                    for o in range(4):
                        a, c = o // DC, o % DC
                        for ic in range(DC):
                            mm = pe.matmul(ps[:, 2 + o, :], w[:, a, ic, c * P:(c + 1) * P], xt[:, ic, :],
                                           start=(ic == 0), stop=(ic == DC - 1))
                        mm.then_inc(sem["qk_ps"], 1)
                    for s in range(SUB):
                        for ic in range(DC):
                            mm = pe.matmul(ps[:, 6 + s // 2, (s % 2) * D:(s % 2 + 1) * D], xt[:, ic, s * P:(s + 1) * P],
                                           w[:, 2, ic, :], start=(ic == 0), stop=(ic == DC - 1))
                    mm.then_inc(sem["v_ps"], 1)

                @block.scalar
                def _(act):
                    act.wait_ge(sem["xt_ps"], 1)
                    act.activation(xt[:, :, :], ps[:, 0:DC, :], ACT.Copy).then_inc(sem["xt"], 1)
                    for o in range(4):
                        a, c = o // DC, o % DC
                        act.wait_ge(sem["qk_ps"], o + 1)
                        act.activation(part[:, a, 0, c, :], ps[:, 2 + o, :], ACT.Copy,
                                       scale=(DH ** -0.5, 1.0)[a]).then_inc(sem["p1"], 1)
                    act.wait_ge(sem["v_ps"], 1)
                    act.activation(v[:, :, :, 0:DH],
                                   ps[:, 6:8, :].rearrange("p b (s h e) -> p (b s) h e", s=2, e=DH), ACT.Copy).then_inc(sem["v"], 1)
            nc.all_engine_barrier(sems_to_clear=cleared(sem))



TILES = [1, 3, 5, 7, 6, 4, 2, 0]
QSLOTS = 4
KROWS = 6 * DH
SROWS = KROWS + 2
QPARTS = (0, 0, 1, 1, 0, 2)
KPARTS = (0, 1, 0, 1, 2, 0)
MAXSLOTS = 3


def attend_schedule():
    max_steps = [[("m", n, s, b) for s in range(SUB) for b in range(t + 1)] for n, t in enumerate(TILES)]
    flat = [(n, st) for n, steps in enumerate(max_steps) for st in steps]
    out, at, turned = [], 0, 0

    def advance(k, upto):
        nonlocal at
        while k > 0 and at < len(flat) and flat[at][0] <= upto:
            out.append(flat[at][1])
            at += 1
            k -= 1

    def done(n):
        return at >= sum(len(s) for s in max_steps[:n + 1])

    chunks = [(n, c) for n, t in enumerate(TILES) for c in range(SUB * (t + 1))]
    advance(len(flat), 0)
    pending = None
    for i, (n, c) in enumerate(chunks):
        if c == 0:
            advance(len(flat), n)
            while turned <= n:
                out.append(("t", turned))
                turned += 1
        out.append(("s", n, c))
        if pending:
            out.append(("a", *pending))
        pending = (n, c)
        advance(1, n + QSLOTS - 1)
        if turned < len(TILES) and turned == n + 1 and done(turned) and c == SUB * (TILES[n] + 1) - 3:
            out.append(("t", turned))
            turned += 1
    out.append(("a", *pending))
    return out


def attend(nc, io, k, ps, scr):
    steps = attend_schedule()
    chunks = [(n, c) for n, t in enumerate(TILES) for c in range(SUB * (t + 1))]
    chunk_no = {nc_: i for i, nc_ in enumerate(chunks)}
    last_chunk = [chunk_no[(n, SUB * (t + 1) - 1)] for n, t in enumerate(TILES)]
    ring = []
    for st in steps:
        if st[0] == "m":
            ring += [(*st, j) for j in range(G)]
        elif st[0] == "t":
            ring.append(st)
    ring_no = {u: i for i, u in enumerate(ring)}
    NTL = len(TILES)

    def off(n, c):
        return max(0, c - SUB * TILES[n]) * P

    names = [f"k_in{i}" for i in range(NT)] + [f"v_in{i}" for i in range(NT)] + [f"q_in{n}" for n in range(NTL)] + \
            [f"rows_in{n}" for n in range(NTL)] + [f"stored{n}" for n in range(NTL)] + \
            ["scores", "probs", "summed", "max_ps", "max_used", "neg_max", "turned", "out_sb", "dve"]
    with ExitStack() as ctx:
        sb = lambda n, shape, dt=F32: ctx.enter_context(nc.sbuf_tensor(n, shape, dt))
        wsem = stage_sems(ctx, nc, "attnw", ["ones"])
        sem = loop_sems(k.loop_sems, names)
        k_in, v_in = [sem[f"k_in{i}"] for i in range(NT)], [sem[f"v_in{i}"] for i in range(NT)]
        q_in, rows_in, stored = ([sem[f"{x}{n}"] for n in range(NTL)] for x in ("q_in", "rows_in", "stored"))
        kb = sb("kb", [P, G, N], BF16)
        qb = sb("qb", [P, QSLOTS, G, T], BF16)
        vb = sb("vb", [P, N // P, G * 2 * DH])
        pb = sb("pb", [P, 4, 2, T])
        mx = sb("mx", [P, 2, G, SUB, NT])
        nm = sb("nm", [P, G, SUB])
        cb = sb("cb", [P, 2, SUB, G, 2], BF16)
        cr = sb("cr", [2 * G, 2, T], BF16)
        ob = sb("ob", [P, QSLOTS, T])
        AV, RING = 4, 5
        with nc.Block() as block:
            @block.vector
            def _(dve):
                dve.memset(kb[KROWS:SROWS, :, :], 1.0).then_inc(wsem["ones"], 1)
                dve.wait_ge(wsem["ones"], 1)
        with nc.Fori(0, NG) as g:
            with nc.Block() as block:
                @block.sync
                def _(sp):
                    qv = scr.q.rearrange("a (g j d) n -> a g d j n", g=NG, j=G)
                    kv = scr.k.rearrange("a (g j d) n -> a g d j n", g=NG, j=G)
                    vv = scr.v.rearrange("(c p) (g m) -> g p c m", p=P, g=NG)
                    ov = scr.o.rearrange("(g r) n -> g r n", g=NG)

                    def load_q(n):
                        if n >= QSLOTS:
                            sp.wait_ge(sem["scores"], 2 * (last_chunk[n - QSLOTS] + 1))
                        for r, a in enumerate(QPARTS):
                            sp.dma_start(qb[r * DH:(r + 1) * DH, n % QSLOTS],
                                         qv[a, g][:, :, TILES[n] * T:(TILES[n] + 1) * T]).then_inc(q_in[n], 16)

                    def load_k(i):
                        for r, a in enumerate(KPARTS):
                            sp.dma_start(kb[r * DH:(r + 1) * DH, :, i * T:(i + 1) * T],
                                         kv[a, g][:, :, i * T:(i + 1) * T]).then_inc(k_in[i], 16)

                    def load_v(i):
                        sp.dma_start(vb[:, i * SUB:(i + 1) * SUB], vv[g][:, i * SUB:(i + 1) * SUB]).then_inc(v_in[i], 16)

                    def store(n):
                        sp.wait_ge(sem["out_sb"], n + 1)
                        sp.dma_start(ov[g][:, TILES[n] * T:(TILES[n] + 1) * T], ob[:, n % QSLOTS]).then_inc(stored[n], 16)

                    def send_rows(n):
                        sp.wait_ge(sem["turned"], n + 1)
                        for j in range(G):
                            sp.dma_start(qb[KROWS:SROWS, n % QSLOTS, j], cr[2 * j:2 * j + 2, n % 2]).then_inc(rows_in[n], 16)

                    load_q(0)
                    load_k(0)
                    load_k(1)
                    load_q(1)
                    load_v(0)
                    load_v(1)
                    for i in range(2, NT):
                        load_k(i)
                        load_v(i)
                        if i % 2 == 1 and (i + 1) // 2 < QSLOTS:
                            load_q((i + 1) // 2)
                    send_rows(0)
                    for n in range(NTL):
                        if n + 1 < NTL:
                            send_rows(n + 1)
                        if n + QSLOTS < NTL:
                            load_q(n + QSLOTS)
                        store(n)
                    for n in range(NTL):
                        sp.wait_ge(stored[n], 16)

                @block.tensor
                def _(pe):
                    def ring_bank(u):
                        i = ring_no[u]
                        if i >= MAXSLOTS:
                            pe.wait_ge(sem["max_used"], i - MAXSLOTS + 1)
                        return RING + i % MAXSLOTS

                    seen_k = seen_v = 0
                    for st in steps:
                        n = st[1]
                        t = TILES[n]
                        if st[0] == "m":
                            s, b = st[2], st[3]
                            if s == 0 and b == 0:
                                pe.wait_ge(q_in[n], 16 * len(QPARTS))
                            while seen_k <= b:
                                pe.wait_ge(k_in[seen_k], 16 * len(KPARTS))
                                seen_k += 1
                            width = T if b < t else (s + 1) * P
                            for j in range(G):
                                bank = ring_bank((*st, j))
                                mm = pe.matmul(ps[:, bank, 0:width], qb[0:KROWS, n % QSLOTS, j, s * P:(s + 1) * P],
                                               kb[0:KROWS, j, b * T:b * T + width], start=True, stop=(b < t))
                                if b == t:
                                    mm = pe.matmul(ps[:, bank, s * P:width], k.identb[:, :], k.mask_qk[:, :],
                                                   start=False, stop=True)
                                mm.then_inc(sem["max_ps"], 1)
                        elif st[0] == "t":
                            pe.wait_ge(sem["neg_max"], n + 1)
                            bank = ring_bank(st)
                            for s in range(SUB):
                                mm = pe.matmul(ps[0:2 * G, bank, s * P:(s + 1) * P], cb[:, n % 2, s, :, :].rearrange("p j a -> p (j a)"),
                                               k.identb[:, :], start=True, stop=True)
                            mm.then_inc(sem["max_ps"], 1)
                        elif st[0] == "s":
                            c = st[2]
                            q = chunk_no[(n, c)]
                            o = off(n, c)
                            if c == 0:
                                pe.wait_ge(rows_in[n], 16 * G)
                            diagonal = c >= SUB * t
                            for pair in range(2):
                                u = 2 * q + pair
                                if u >= 2:
                                    pe.wait_ge(sem["probs"], u - 1)
                                for hh in range(2):
                                    j = 2 * pair + hh
                                    bank = 2 * pair + hh
                                    mm = pe.matmul(ps[:, bank, o:T], kb[0:SROWS, j, c * P:(c + 1) * P],
                                                   qb[0:SROWS, n % QSLOTS, j, o:T], start=True, stop=not diagonal)
                                    if diagonal:
                                        mm = pe.matmul(ps[:, bank, o:o + P], k.identb[:, :], k.mask_kq[:, :],
                                                       start=False, stop=True)
                                mm.then_inc(sem["scores"], 1)
                        else:
                            c = st[2]
                            q = chunk_no[(n, c)]
                            o = off(n, c)
                            while seen_v <= c // SUB:
                                pe.wait_ge(v_in[seen_v], 16)
                                seen_v += 1
                            if c == 0 and n > 0:
                                pe.wait_ge(sem["out_sb"], n)
                            pe.wait_ge(sem["probs"], 2 * q + 2)
                            for j in range(G):
                                mm = pe.matmul(ps[32 * j:32 * j + 32, AV, o:T], vb[:, c, 32 * j:32 * j + 32],
                                               pb[:, 2 * (q % 2) + j // 2, j % 2, o:T],
                                               start=(c == 0), stop=(q == last_chunk[n]), tile_position=(0, 32 * j),
                                               skip_group_check=True)
                            mm.then_inc(sem["summed"], 1)

                @block.scalar
                def _(act):
                    def copy_out(n):
                        act.wait_ge(sem["summed"], last_chunk[n] + 1)
                        if n >= QSLOTS:
                            act.wait_ge(stored[n - QSLOTS], 16)
                        act.activation(ob[:, n % QSLOTS], ps[:, AV, :], ACT.Copy).then_inc(sem["out_sb"], 1)

                    for q, (n, c) in enumerate(chunks):
                        o = off(n, c)
                        for pair in range(2):
                            u = 2 * q + pair
                            act.wait_ge(sem["scores"], u + 1)
                            if q >= 2 and pair == 0:
                                act.wait_ge(sem["summed"], q - 1)
                            act.activation(pb[:, 2 * (q % 2) + pair, :, o:T], ps[:, 2 * pair:2 * pair + 2, o:T],
                                           ACT.Exp).then_inc(sem["probs"], 1)
                        if c == 1 and n > 0:
                            copy_out(n - 1)
                    copy_out(NTL - 1)

                @block.vector
                def _(dve):
                    ch = Chain(dve, sem["dve"])
                    for i, u in enumerate(ring):
                        n = u[1]
                        t = TILES[n]
                        dve.wait_ge(sem["max_ps"], i + 1)
                        bank = RING + i % MAXSLOTS
                        if u[0] == "m":
                            s, b, j = u[2:]
                            width = T if b < t else (s + 1) * P
                            dve.tensor_reduce(mx[:, n % 2, j, s, b:b + 1], ps[:, bank, 0:width], AX, ALU.max)\
                               .then_inc(sem["max_used"], 1)
                            if (s, b, j) == (SUB - 1, t, G - 1):
                                dve.wait_ge(sem["max_used"], i + 1)
                                if n >= 2:
                                    dve.wait_ge(sem["turned"], n - 1)
                                ch.link(dve.tensor_reduce(nm[:, :, :], mx[:, n % 2, :, :, 0:t + 1], AX, ALU.max))
                                nms = nm[:, :, :].rearrange("p j s -> p s j")
                                ch.link(dve.tensor_scalar(cb[:, n % 2, :, :, 0], nms, -1.0, None, ALU.mult))
                                dve.scalar_tensor_tensor(out=cb[:, n % 2, :, :, 1], in0=nms, scalar=-1.0, in1=cb[:, n % 2, :, :, 0],
                                                         op0=ALU.mult, op1=ALU.subtract).then_inc(sem["neg_max"], 1)
                                dve.wait_ge(sem["neg_max"], n + 1)
                        else:
                            if n >= 2:
                                dve.wait_ge(rows_in[n - 2], 16 * G)
                            dve.tensor_copy(cr[:, n % 2, :], ps[0:2 * G, bank, :]).then_inc(sem["turned"], 1)
                            dve.wait_ge(sem["turned"], n + 1)
                            dve.engine_nop().then_inc(sem["max_used"], 1)
            nc.all_engine_barrier(sems_to_clear=cleared(sem))



def mix(nc, io, k, ps, scr):
    XP, TP, GP, EP, LP = 0, 2, 4, 5, 7
    names = ["x_in", "o_in", "den_in", "dve", "pool", "on", "o_ps", "var", "rstd", "xn", "xt_ps", "xt", "gl_ps", "expo",
             "expd", "gate", "gt_ps", "gt", "bias_ps", "e_ps", "e_used", "hot", "l_ps", "xcopy"]
    with ExitStack() as ctx:
        sb = lambda n, shape, dt=F32: ctx.enter_context(nc.sbuf_tensor(n, shape, dt))
        wsem = stage_sems(ctx, nc, "mixw", ["in_", "zero", "lrow", "lt_ps", "lt"])
        sem = loop_sems(k.loop_sems, names)
        wout, we, eb = sb("w_out", [P, DC, D]), sb("w_e", [P, DC, E, D]), sb("e_bias", [E, D])
        o, den = sb("o_c", [P, DC, T]), sb("den_c", [P, DC, T])
        x, x1 = sb("x_c", [P, SUB, D]), sb("x1_c", [P, SUB, D])
        xn, xt = sb("xn_c", [P, SUB, D]), sb("xt_c", [P, DC, T])
        st, mv, rstd = sb("st_c", [P, SUB, 6]), sb("mv_c", [P, SUB, 2]), sb("rstd_c", [P, SUB])
        lg, gm, gs = sb("lg", [P, SUB, E]), sb("gm", [P, SUB]), sb("gs", [P, SUB])
        more, ties = sb("more", [P, SUB, E, E]), sb("ties", [P, SUB, E, E])
        rank, ex, gate = sb("rank", [P, SUB, E]), sb("ex", [P, SUB, E]), sb("gate", [P, SUB, E])
        gt = sb("gt", [E, T])
        hot, tok = sb("hot", [P, SUB, M]), k.tok
        lx = sb("lx", [M, D])
        with nc.Block() as block:
            @block.sync
            def _(sp):
                sp.dma_start(wout[:], io["L0_attn_Wout"].rearrange("(c h) e n -> (h e) c n", c=DC)).then_inc(wsem["in_"], 16)
                for e in range(E):
                    sp.dma_start(we[:, :, e], io["L0_ffn_expert_w"][e].rearrange("(c p) n -> p c n", p=P)).then_inc(wsem["in_"], 16)
                sp.dma_start(eb[:], io["L0_ffn_expert_b"]).then_inc(wsem["in_"], 16)
                sp.wait_ge(wsem["in_"], 16 * (E + 2))

            @block.vector
            def _(dve):
                dve.memset(hot[:], 0.0).then_inc(wsem["zero"], 1)

            @block.tensor
            def _(pe):
                pe.wait_ge(wsem["zero"], 1)
                pe.matmul(ps[0:M, LP, 0:D], hot[:, 0, :], hot[:].rearrange("p s m -> p (s m)"), start=True, stop=True).then_inc(wsem["lrow"], 1)
                pe.wait_ge(wsem["lrow"], 1)
        with nc.Fori(0, NT) as i:
            with nc.Block() as block:
                @block.sync
                def _(sp):
                    ov = scr.o.rearrange("(c h two e) (i n) -> i two c h e n", c=DC, two=2, e=DH, n=T)
                    for c in range(DC):
                        sp.dma_start(den[:, c], ov[i, 1, c]).then_inc(sem["den_in"], 16)
                        sp.dma_start(o[:, c], ov[i, 0, c]).then_inc(sem["o_in"], 16)
                    sp.dma_start(x[:], io["L0_attn_x"].rearrange("o (i s p) d -> (o i) p s d", s=SUB, p=P)[i]).then_inc(sem["x_in"], 16)

                @block.tensor
                def _(pe):
                    pe.wait_ge(sem["on"], 1)
                    for s in range(SUB):
                        for c in range(DC):
                            mm = pe.matmul(ps[:, XP + s // 2, (s % 2) * D:(s % 2 + 1) * D], o[:, c, s * P:(s + 1) * P],
                                           wout[:, c, :], start=(c == 0), stop=(c == DC - 1))
                        mm.then_inc(sem["o_ps"], 1)
                    transpose_tile(pe, ps, TP, xn, k.ident, sem["xn"], 0, sem["xt_ps"])
                    pe.wait_ge(sem["xt"], 1)
                    for s in range(SUB):
                        for c in range(DC):
                            mm = pe.matmul(ps[:, GP, s * E:(s + 1) * E], xt[:, c, s * P:(s + 1) * P], k.gate_w[:, c, :],
                                           start=(c == 0), stop=(c == DC - 1))
                    mm.then_inc(sem["gl_ps"], 1)
                    n = 0
                    for s in range(SUB):
                        for e in range(0, E, 2):
                            if n >= 2:
                                pe.wait_ge(sem["e_used"], n - 1)
                            for c in range(DC):
                                mm = pe.matmul(ps[:, EP + n % 2, :], xt[:, c, s * P:(s + 1) * P],
                                               we[:, c, e:e + 2, :].rearrange("p e n -> p (e n)"), start=(c == 0), stop=(c == DC - 1))
                            mm.then_inc(sem["e_ps"], 1)
                            n += 1
                            if n == 2:
                                pe.wait_ge(sem["gate"], 1)
                                for s2 in range(SUB):
                                    tr = pe.transpose(ps[0:E, GP, s2 * P:(s2 + 1) * P], gate[:, s2, :], k.ident[:, :])
                                tr.then_inc(sem["gt_ps"], 1)
                                pe.wait_ge(sem["gt"], 1)
                                for s2 in range(SUB):
                                    mm = pe.matmul(ps[:, XP + s2 // 2, (s2 % 2) * D:(s2 % 2 + 1) * D], gt[:, s2 * P:(s2 + 1) * P],
                                                   eb[:, :], start=True, stop=True)
                                mm.then_inc(sem["bias_ps"], 1)
                    transpose_tile(pe, ps, TP, xn, k.ident, sem["xn"], SUB, sem["xt_ps"])
                    pe.wait_ge(sem["hot"], 1)
                    for s in range(SUB):
                        mm = pe.matmul(ps[0:M, LP, 0:D], hot[:, s, :], xn[:, s, :], start=False, stop=True,
                                       skip_group_check=True)
                    mm.then_inc(sem["l_ps"], 1)

                @block.vector
                def _(dve):
                    ch = Chain(dve, sem["dve"])
                    dve.wait_ge(sem["den_in"], 32)
                    ch.link(dve.reciprocal(den[:], den[:]))
                    dve.wait_ge(sem["o_in"], 32)
                    dve.tensor_tensor(o[:], o[:], den[:], ALU.mult).then_inc(sem["on"], 1)
                    dve.wait_ge(sem["x_in"], 16)
                    for s in range(SUB):
                        dve.wait_ge(sem["o_ps"], 2 * (s // 2) + 2)
                        ch.step(dve.tensor_tensor(x1[:, s, :], x[:, s, :], ps[:, XP + s // 2, (s % 2) * D:(s % 2 + 1) * D], ALU.add))
                    ch.wait()
                    ln_stats(dve, ch, x1, st, mv, sem["var"])
                    ln_apply(dve, x1, xn, mv, rstd, sem["rstd"], 1, sem["xn"])
                    full = [P, SUB, E, E]
                    dve.wait_ge(sem["gl_ps"], 1)
                    ch.link(dve.tensor_tensor(lg[:], ps[:, GP, 0:SUB * E].rearrange("p (s e) -> p s e", s=SUB),
                                              bc(k.gate_b[:, :], 1, [P, SUB, E]), ALU.add))
                    ch.step(dve.tensor_tensor(more[:], bc(lg[:], 2, full), bc(lg[:], 3, full), ALU.is_gt))
                    ch.step(dve.tensor_tensor(ties[:], bc(lg[:], 2, full), bc(lg[:], 3, full), ALU.is_equal))
                    ch.step(dve.tensor_reduce(gm[:], lg[:], AX, ALU.max))
                    ch.wait()
                    ch.step(dve.tensor_tensor(ties[:], ties[:], bc(k.before[:], 1, full), ALU.mult))
                    dve.tensor_tensor(lg[:], lg[:], bc(gm[:], 2, [P, SUB, E]), ALU.subtract).then_inc(sem["expd"], 1)
                    ch.wait()
                    ch.link(dve.tensor_tensor(more[:], more[:], ties[:], ALU.add))
                    ch.link(dve.tensor_reduce(rank[:], more[:], AX, ALU.add))
                    dve.wait_ge(sem["expo"], 1)
                    ch.link(dve.scalar_tensor_tensor(out=gate[:], in0=rank[:], scalar=float(TOP), in1=ex[:], op0=ALU.is_lt, op1=ALU.mult))
                    ch.link(dve.tensor_reduce(gs[:], gate[:], AX, ALU.add))
                    ch.link(dve.reciprocal(gs[:], gs[:]))
                    dve.tensor_tensor(gate[:], gate[:], bc(gs[:], 2, [P, SUB, E]), ALU.mult).then_inc(sem["gate"], 1)
                    dve.wait_ge(sem["gate"], 1)
                    n = 0
                    for s in range(SUB):
                        for e in range(0, E, 2):
                            dve.wait_ge(sem["e_ps"], n + 1)
                            ch.link(dve.scalar_tensor_tensor(out=x1[:, s, :], in0=ps[:, EP + n % 2, 0:D], scalar=gate[:, s, e:e + 1],
                                                             in1=x1[:, s, :], op0=ALU.mult, op1=ALU.add))
                            ch.link(dve.scalar_tensor_tensor(out=x1[:, s, :], in0=ps[:, EP + n % 2, D:2 * D], scalar=gate[:, s, e + 1:e + 2],
                                                             in1=x1[:, s, :], op0=ALU.mult, op1=ALU.add))
                            dve.engine_nop().then_inc(sem["e_used"], 1)
                            n += 1
                        if s == 0:
                            dve.wait_ge(sem["bias_ps"], 1)
                        ch.link(dve.tensor_tensor(x1[:, s, :], x1[:, s, :], ps[:, XP + s // 2, (s % 2) * D:(s % 2 + 1) * D], ALU.add))
                    ln_stats(dve, ch, x1, st, mv, sem["var"])
                    dve.wait_ge(sem["xt_ps"], 1)
                    ln_apply(dve, x1, xn, mv, rstd, sem["rstd"], 2, sem["xn"])
                    ch.link(dve.tensor_tensor(hot[:], bc(k.idx[:, :], 1, [P, SUB, M]), bc(tok[:], 2, [P, SUB, M]), ALU.is_equal))
                    dve.tensor_scalar(tok[:], tok[:], float(T), None, ALU.add).then_inc(sem["hot"], 1)

                @block.gpsimd
                def _(pool):
                    ch = Chain(pool, sem["pool"])
                    ln_rstd(pool, ch, mv, rstd, k.neghalf, sem["var"], SUB, sem["rstd"])
                    ln_rstd(pool, ch, mv, rstd, k.neghalf, sem["var"], 2 * SUB, sem["rstd"])
                    pool.wait_ge(sem["xn"], 2 * SUB)
                    pool.tensor_copy(k.x2[:, bass.ds(i * SUB, SUB), :], x1[:]).then_inc(sem["xcopy"], 1)
                    pool.wait_ge(sem["xcopy"], 1)

                @block.scalar
                def _(act):
                    act.wait_ge(sem["xt_ps"], 1)
                    act.activation(xt[:], ps[:, TP:TP + DC, :], ACT.Copy).then_inc(sem["xt"], 1)
                    act.wait_ge(sem["expd"], 1)
                    act.activation(ex[:], lg[:], ACT.Exp).then_inc(sem["expo"], 1)
                    act.wait_ge(sem["gt_ps"], 1)
                    act.activation(gt[:], ps[0:E, GP, :], ACT.Copy).then_inc(sem["gt"], 1)
                    act.wait_ge(sem["xt_ps"], 2)
                    act.activation(k.xn3t[:, :, bass.ds(i * T, T)], ps[:, TP:TP + DC, :], ACT.Copy).then_inc(sem["xt"], 1)
            nc.all_engine_barrier(sems_to_clear=cleared(sem))
        with nc.Block() as block:
            @block.vector
            def _(dve):
                dve.tensor_copy(lx[:], ps[0:M, LP, 0:D]).then_inc(wsem["lt"], 1)
                dve.wait_ge(wsem["lt_ps"], 1)
                dve.tensor_copy(k.lxt[:], ps[:, 0, 0:DC * M].rearrange("p (c m) -> p c m", c=DC)).then_inc(wsem["lt"], 1)

            @block.tensor
            def _(pe):
                pe.wait_ge(wsem["lt"], 1)
                for c in range(DC):
                    tr = pe.transpose(ps[:, 0, c * M:(c + 1) * M], lx[:, c * P:(c + 1) * P], k.ident[0:M, 0:M])
                tr.then_inc(wsem["lt_ps"], 1)



NROW, OROW = 64, 96
LROWS = OROW + 1


def landmark_operands(nc, io, k, ps, la, lk, scr):
    with ExitStack() as ctx:
        sb = lambda n, shape, dt=F32: ctx.enter_context(nc.sbuf_tensor(n, shape, dt))
        sem = stage_sems(ctx, nc, "lm", ["dve", "act", "l_ps", "lk", "sq", "n_ps", "ready", "w_ps", "w", "out"])
        sq, sql = sb("sq_la", [64, G, G * M]), sb("sq_lk", [64, G, M])
        wm = sb("wm", [M, H, M])
        laf = la[:].rearrange("p g j m -> p g (j m)")
        with nc.Block() as block:
            @block.tensor
            def _(pe):
                for c in range(DC):
                    for ic in range(DC):
                        mm = pe.matmul(ps[:, 0, c * M:(c + 1) * M], k.wk1[:, ic, c * P:(c + 1) * P], k.lxt[:, ic, :],
                                       start=(ic == 0), stop=(ic == DC - 1))
                mm.then_inc(sem["l_ps"], 1)
                pe.wait_ge(sem["sq"], 2)
                pe.matmul(ps[NROW:NROW + 32, 1, 0:G * M], k.sel[:, :], sql[:].rearrange("p g m -> p (g m)"), start=True, stop=True,
                          tile_position=(0, NROW)).then_inc(sem["n_ps"], 1)
                for b in range(2):
                    mm = pe.matmul(ps[OROW:OROW + 1, 2 + b, :], k.quarter[:, :], sq[:, 2 * b:2 * b + 2, :].rearrange("p g m -> p (g m)"),
                                   start=True, stop=True, tile_position=(0, OROW))
                mm.then_inc(sem["n_ps"], 1)
                pe.wait_ge(sem["ready"], 1)
                for g in range(G):
                    mm = pe.matmul(ps[0:M, 4 + g // 2, (g % 2) * D:(g % 2 + 1) * D], lk[0:LROWS, g, :], laf[0:LROWS, g],
                                   start=True, stop=True)
                mm.then_inc(sem["w_ps"], 1)

            @block.vector
            def _(dve):
                ch = Chain(dve, sem["dve"])
                ch.step(dve.memset(lk[OROW:LROWS], 1.0))
                for g in range(G):
                    ch.step(dve.tensor_copy(la[NROW:NROW + 32, g], k.blk1[NROW:NROW + 32]))
                dve.wait_ge(sem["l_ps"], 1)
                for g in range(G):
                    r, c = 64 * (g % 2), g // 2
                    ch.step(dve.tensor_scalar(lk[0:64, g, :], ps[r:r + 64, 0, c * M:(c + 1) * M], k.bk1[r:r + 64, c:c + 1], None, ALU.add))
                ch.wait()
                for g in range(G):
                    ch.step(dve.tensor_tensor(la[0:64, g], bc(lk[0:64, g, :], 1, [64, G, M]), k.blk2[:], ALU.mult))
                dve.tensor_tensor(sql[:], lk[0:64], lk[0:64], ALU.mult).then_inc(sem["sq"], 1)
                ch.wait()
                dve.tensor_tensor(sq[:], laf[0:64], laf[0:64], ALU.mult).then_inc(sem["sq"], 1)
                dve.wait_ge(sem["n_ps"], 2)
                ch.step(dve.tensor_copy(lk[NROW:NROW + 32], ps[NROW:NROW + 32, 1, 0:G * M].rearrange("p (g m) -> p g m", g=G)))
                ch.link(dve.tensor_copy(laf[OROW:LROWS].rearrange("p (b g) m -> p b (g m)", b=2), ps[OROW:LROWS, 2:4, :]))
                dve.engine_nop().then_inc(sem["ready"], 1)
                dve.wait_ge(sem["w_ps"], 1)
                dve.tensor_scalar(wm[:].rearrange("p (b h) m -> p b (h m)", b=2), ps[0:M, 4:6, :], 0.0, None, ALU.max).then_inc(sem["w"], 1)
                dve.wait_ge(sem["w"], 2)
                dve.tensor_tensor(wm[:], wm[:], bc(k.regi[:], 1, [M, H, M]), ALU.add).then_inc(sem["w"], 1)

            @block.scalar
            def _(act):
                act.wait_ge(sem["w"], 1)
                act.activation(wm[:], wm[:], ACT.Exp, scale=k.negt[0:M, 0:1]).then_inc(sem["w"], 1)

            @block.sync
            def _(sp):
                sp.wait_ge(sem["w"], 3)
                sp.dma_start(scr.w.rearrange("h a b -> a h b"), wm[:]).then_inc(sem["out"], 16)
                sp.wait_ge(sem["out"], 16)


def invert(nc, io, k, ps, scr, winv):
    with ExitStack() as ctx:
        sb = lambda n, shape, dt=F32: ctx.enter_context(nc.sbuf_tensor(n, shape, dt))
        wsem = stage_sems(ctx, nc, "invw", ["in_", "zero", "done", "out", "back"])
        sem = stage_sems(ctx, nc, "inv", ["dve", "piv", "swept"])
        a = sb("a_inv", [P, 8, M])
        u = sb("u_inv", [P, 8, M])
        rd, sc, col = sb("rd_inv", [P, 1]), sb("sc_inv", [P, 8]), sb("col_inv", [P, M])
        own = k.own[:].rearrange("p (c j) -> p c j", j=8)
        with nc.Block() as block:
            @block.sync
            def _(sp):
                sp.dma_start(a[:], scr.w.rearrange("h (c j) i -> (h c) j i", j=8)).then_inc(wsem["in_"], 16)
                sp.wait_ge(wsem["in_"], 16)

            @block.gpsimd
            def _(pool):
                pool.memset(winv[:], 0.0).then_inc(wsem["zero"], 1)
                pool.wait_ge(wsem["zero"], 1)
        with nc.Block() as block:
            @block.tensor
            def _(pe):
                for p in range(M):
                    if p:
                        pe.wait_ge(sem["swept"], p)
                    pe.matmul(ps[:, p % 2, 0:M], k.spread[:, p // 8, :], a[:, p % 8, :], start=True, stop=True).then_inc(sem["piv"], 1)

            @block.vector
            def _(dve):
                ch = Chain(dve, sem["dve"])
                for p in range(M):
                    dve.wait_ge(sem["piv"], p + 1)
                    pc = ps[:, p % 2, 0:M]
                    ch.step(dve.reciprocal(rd[:], pc[:, p:p + 1]))
                    ch.step(dve.tensor_tensor(sc[:], a[:, :, p], own[:, p, :], ALU.subtract))
                    ch.step(dve.tensor_tensor(col[:], pc, k.unit[:, M - 1 - p:2 * M - 1 - p], ALU.subtract))
                    ch.wait()
                    ch.link(dve.tensor_scalar(sc[:], sc[:], rd[:, 0:1], None, ALU.mult))
                    ch.link(dve.tensor_tensor(u[:], bc(sc[:], 2, [P, 8, M]), bc(col[:], 1, [P, 8, M]), ALU.mult))
                    ch.step(dve.tensor_tensor(a[:], a[:], u[:], ALU.subtract))
                    ch.wait()
                    dve.engine_nop().then_inc(sem["swept"], 1)
                ch.link(dve.scalar_tensor_tensor(out=a[:], in0=own.rearrange("p i j -> p j i"), scalar=2.0, in1=a[:],
                                                 op0=ALU.mult, op1=ALU.subtract))
                dve.engine_nop().then_inc(wsem["done"], 1)

            @block.sync
            def _(sp):
                sp.wait_ge(wsem["done"], 1)
                sp.dma_start(scr.wi.rearrange("h (c j) i -> (h c) j i", j=8), a[:]).then_inc(wsem["out"], 16)
                sp.wait_ge(wsem["out"], 16)
                wv = scr.wi.rearrange("(r two) a b -> two a r b", two=2)
                for two in range(2):
                    sp.dma_start(winv[64 * two:64 * two + 64, :, 64 * two:64 * two + 64], wv[two]).then_inc(wsem["back"], 16)
                sp.wait_ge(wsem["back"], 32)


def rows_of(k, i):
    return k.xn3t[:, :, bass.ds(i * T, T)]


def operand_pe(pe, k, ps, w, xt, sq, sem, NB):
    for c in range(DC):
        for ic in range(DC):
            mm = pe.matmul(ps[:, c, :], w[:, ic, c * P:(c + 1) * P], xt[:, ic, :], start=(ic == 0), stop=(ic == DC - 1))
        mm.then_inc(sem["a_ps"], 1)
    pe.wait_ge(sem["sq"], 1)
    for g in range(G):
        mm = pe.matmul(ps[32 * g:32 * g + 32, NB, :], k.sel[:, :], sq[:, g, :], start=True, stop=True,
                       tile_position=(0, 32 * g), skip_group_check=True)
    mm.then_inc(sem["an_ps"], 1)


def operand_dve(dve, ps, a, b, sem, NB):
    for c in range(DC):
        dve.wait_ge(sem["a_ps"], c + 1)
        dve.tensor_scalar(a[0:64, 2 * c + 1, :], ps[64:128, c, :], b[64:128, c:c + 1], None, ALU.add).then_inc(sem["a_dve"], 1)
    dve.wait_ge(sem["an_ps"], 1)
    for g in (1, 3):
        dve.tensor_copy(a[NROW:NROW + 32, g, :], ps[32 * g:32 * g + 32, NB, :]).then_inc(sem["an_dve"], 1)


def operand_act(act, ps, a, b, sq, sem, NB):
    for c in range(DC):
        act.wait_ge(sem["a_ps"], c + 1)
        act.activation(a[0:64, 2 * c, :], ps[0:64, c, :], ACT.Identity, bias=b[0:64, c:c + 1]).then_inc(sem["a_act"], 1)
    act.wait_ge(sem["a_act"], DC)
    act.wait_ge(sem["a_dve"], DC)
    act.activation(sq[:], a[0:64], ACT.Square).then_inc(sem["sq"], 1)
    act.wait_ge(sem["an_ps"], 1)
    for g in (0, 2):
        act.activation(a[NROW:NROW + 32, g, :], ps[32 * g:32 * g + 32, NB, :], ACT.Copy).then_inc(sem["an_act"], 1)


OPERAND = ["a_ps", "a_dve", "a_act", "sq", "an_ps", "an_dve", "an_act"]


def keys(nc, io, k, ps, a, xt, sq, zt, acc):
    with ExitStack() as ctx:
        sb = lambda n, shape, dt=F32: ctx.enter_context(nc.sbuf_tensor(n, shape, dt))
        wsem = stage_sems(ctx, nc, "keysw", ["zero", "z_ps"])
        sem = loop_sems(k.loop_sems, OPERAND + ["xt_in", "v_ps", "v", "c_ps", "clamp", "phi", "z_ps", "acc"])
        v = sb("v_e", [P, SUB, D])
        cl, phi = sb("cl_e", [P, 2, H * M]), sb("phi_e", [P, 2, H * M])
        with nc.Block() as block:
            @block.vector
            def _(dve):
                dve.memset(acc[:], 0.0).then_inc(wsem["zero"], 1)
                dve.memset(a[OROW:LROWS], 1.0).then_inc(wsem["zero"], 1)

            @block.tensor
            def _(pe):
                pe.wait_ge(wsem["zero"], 2)
                for b in range(2):
                    mm = pe.matmul(ps[:, 6 + b, :], acc[:, 0:P], acc[:, 0:T], start=True, stop=True)
                mm.then_inc(wsem["z_ps"], 1)
                pe.wait_ge(wsem["z_ps"], 1)
        with nc.Fori(0, NT) as i:
            with nc.Block() as block:
                @block.sync
                def _(sp):
                    sp.dma_start(xt[:], rows_of(k, i)).then_inc(sem["xt_in"], 16)

                @block.tensor
                def _(pe):
                    pe.wait_ge(sem["xt_in"], 16)
                    operand_pe(pe, k, ps, k.wk1, xt, sq, sem, 2)
                    pe.wait_ge(sem["a_act"], DC)
                    pe.wait_ge(sem["a_dve"], DC)
                    for s in range(SUB):
                        for ic in range(DC):
                            mm = pe.matmul(ps[:, s // 2, (s % 2) * D:(s % 2 + 1) * D], xt[:, ic, s * P:(s + 1) * P],
                                           k.wv1[:, ic, :], start=(ic == 0), stop=(ic == DC - 1))
                    mm.then_inc(sem["v_ps"], 1)
                    pe.wait_ge(sem["an_act"], 2)
                    pe.wait_ge(sem["an_dve"], 2)
                    for s in range(SUB + 1):
                        if s < SUB:
                            if s >= 2:
                                pe.wait_ge(sem["clamp"], s - 1)
                            for g in range(G):
                                mm = pe.matmul(ps[:, 2 + 2 * (s % 2) + g // 2, (g % 2) * D:(g % 2 + 1) * D],
                                               a[0:LROWS, g, s * P:(s + 1) * P], k.la[0:LROWS, g].rearrange("p j m -> p (j m)"),
                                               start=True, stop=True)
                            mm.then_inc(sem["c_ps"], 1)
                        if s > 0:
                            if s == 1:
                                pe.wait_ge(sem["v"], 1)
                            pe.wait_ge(sem["phi"], s)
                            for b in range(2):
                                mm = pe.matmul(ps[:, 6 + b, :], v[:, s - 1, b * P:(b + 1) * P], phi[:, (s - 1) % 2, b * T:(b + 1) * T],
                                               start=False, stop=True, skip_group_check=True)
                            mm.then_inc(sem["z_ps"], 1)

                @block.vector
                def _(dve):
                    operand_dve(dve, ps, a, k.bk1, sem, 2)
                    dve.wait_ge(sem["v_ps"], 1)
                    dve.tensor_tensor(v[:], ps[:, 0:2, :].rearrange("p b (s n) -> p (b s) n", s=2), bc(k.bv1[:, :], 1, [P, SUB, D]),
                                      ALU.add).then_inc(sem["v"], 1)
                    for s in range(SUB):
                        dve.wait_ge(sem["c_ps"], s + 1)
                        if s >= 2:
                            dve.wait_ge(sem["phi"], s - 1)
                        b = 2 + 2 * (s % 2)
                        dve.tensor_scalar(cl[:, s % 2].rearrange("p (b n) -> p b n", b=2), ps[:, b:b + 2, :], 0.0, None,
                                          ALU.max).then_inc(sem["clamp"], 1)

                @block.scalar
                def _(act):
                    operand_act(act, ps, a, k.bk1, sq, sem, 2)
                    for s in range(SUB):
                        act.wait_ge(sem["clamp"], s + 1)
                        if s >= 2:
                            act.wait_ge(sem["z_ps"], s - 1)
                            act.wait_ge(sem["acc"], s - 1)
                        act.activation(phi[:, s % 2], cl[:, s % 2], ACT.Exp, scale=k.negt[:, 0:1]).then_inc(sem["phi"], 1)

                @block.gpsimd
                def _(pool):
                    for s in range(SUB):
                        pool.wait_ge(sem["phi"], s + 1)
                        pool.tensor_tensor(acc[:], acc[:], phi[:, s % 2], ALU.add).then_inc(sem["acc"], 1)
                        pool.wait_ge(sem["acc"], s + 1)
            nc.all_engine_barrier(sems_to_clear=cleared(sem))


def solve(nc, io, k, ps, winv, zt, acc):
    with ExitStack() as ctx:
        sb = lambda n, shape, dt=F32: ctx.enter_context(nc.sbuf_tensor(n, shape, dt))
        sem = stage_sems(ctx, nc, "solve", ["zt", "s_ps", "z_ps", "z", "y_ps", "y"])
        z = sb("z_s", [P, PAIRS, 2 * DH + 2])
        with nc.Block() as block:
            @block.vector
            def _(dve):
                dve.tensor_tensor(zt[:].rearrange("p c (h m) -> p c h m", m=M), ps[:, 6:8, :].rearrange("p c (h m) -> p c h m", m=M),
                                  bc(k.headmask[:], 1, [P, DC, 8, M]), ALU.mult).then_inc(sem["zt"], 1)
                dve.wait_ge(sem["z_ps"], 1)
                for r in range(PAIRS):
                    o = 2 * DH * (r % 4)
                    dve.tensor_copy(z[:, r, 0:2 * DH], ps[:, r // 4, (r % 4) * P + o:(r % 4) * P + o + 2 * DH]).then_inc(sem["z"], 1)
                dve.wait_ge(sem["s_ps"], 1)
                dve.tensor_tensor(z[:, :, 2 * DH:], bc(ps[:, 2, 0:PAIRS], 2, [P, PAIRS, 2]), bc(k.half[:, :], 1, [P, PAIRS, 2]),
                                  ALU.mult).then_inc(sem["z"], 1)
                dve.wait_ge(sem["y_ps"], 1)
                yv = ps[:, 3, 0:PAIRS * 64].rearrange("p (r n) -> p r n", n=64)
                dve.tensor_copy(k.y[:, :, 0, :], yv[:, :, 0:2 * DH]).then_inc(sem["y"], 1)
                for a in range(2):
                    dve.tensor_copy(k.y[:, :, 1, a * DH:(a + 1) * DH], yv[:, :, 2 * DH + a:2 * DH + a + 1].broadcast_to([P, PAIRS, DH]))\
                       .then_inc(sem["y"], 1)

            @block.tensor
            def _(pe):
                for r in range(PAIRS):
                    mm = pe.matmul(ps[:, 2, r:r + 1], acc[:, r * P:(r + 1) * P], k.ones[:, :], start=True, stop=True)
                mm.then_inc(sem["s_ps"], 1)
                pe.wait_ge(sem["zt"], 1)
                for r in range(PAIRS):
                    tr = pe.transpose(ps[:, r // 4, (r % 4) * P:(r % 4 + 1) * P], zt[:, r // 4, (r % 4) * P:(r % 4 + 1) * P], k.ident[:, :])
                tr.then_inc(sem["z_ps"], 1)
                pe.wait_ge(sem["z"], PAIRS + 1)
                for r in range(PAIRS):
                    mm = pe.matmul(ps[:, 3, r * 64:r * 64 + 2 * DH + 2], winv[:, r, :], z[:, r, :], start=True, stop=True)
                mm.then_inc(sem["y_ps"], 1)


def landmarks(nc, io, k, ps, scr):
    with ExitStack() as ctx:
        sb = lambda n, shape, dt=F32: ctx.enter_context(nc.sbuf_tensor(n, shape, dt))
        winv = sb("winv", [P, PAIRS, P])
        with ExitStack() as inner:
            lk = inner.enter_context(nc.sbuf_tensor("lk", [P, G, M], F32))
            landmark_operands(nc, io, k, ps, k.la, lk, scr)
            invert(nc, io, k, ps, scr, winv)
        a, xt, sq = sb("a_keys", [P, G, T]), sb("xt_keys", [P, DC, T]), sb("sq_keys", [64, G, T])
        zt, acc = sb("zt", [P, DC, T]), sb("acc", [P, H * M])
        keys(nc, io, k, ps, a, xt, sq, zt, acc)
        solve(nc, io, k, ps, winv, zt, acc)



def queries(nc, io, k, ps, out):
    with ExitStack() as ctx:
        sb = lambda n, shape, dt=F32: ctx.enter_context(nc.sbuf_tensor(n, shape, dt))
        wsem = stage_sems(ctx, nc, "qryw", ["one"])
        sem = loop_sems(k.loop_sems, OPERAND + ["xt_in", "c_ps", "clamp", "phi", "n_ps", "on", "dve", "pool", "xb", "o_ps", "var",
                                             "rstd", "xn", "xt_ps", "xt", "f_ps", "res", "out"])
        a, xt, sq = sb("a_q", [P, G, T]), sb("xt_q", [P, DC, T]), sb("sq_q", [64, G, T])
        cl, phi = sb("cl_q", [P, 2, T]), sb("phi_q", [P, PAIRS, T])
        nr, ot = sb("nr_q", [P, DC, T]), sb("ot_q", [P, DC, T])
        xb, x3, xn, x4 = (sb(f"{n}_q", [P, SUB, D]) for n in ("xb", "x3", "xn", "x4"))
        st, mv, rstd = sb("st_q", [P, SUB, 6]), sb("mv_q", [P, SUB, 2]), sb("rstd_q", [P, SUB])
        xt4 = sb("xt4_q", [P, DC, T])
        with nc.Block() as block:
            @block.vector
            def _(dve):
                dve.memset(a[OROW:LROWS], 1.0).then_inc(wsem["one"], 1)
                dve.wait_ge(wsem["one"], 1)
        with nc.Fori(0, NT) as i:
            with nc.Block() as block:
                @block.sync
                def _(sp):
                    sp.dma_start(xt[:], rows_of(k, i)).then_inc(sem["xt_in"], 16)
                    sp.wait_ge(sem["res"], SUB)
                    sp.dma_start(out.rearrange("o (i s p) d -> (o i) p s d", s=SUB, p=P)[i], x4[:]).then_inc(sem["out"], 16)
                    sp.wait_ge(sem["out"], 16)

                @block.tensor
                def _(pe):
                    pe.wait_ge(sem["xt_in"], 16)
                    operand_pe(pe, k, ps, k.wq1, xt, sq, sem, 2)
                    pe.wait_ge(sem["an_act"], 2)
                    pe.wait_ge(sem["an_dve"], 2)
                    for r in range(PAIRS):
                        if r >= 2:
                            pe.wait_ge(sem["clamp"], r - 1)
                        pe.matmul(ps[:, 2 + r % 2, :], k.la[0:LROWS, r // 2, 2 * (r % 2):2 * (r % 2) + 2].rearrange("p j m -> p (j m)"),
                                  a[0:LROWS, r // 2, :], start=True, stop=True).then_inc(sem["c_ps"], 1)
                    for c in range(DC):
                        pe.wait_ge(sem["phi"], 4 * c + 4)
                        for w in range(2):
                            for r in range(4 * c, 4 * c + 4):
                                mm = pe.matmul(ps[32 * (r % 4):32 * (r % 4) + 32, 4 + 2 * w + c, :], k.y[:, r, w, :], phi[:, r, :],
                                               start=True, stop=True, tile_position=(0, 32 * (r % 4)), skip_group_check=True)
                        mm.then_inc(sem["n_ps"], 1)
                    pe.wait_ge(sem["on"], DC)
                    for s in range(SUB):
                        for c in range(DC):
                            mm = pe.matmul(ps[:, s // 2, (s % 2) * D:(s % 2 + 1) * D], ot[:, c, s * P:(s + 1) * P], k.wo1[:, c, :],
                                           start=(c == 0), stop=(c == DC - 1))
                        mm.then_inc(sem["o_ps"], 1)
                    transpose_tile(pe, ps, 2, xn, k.ident, sem["xn"], 0, sem["xt_ps"])
                    pe.wait_ge(sem["xt"], 1)
                    for s in range(SUB):
                        for c in range(DC):
                            mm = pe.matmul(ps[:, 4 + s // 2, (s % 2) * D:(s % 2 + 1) * D], xt4[:, c, s * P:(s + 1) * P], k.wf[:, c, :],
                                           start=(c == 0), stop=(c == DC - 1))
                        mm.then_inc(sem["f_ps"], 1)

                @block.vector
                def _(dve):
                    ch = Chain(dve, sem["dve"])
                    operand_dve(dve, ps, a, k.bq1, sem, 2)
                    for r in range(PAIRS):
                        dve.wait_ge(sem["c_ps"], r + 1)
                        if r >= 2:
                            dve.wait_ge(sem["phi"], r - 1)
                        dve.tensor_scalar(cl[:, r % 2], ps[:, 2 + r % 2, :], 0.0, None, ALU.max).then_inc(sem["clamp"], 1)
                    for c in range(DC):
                        dve.wait_ge(sem["n_ps"], c + 1)
                        ch.link(dve.tensor_scalar(nr[:, c], ps[:, 6 + c, :], NORM_MIN, None, ALU.max))
                        ch.link(dve.reciprocal(nr[:, c], nr[:, c]))
                        dve.tensor_tensor(ot[:, c], ps[:, 4 + c, :], nr[:, c], ALU.mult).then_inc(sem["on"], 1)
                    dve.wait_ge(sem["xb"], 1)
                    for s in range(SUB):
                        dve.wait_ge(sem["o_ps"], 2 * (s // 2) + 2)
                        ch.step(dve.tensor_tensor(x3[:, s, :], xb[:, s, :], ps[:, s // 2, (s % 2) * D:(s % 2 + 1) * D], ALU.add))
                    ch.wait()
                    ln_stats(dve, ch, x3, st, mv, sem["var"])
                    ln_apply(dve, x3, xn, mv, rstd, sem["rstd"], 1, sem["xn"])
                    for s in range(SUB):
                        dve.wait_ge(sem["f_ps"], 2 * (s // 2) + 2)
                        dve.tensor_tensor(x4[:, s, :], x3[:, s, :], ps[:, 4 + s // 2, (s % 2) * D:(s % 2 + 1) * D], ALU.add).then_inc(sem["res"], 1)

                @block.gpsimd
                def _(pool):
                    ch = Chain(pool, sem["pool"])
                    pool.tensor_tensor(xb[:], k.x2[:, bass.ds(i * SUB, SUB), :], bc(k.bo1[:, :], 1, [P, SUB, D]), ALU.add).then_inc(sem["xb"], 1)
                    ln_rstd(pool, ch, mv, rstd, k.neghalf, sem["var"], SUB, sem["rstd"])

                @block.scalar
                def _(act):
                    operand_act(act, ps, a, k.bq1, sq, sem, 2)
                    for r in range(PAIRS):
                        act.wait_ge(sem["clamp"], r + 1)
                        act.activation(phi[:, r], cl[:, r % 2], ACT.Exp, scale=k.negt[:, 0:1]).then_inc(sem["phi"], 1)
                    act.wait_ge(sem["xt_ps"], 1)
                    act.activation(xt4[:], ps[:, 2:4, :], ACT.Copy).then_inc(sem["xt"], 1)
            nc.all_engine_barrier(sems_to_clear=cleared(sem))



class Names:
    pass


def build(nc, io, out, stages=("project", "attend", "mix", "landmarks", "queries")):
    scr = Names()
    scr.q = nc.dram_tensor("q_parts", (3, D, N), BF16, kind="Internal").ap()
    scr.k = nc.dram_tensor("k_parts", (3, D, N), BF16, kind="Internal").ap()
    scr.v = nc.dram_tensor("v_ones", (N, H * 2 * DH), F32, kind="Internal").ap()
    scr.o = nc.dram_tensor("attn_sums", (H * 2 * DH, N), F32, kind="Internal").ap()
    scr.w = nc.dram_tensor("kernel_matrix", (H, M, M), F32, kind="Internal").ap()
    scr.wi = nc.dram_tensor("kernel_inverse", (H, M, M), F32, kind="Internal").ap()
    with ExitStack() as ctx:
        sb = lambda n, shape, dt=F32: ctx.enter_context(nc.sbuf_tensor(n, shape, dt))
        ps = ctx.enter_context(nc.psum_tensor("ps", [P, 8, T], F32))
        k = Names()
        k.loop_sems = [ctx.enter_context(nc.semaphore(f"loop_{i}")) for i in range(LOOP_SEMS)]
        assert [s.num for s in k.loop_sems] == list(range(k.loop_sems[0].num, k.loop_sems[0].num + LOOP_SEMS))
        k.wq1, k.wk1, k.wv1, k.wo1, k.wf = (sb(n, [P, DC, D]) for n in ("wq1", "wk1", "wv1", "wo1", "wf"))
        k.gate_w = sb("gate_wt", [P, DC, E])
        k.gate_b = sb("gate_bias", [P, E])
        k.bq1, k.bk1 = sb("bq1", [P, DC]), sb("bk1", [P, DC])
        k.bv1, k.bo1 = sb("bv1", [P, D]), sb("bo1", [P, D])
        k.negt = sb("negt", [P, 1])
        k.ident, k.identb = sb("ident", [P, P]), sb("identb", [P, P], BF16)
        k.mask_kq, k.mask_qk = sb("mask_kq", [P, P], BF16), sb("mask_qk", [P, P], BF16)
        k.neghalf, k.ones = sb("neghalf", [P, SUB]), sb("ones", [P, 1])
        k.quarter = sb("quarter", [64, 1])
        k.half = sb("half", [P, 2])
        k.sel = sb("sel", [64, 32])
        k.blk2 = sb("blk2", [64, G, M])
        k.blk1 = sb("blk1", [P, G, M])
        k.headmask = sb("headmask", [P, 8, M])
        k.regi = sb("regi", [M, M])
        k.before = sb("before", [P, E, E])
        k.spread = sb("spread", [P, 8, P])
        k.unit = sb("unit", [P, 2 * M - 1])
        k.own = sb("own", [P, 8 * 8 * 8])
        k.idx, k.tok = sb("idx_f", [P, M]), sb("tok", [P, SUB])
        setup(nc, io, k, ps)
        if "project" in stages:
            project(nc, io, k, ps, scr)
        if "attend" in stages:
            attend(nc, io, k, ps, scr)
        if "mix" in stages:
            k.x2, k.xn3t = sb("x2", [P, N // P, D]), sb("xn3t", [P, DC, N])
            k.lxt = sb("lxt", [P, DC, M])
            mix(nc, io, k, ps, scr)
        if "landmarks" in stages:
            k.la, k.y = sb("la", [P, G, G, M]), sb("y", [P, PAIRS, 2, 32])
            landmarks(nc, io, k, ps, scr)
        if "queries" in stages:
            queries(nc, io, k, ps, out)
    return scr


_INS = ["L0_attn_x", "L0_attn_Wq", "L0_attn_Wk", "L0_attn_Wv", "L0_attn_Wout", "L0_ffn_gate_w", "L0_ffn_gate_b",
        "L0_ffn_expert_w", "L0_ffn_expert_b", "L1_attn_Wq", "L1_attn_bq", "L1_attn_Wk", "L1_attn_bk", "L1_attn_Wv",
        "L1_attn_bv", "L1_attn_Wo", "L1_attn_bo", "L1_attn_temperature", "L1_attn_landmark_idx", "L1_ffn_weight"]


def kernel(**inputs):
    import numpy as _np
    import concourse.bacc as _bacc
    from concourse import mybir as _mybir
    from concourse.bass_utils import run_bass_kernel_spmd as _run

    nc = _bacc.Bacc("TRN2", target_bir_lowering=False, num_devices=1)
    arrays, io = {}, {}
    for name in _INS:
        a = _np.ascontiguousarray(inputs[name])
        if a.ndim == 0:
            a = a.reshape(1)
        arrays[f"in_{name}"] = a
        io[name] = nc.dram_tensor(f"in_{name}", a.shape, _mybir.dt.from_np(a.dtype), kind="ExternalInput").ap()
    out = nc.dram_tensor("out_x", (1, N, D), F32, kind="ExternalOutput").ap()
    build(nc, io, out)
    r = _run(nc, [arrays], core_ids=[0])
    return r.results[0]["out_x"]
```

```python
from contextlib import ExitStack

import concourse.bass as bass
from concourse import mybir

F32 = mybir.dt.float32
BF16 = mybir.dt.bfloat16
I32 = mybir.dt.int32
ALU = mybir.AluOpType
ACT = mybir.ActivationFunctionType
AX = mybir.AxisListType.X

P = 128
N = 4096
D = 256
DC = D // P
H = 16
DH = D // H
T = 512
NT = N // T
SUB = T // P
G = 4
NG = H // G
E = 8
TOP = 2
M = 64
PAIRS = H // 2
LN_EPS = 1e-5
REG = 1e-6
NORM_MIN = 1e-10
MASKED = -3.0e38


def stage_sems(ctx, nc, stage, names):
    return {n: ctx.enter_context(nc.semaphore(f"{stage}_{n}")) for n in names}


def loop_sems(pool, names):
    assert len(names) <= len(pool)
    return dict(zip(names, pool))


def cleared(sems):
    nums = [s.num for s in sems.values()]
    return range(min(nums), max(nums) + 1)


LOOP_SEMS = 52


class Chain:

    def __init__(self, eng, sem):
        self.eng, self.sem, self.n = eng, sem, 0

    def step(self, ins):
        ins.then_inc(self.sem, 1)
        self.n += 1

    def wait(self):
        self.eng.wait_ge(self.sem, self.n)

    def link(self, ins):
        self.step(ins)
        self.wait()


def bc(ap, axis, shape):
    return ap.unsqueeze(axis).broadcast_to(shape)



def ln_stats(dve, ch, x, st, mv, s_var):
    for s in range(SUB):
        ch.step(dve.bn_stats(st[:, s, :], x[:, s, :]))
    ch.wait()
    for s in range(SUB):
        dve.bn_aggr(mv[:, s, :], st[:, s, :]).then_inc(s_var, 1)


def ln_rstd(pool, ch, mv, rstd, neghalf, s_var, n_var, s_rstd):
    pool.wait_ge(s_var, n_var)
    ch.link(pool.tensor_scalar(rstd[:, :], mv[:, :, 1], LN_EPS, None, ALU.add))
    pool.tensor_tensor(rstd[:, :], rstd[:, :], neghalf[:, 0:SUB], ALU.pow).then_inc(s_rstd, 1)


def ln_apply(dve, x, xn, mv, rstd, s_rstd, n_rstd, s_xn):
    dve.wait_ge(s_rstd, n_rstd)
    for s in range(SUB):
        dve.tensor_scalar(xn[:, s, :], x[:, s, :], mv[:, s, 0:1], rstd[:, s:s + 1],
                          ALU.subtract, ALU.mult).then_inc(s_xn, 1)


def transpose_tile(pe, ps, bank, xn, ident, s_xn, n_xn, s_ps):
    for s in range(SUB):
        pe.wait_ge(s_xn, n_xn + s + 1)
        for c in range(DC):
            last = pe.transpose(ps[:, bank + c, s * P:(s + 1) * P], xn[:, s, c * P:(c + 1) * P], ident[:, :])
    last.then_inc(s_ps, 1)



def setup(nc, io, k, ps):
    names = ["w_in", "sgn_in", "gate_in", "small_in", "pool", "dve", "id_ok", "tr_ps", "tr_sb", "sgn"]
    with ExitStack() as ctx:
        sem = stage_sems(ctx, nc, "setup", names)
        raw = ctx.enter_context(nc.sbuf_tensor("raw", [P, 5, DC, D], F32))
        sgn = ctx.enter_context(nc.sbuf_tensor("sgn", [P, DC, D], F32))
        neg = ctx.enter_context(nc.sbuf_tensor("neg", [P, DC, D], F32))
        graw = ctx.enter_context(nc.sbuf_tensor("graw", [E, D], F32))
        zeros = ctx.enter_context(nc.sbuf_tensor("zeros", [P, 8, P], F32))
        idx = ctx.enter_context(nc.sbuf_tensor("idx", [P, M], I32))
        under = ctx.enter_context(nc.sbuf_tensor("under", [P, M], F32))
        m8 = ctx.enter_context(nc.sbuf_tensor("m8", [P, 8], F32))
        i8 = ctx.enter_context(nc.sbuf_tensor("i8", [P, 8, 8], F32))
        weights = [("L1_attn_Wq", k.wq1), ("L1_attn_Wk", k.wk1), ("L1_attn_Wv", k.wv1), ("L1_attn_Wo", k.wo1),
                   ("L1_ffn_weight", k.wf)]
        with nc.Block() as block:
            @block.sync
            def _(sp):
                for i, (name, _) in enumerate(weights):
                    sp.dma_start(raw[:, i], io[name].rearrange("(c p) n -> p c n", p=P)).then_inc(sem["w_in"], 16)
                sp.dma_start(graw[:, :], io["L0_ffn_gate_w"]).then_inc(sem["gate_in"], 16)
                for tile, ap in ((k.bq1, io["L1_attn_bq"]), (k.bk1, io["L1_attn_bk"])):
                    sp.dma_start(tile[:, :], ap.rearrange("(c p) -> p c", p=P),
                                 allow_slow_non_contiguous=True).then_inc(sem["small_in"], 16)
                for tile, ap in ((k.bv1, io["L1_attn_bv"]), (k.bo1, io["L1_attn_bo"]), (k.gate_b, io["L0_ffn_gate_b"]),
                                 (idx, io["L1_attn_landmark_idx"]), (k.negt, io["L1_attn_temperature"])):
                    sp.dma_start(tile[:, :], ap.partition_broadcast(P)).then_inc(sem["small_in"], 16)

            @block.gpsimd
            def _(pool):
                ch = Chain(pool, sem["pool"])
                for tile, v in ((zeros, 0.0), (k.neghalf, -0.5), (k.ones, 1.0), (k.blk2, -2.0), (k.headmask, 1.0),
                                (k.sel, 1.0), (k.quarter, 0.25), (k.half, 0.0)):
                    ch.link(pool.memset(tile[:], v))
                ch.link(pool.memset(k.blk1[:], 0.0))
                ch.wait()
                ch.link(pool.memset(k.half[0:64, 0:1], 1.0))
                ch.link(pool.memset(k.half[64:128, 1:2], 1.0))
                z = zeros[:, 0, :]
                pool.affine_select(out=k.ident[:, :], in_=z, pattern=[[-1, P]], compare_op=ALU.not_equal, fill=1.0,
                                   base=0, channel_multiplier=1).then_inc(sem["id_ok"], 1)
                pool.wait_ge(sem["id_ok"], 1)
                ch.link(pool.affine_select(out=k.identb[:, :], in_=z, pattern=[[-1, P]], compare_op=ALU.not_equal,
                                           fill=1.0, base=0, channel_multiplier=1))
                ch.link(pool.affine_select(out=k.mask_kq[:, :], in_=z, pattern=[[1, P]], compare_op=ALU.is_ge,
                                           fill=MASKED, base=0, channel_multiplier=-1))
                ch.link(pool.affine_select(out=k.mask_qk[:, :], in_=z, pattern=[[-1, P]], compare_op=ALU.is_ge,
                                           fill=MASKED, base=0, channel_multiplier=1))
                for tile, pat, rows in ((k.sel, [[-DH, 32]], 64), (k.blk2, [[-DH, G], [0, M]], 64),
                                        (k.headmask, [[-DH, 8], [0, M]], P)):
                    ch.link(pool.affine_select(out=tile[:], in_=tile[:], pattern=pat, compare_op=ALU.is_ge,
                                               fill=0.0, base=0, channel_multiplier=1))
                    ch.link(pool.affine_select(out=tile[:], in_=tile[:], pattern=[[-s, n] for s, n in pat],
                                               compare_op=ALU.is_ge, fill=0.0, base=DH - 1, channel_multiplier=-1))
                ch.link(pool.affine_select(out=k.blk1[64:96], in_=k.blk1[64:96], pattern=[[-1, G], [0, M]],
                                           compare_op=ALU.not_equal, fill=1.0, base=0, channel_multiplier=1))
                ch.link(pool.affine_select(out=k.regi[:, :], in_=z[0:M, 0:M], pattern=[[-1, M]],
                                           compare_op=ALU.not_equal, fill=REG, base=0, channel_multiplier=1))
                ch.link(pool.affine_select(out=k.before[:, :, :], in_=zeros[:, 0, 0:64].rearrange("p (a b) -> p a b", a=8),
                                           pattern=[[-1, E], [1, E]], compare_op=ALU.is_ge, fill=1.0, base=0,
                                           channel_multiplier=0))
                ch.link(pool.affine_select(out=k.spread[:, :, :], in_=zeros[:, :, :].rearrange("p c (h r) -> p c h r", r=8),
                                           pattern=[[-1, 8], [-8, H], [0, 8]], compare_op=ALU.not_equal, fill=1.0,
                                           base=0, channel_multiplier=1))
                ch.link(pool.affine_select(out=i8[:, :, :], in_=zeros[:, 0, 0:64].rearrange("p (a b) -> p a b", a=8),
                                           pattern=[[-1, 8], [1, 8]], compare_op=ALU.not_equal, fill=1.0, base=0,
                                           channel_multiplier=0))
                ch.link(pool.affine_select(out=k.unit[:, :], in_=zeros[:, 0, 0:2 * M - 1], pattern=[[1, 2 * M - 1]],
                                           compare_op=ALU.not_equal, fill=1.0, base=1 - M, channel_multiplier=0))
                ch.link(pool.iota(k.tok[:, :], pattern=[[P, SUB]], base=0, channel_multiplier=1,
                                  allow_small_or_imprecise_dtypes=True))
                ch.wait()
                pool.engine_nop().then_inc(sem["id_ok"], 1)

            @block.tensor
            def _(pe):
                pe.wait_ge(sem["id_ok"], 1)
                pe.wait_ge(sem["w_in"], 80)
                for i in range(5):
                    src = sgn if i == 4 else raw[:, i]
                    if i == 4:
                        pe.wait_ge(sem["sgn"], 1)
                    if i >= 2:
                        pe.wait_ge(sem["tr_sb"], i - 1)
                    for oc in range(DC):
                        for ic in range(DC):
                            last = pe.transpose(ps[:, 2 * (i % 2) + ic, oc * P:(oc + 1) * P],
                                                src[:, oc, ic * P:(ic + 1) * P], k.ident[:, :])
                    last.then_inc(sem["tr_ps"], 1)
                pe.wait_ge(sem["gate_in"], 16)
                for ic in range(DC):
                    last = pe.transpose(ps[:, 4, ic * E:(ic + 1) * E], graw[:, ic * P:(ic + 1) * P],
                                        k.ident[0:E, 0:E])
                last.then_inc(sem["tr_ps"], 1)

            @block.vector
            def _(dve):
                ch = Chain(dve, sem["dve"])
                dve.wait_ge(sem["w_in"], 80)
                ch.step(dve.tensor_scalar(sgn[:], raw[:, 4], 0.0, None, ALU.is_gt))
                ch.step(dve.tensor_scalar(neg[:], raw[:, 4], 0.0, None, ALU.is_lt))
                ch.wait()
                dve.tensor_tensor(sgn[:], sgn[:], neg[:], ALU.subtract).then_inc(sem["sgn"], 1)
                for i, (_, dst) in enumerate(weights):
                    dve.wait_ge(sem["tr_ps"], i + 1)
                    b = 2 * (i % 2)
                    dve.tensor_copy(dst[:, :, :], ps[:, b:b + DC, 0:D]).then_inc(sem["tr_sb"], 1)
                dve.wait_ge(sem["tr_ps"], 6)
                ch.step(dve.tensor_copy(k.gate_w[:, :, :], ps[:, 4, 0:DC * E].rearrange("p (c e) -> p c e", c=DC)))
                dve.wait_ge(sem["small_in"], 16 * 7)
                ch.link(dve.tensor_copy(k.idx[:, :], idx[:, :]))
                ch.link(dve.tensor_scalar(under[:, :], k.idx[:, :], 0.0, float(N), ALU.is_lt, ALU.mult))
                ch.link(dve.tensor_tensor(k.idx[:, :], k.idx[:, :], under[:, :], ALU.add))
                ch.step(dve.tensor_scalar(k.idx[:, :], k.idx[:, :], 0.0, float(N - 1), ALU.max, ALU.min))
                ch.link(dve.reciprocal(k.negt[:, :], k.negt[:, :]))
                ch.step(dve.tensor_scalar(k.negt[:, :], k.negt[:, :], -1.0, None, ALU.mult))
                dve.wait_ge(sem["id_ok"], 2)
                ch.link(dve.tensor_reduce(m8[:, :], k.spread[:, :, :], AX, ALU.max))
                ch.step(dve.tensor_tensor(k.own[:, :].rearrange("p (a b c) -> p a b c", a=8, b=8),
                                          bc(bc(m8[:, :], 2, [P, 8, 8]), 3, [P, 8, 8, 8]),
                                          bc(i8[:, :, :], 1, [P, 8, 8, 8]), ALU.mult))



def project(nc, io, k, ps, scr):
    XP, QP, VP = 0, 2, 6
    names = ["x_in", "dve", "pool", "var", "rstd", "xn", "xt_ps", "xt", "qk_ps", "v_ps", "p1", "rest", "p2", "p3", "v", "out"]
    with ExitStack() as ctx:
        sb = lambda n, shape, dt=F32: ctx.enter_context(nc.sbuf_tensor(n, shape, dt))
        wsem = stage_sems(ctx, nc, "projw", ["in_", "ones"])
        sem = loop_sems(k.loop_sems, names)
        w = sb("w_qkv", [P, 3, DC, D])
        x = sb("x_a", [P, SUB, D])
        xn = sb("xn_a", [P, SUB, D])
        st = sb("st_a", [P, SUB, 6])
        mv = sb("mv_a", [P, SUB, 2])
        rstd = sb("rstd_a", [P, SUB])
        xt = sb("xt_a", [P, DC, T])
        part = sb("part", [P, 2, 3, DC, T], BF16)
        rest = sb("rest", [P, 4, T])
        v = sb("v_a", [P, SUB, H, 2 * DH])
        scale = (DH ** -0.5, 1.0)
        with nc.Block() as block:
            @block.sync
            def _(sp):
                for i, name in enumerate(("L0_attn_Wq", "L0_attn_Wk", "L0_attn_Wv")):
                    sp.dma_start(w[:, i], io[name].rearrange("(c p) h e -> p c (h e)", p=P)).then_inc(wsem["in_"], 16)
                sp.wait_ge(wsem["in_"], 48)

            @block.gpsimd
            def _(pool):
                pool.memset(v[:, :, :, DH:2 * DH], 1.0).then_inc(wsem["ones"], 1)
                pool.wait_ge(wsem["ones"], 1)

        def step(i, start, products):
            with nc.Block() as block:
                @block.sync
                def _(sp):
                    if start:
                        sp.dma_start(x[:], io["L0_attn_x"].rearrange("o (i s p) d -> (o i) p s d", s=SUB, p=P)[i + 1]).then_inc(sem["x_in"], 16)
                    if products:
                        for a, dst in ((0, scr.q), (1, scr.k)):
                            for n, made in enumerate(("p1", "p2", "p3")):
                                sp.wait_ge(sem[made], 2 * (a + 1))
                                sp.dma_start(dst.rearrange("a (c p) (i n) -> i a p c n", c=DC, n=T)[i, n],
                                             part[:, a, n]).then_inc(sem["out"], 16)
                        sp.wait_ge(sem["v"], 1)
                        sp.dma_start(scr.v.rearrange("(i s p) n -> i p s n", s=SUB, p=P)[i],
                                     v[:].rearrange("p s h e -> p s (h e)")).then_inc(sem["out"], 16)
                        sp.wait_ge(sem["out"], 16 * 7)

                @block.vector
                def _(dve):
                    ch = Chain(dve, sem["dve"])

                    def remainder(o):
                        a, c = o // DC, o % DC
                        dve.wait_ge(sem["p1"], o + 1)
                        dve.scalar_tensor_tensor(out=rest[:, o, :], in0=ps[:, QP + o, :], scalar=scale[a], in1=part[:, a, 0, c, :],
                                                 op0=ALU.mult, op1=ALU.subtract).then_inc(sem["rest"], 1)

                    if products:
                        remainder(0)
                        remainder(1)
                    if start:
                        dve.wait_ge(sem["x_in"], 16)
                        ln_stats(dve, ch, x, st, mv, sem["var"])
                    if products:
                        remainder(2)
                    if start:
                        ln_apply(dve, x, xn, mv, rstd, sem["rstd"], 1, sem["xn"])
                    if products:
                        remainder(3)

                @block.gpsimd
                def _(pool):
                    ch = Chain(pool, sem["pool"])
                    for o in range(4):
                        if products:
                            a, c = o // DC, o % DC
                            pool.wait_ge(sem["p2"], o + 1)
                            pool.tensor_tensor(part[:, a, 2, c, :], rest[:, o, :], part[:, a, 1, c, :], ALU.subtract).then_inc(sem["p3"], 1)
                        if start and o == 1:
                            ln_rstd(pool, ch, mv, rstd, k.neghalf, sem["var"], SUB, sem["rstd"])

                @block.tensor
                def _(pe):
                    if products:
                        for o in range(4):
                            a, c = o // DC, o % DC
                            for ic in range(DC):
                                mm = pe.matmul(ps[:, QP + o, :], w[:, a, ic, c * P:(c + 1) * P], xt[:, ic, :],
                                               start=(ic == 0), stop=(ic == DC - 1))
                            mm.then_inc(sem["qk_ps"], 1)
                        for s in range(SUB):
                            for ic in range(DC):
                                mm = pe.matmul(ps[:, VP + s // 2, (s % 2) * D:(s % 2 + 1) * D], xt[:, ic, s * P:(s + 1) * P],
                                               w[:, 2, ic, :], start=(ic == 0), stop=(ic == DC - 1))
                        mm.then_inc(sem["v_ps"], 1)
                    if start:
                        transpose_tile(pe, ps, XP, xn, k.ident, sem["xn"], 0, sem["xt_ps"])

                @block.scalar
                def _(act):
                    def second(o):
                        a, c = o // DC, o % DC
                        act.wait_ge(sem["rest"], o + 1)
                        act.activation(part[:, a, 1, c, :], rest[:, o, :], ACT.Copy).then_inc(sem["p2"], 1)

                    if products:
                        for o in range(4):
                            a, c = o // DC, o % DC
                            act.wait_ge(sem["qk_ps"], o + 1)
                            act.activation(part[:, a, 0, c, :], ps[:, QP + o, :], ACT.Copy, scale=scale[a]).then_inc(sem["p1"], 1)
                            if o:
                                second(o - 1)
                        second(3)
                        act.wait_ge(sem["v_ps"], 1)
                        act.activation(v[:, :, :, 0:DH],
                                       ps[:, VP:VP + 2, :].rearrange("p b (s h e) -> p (b s) h e", s=2, e=DH), ACT.Copy).then_inc(sem["v"], 1)
                    if start:
                        act.wait_ge(sem["xt_ps"], 1)
                        act.activation(xt[:, :, :], ps[:, XP:XP + DC, :], ACT.Copy).then_inc(sem["xt"], 1)
            nc.all_engine_barrier(sems_to_clear=cleared(sem))

        step(-1, start=True, products=False)
        with nc.Fori(0, NT - 1) as i:
            step(i, start=True, products=True)
        step(NT - 1, start=False, products=True)



TILES = [2, 7, 6, 5, 4, 3, 1, 0]
QSLOTS = 4
KROWS = 6 * DH
SROWS = KROWS + 2
QPARTS = (0, 0, 1, 1, 0, 2)
KPARTS = (0, 1, 0, 1, 2, 0)
MAXSLOTS = 3


def attend_schedule():
    HOP, ROWS_IN, LOAD, COPY = 0.15, 2.5, 2.5, 0.6
    never = 1e9
    chunks = [(n, c) for n, t in enumerate(TILES) for c in range(SUB * (t + 1))]
    last = [chunks.index((n, SUB * (t + 1) - 1)) for n, t in enumerate(TILES)]
    maxima = [(n, s, b, j) for n, t in enumerate(TILES) for s in range(SUB) for b in range(t + 1) for j in range(G)]
    order = []
    pe = act = dve = copied = 0.0
    exp_end, scores_end, summed, ring_end, max_end, rows = [], [], [], [], {}, {}
    at = {"a": 0, "t": 0, "s": 0, "m": 0}

    def width(n, c):
        return T - P * max(0, c - SUB * TILES[n])

    def ring_free():
        return ring_end[-MAXSLOTS] + HOP if len(ring_end) >= MAXSLOTS else 0.0

    while at["s"] < 2 * len(chunks) or at["a"] < len(chunks):
        ready = {}
        if at["a"] < len(chunks) and at["s"] >= 2 * at["a"] + 2:
            ready["a"] = exp_end[2 * at["a"] + 1] + HOP
            if chunks[at["a"]][1] == 0:
                ready["a"] = max(ready["a"], copied + HOP)
        if at["t"] in max_end:
            ready["t"] = max(max_end[at["t"]] + HOP, ring_free())
        if at["s"] < 2 * len(chunks):
            q = at["s"] // 2
            n, c = chunks[q]
            if at["a"] >= q - 1 and (c > 0 or n in rows):
                ready["s"] = max(rows[n], exp_end[at["s"] - 2] + HOP if at["s"] >= 2 else 0.0)
        if at["m"] < len(maxima):
            n = maxima[at["m"]][0]
            load = scores_end[2 * last[n - QSLOTS] + 1] + LOAD if n >= QSLOTS and len(scores_end) > 2 * last[n - QSLOTS] + 1 else \
                never if n >= QSLOTS else 0.0
            if load < never:
                ready["m"] = max(load, ring_free())
        kind = min(ready, key=lambda x: (max(pe, ready[x]), "atsm".index(x)))
        start = max(pe, ready[kind])
        i = at[kind]
        at[kind] += 1
        if kind == "a":
            n, c = chunks[i]
            pe = start + width(n, c) * 4 / 2400
            summed.append(pe)
            if i == last[n]:
                act = copied = max(act, pe + HOP) + COPY
            order.append(("a", n, c))
        elif kind == "t":
            pe = start + 0.24
            dve = max(dve, pe + HOP) + 0.62
            ring_end.append(dve)
            rows[i] = dve + ROWS_IN
            order.append(("t", i))
        elif kind == "s":
            q = i // 2
            n, c = chunks[q]
            pe = start + 2 * width(n, c) / 2400 + (0.11 if c >= SUB * TILES[n] else 0.0)
            scores_end.append(pe)
            act = max(act, pe + HOP, summed[q - 2] + HOP if q >= 2 else 0.0) + 2 * width(n, c) / 1200 + 0.1
            exp_end.append(act)
            order.append(("s", n, c, i % 2))
        else:
            n, s, b, j = maxima[i]
            w = T if b < TILES[n] else (s + 1) * P
            pe = start + w / 2400 + (0.06 if b == TILES[n] else 0.0)
            dve = max(dve, pe + HOP) + w / 960 + 0.08
            ring_end.append(dve)
            if (s, b, j) == (SUB - 1, TILES[n], G - 1):
                dve += 0.45
                max_end[n] = dve
            order.append(("m", n, s, b, j))
    return order


def attend(nc, io, k, ps, scr):
    steps = attend_schedule()
    chunks = [(n, c) for n, t in enumerate(TILES) for c in range(SUB * (t + 1))]
    chunk_no = {nc_: i for i, nc_ in enumerate(chunks)}
    last_chunk = [chunk_no[(n, SUB * (t + 1) - 1)] for n, t in enumerate(TILES)]
    ring = [st for st in steps if st[0] in "mt"]
    ring_no = {u: i for i, u in enumerate(ring)}
    NTL = len(TILES)

    def off(n, c):
        return max(0, c - SUB * TILES[n]) * P

    names = [f"k_in{i}" for i in range(NT)] + [f"v_in{i}" for i in range(NT)] + [f"q_in{n}" for n in range(NTL)] + \
            [f"rows_in{n}" for n in range(NTL)] + [f"stored{n}" for n in range(NTL)] + \
            ["scores", "probs", "summed", "max_ps", "max_used", "neg_max", "turned", "out_sb", "dve"]
    with ExitStack() as ctx:
        sb = lambda n, shape, dt=F32: ctx.enter_context(nc.sbuf_tensor(n, shape, dt))
        wsem = stage_sems(ctx, nc, "attnw", ["ones"])
        sem = loop_sems(k.loop_sems, names)
        k_in, v_in = [sem[f"k_in{i}"] for i in range(NT)], [sem[f"v_in{i}"] for i in range(NT)]
        q_in, rows_in, stored = ([sem[f"{x}{n}"] for n in range(NTL)] for x in ("q_in", "rows_in", "stored"))
        kb = sb("kb", [P, G, N], BF16)
        qb = sb("qb", [P, QSLOTS, G, T], BF16)
        vb = sb("vb", [P, N // P, G * 2 * DH])
        pb = sb("pb", [P, 4, 2, T])
        mx = sb("mx", [P, 2, G, SUB, NT])
        nm = sb("nm", [P, G, SUB])
        cb = sb("cb", [P, 2, SUB, G, 2], BF16)
        cr = sb("cr", [2 * G, 2, T], BF16)
        ob = sb("ob", [P, QSLOTS, T])
        AV, RING = 4, 5
        with nc.Block() as block:
            @block.vector
            def _(dve):
                dve.memset(kb[KROWS:SROWS, :, :], 1.0).then_inc(wsem["ones"], 1)
                dve.wait_ge(wsem["ones"], 1)
        with nc.Fori(0, NG) as g:
            with nc.Block() as block:
                @block.sync
                def _(sp):
                    qv = scr.q.rearrange("a (g j d) n -> a g d j n", g=NG, j=G)
                    kv = scr.k.rearrange("a (g j d) n -> a g d j n", g=NG, j=G)
                    vv = scr.v.rearrange("(c p) (g m) -> g p c m", p=P, g=NG)
                    ov = scr.o.rearrange("(g r) n -> g r n", g=NG)

                    def load_q(n):
                        if n >= QSLOTS:
                            sp.wait_ge(sem["scores"], 2 * (last_chunk[n - QSLOTS] + 1))
                        for r, a in enumerate(QPARTS):
                            sp.dma_start(qb[r * DH:(r + 1) * DH, n % QSLOTS],
                                         qv[a, g][:, :, TILES[n] * T:(TILES[n] + 1) * T]).then_inc(q_in[n], 16)

                    def load_k(i):
                        for r, a in enumerate(KPARTS):
                            sp.dma_start(kb[r * DH:(r + 1) * DH, :, i * T:(i + 1) * T],
                                         kv[a, g][:, :, i * T:(i + 1) * T]).then_inc(k_in[i], 16)

                    def load_v(i):
                        sp.dma_start(vb[:, i * SUB:(i + 1) * SUB], vv[g][:, i * SUB:(i + 1) * SUB]).then_inc(v_in[i], 16)

                    def store(n):
                        sp.wait_ge(sem["out_sb"], n + 1)
                        sp.dma_start(ov[g][:, TILES[n] * T:(TILES[n] + 1) * T], ob[:, n % QSLOTS]).then_inc(stored[n], 16)

                    def send_rows(n):
                        sp.wait_ge(sem["turned"], n + 1)
                        for j in range(G):
                            sp.dma_start(qb[KROWS:SROWS, n % QSLOTS, j], cr[2 * j:2 * j + 2, n % 2]).then_inc(rows_in[n], 16)

                    load_q(0)
                    load_k(0)
                    load_k(1)
                    load_q(1)
                    load_v(0)
                    load_v(1)
                    for i in range(2, NT):
                        load_k(i)
                        load_v(i)
                        if i % 2 == 1 and (i + 1) // 2 < QSLOTS:
                            load_q((i + 1) // 2)
                    send_rows(0)
                    for n in range(NTL):
                        if n + 1 < NTL:
                            send_rows(n + 1)
                        if n + QSLOTS < NTL:
                            load_q(n + QSLOTS)
                        store(n)
                    for n in range(NTL):
                        sp.wait_ge(stored[n], 16)

                @block.tensor
                def _(pe):
                    def ring_bank(u):
                        i = ring_no[u]
                        if i >= MAXSLOTS:
                            pe.wait_ge(sem["max_used"], i - MAXSLOTS + 1)
                        return RING + i % MAXSLOTS

                    seen_k = seen_v = 0
                    for st in steps:
                        n = st[1]
                        t = TILES[n]
                        if st[0] == "m":
                            s, b, j = st[2:]
                            if (s, b, j) == (0, 0, 0):
                                pe.wait_ge(q_in[n], 16 * len(QPARTS))
                            while seen_k <= b:
                                pe.wait_ge(k_in[seen_k], 16 * len(KPARTS))
                                seen_k += 1
                            width = T if b < t else (s + 1) * P
                            bank = ring_bank(st)
                            mm = pe.matmul(ps[:, bank, 0:width], qb[0:KROWS, n % QSLOTS, j, s * P:(s + 1) * P],
                                           kb[0:KROWS, j, b * T:b * T + width], start=True, stop=(b < t))
                            if b == t:
                                mm = pe.matmul(ps[:, bank, s * P:width], k.identb[:, :], k.mask_qk[:, :],
                                               start=False, stop=True)
                            mm.then_inc(sem["max_ps"], 1)
                        elif st[0] == "t":
                            pe.wait_ge(sem["neg_max"], n + 1)
                            bank = ring_bank(st)
                            for s in range(SUB):
                                mm = pe.matmul(ps[0:2 * G, bank, s * P:(s + 1) * P], cb[:, n % 2, s, :, :].rearrange("p j a -> p (j a)"),
                                               k.identb[:, :], start=True, stop=True)
                            mm.then_inc(sem["max_ps"], 1)
                        elif st[0] == "s":
                            c, pair = st[2:]
                            u = 2 * chunk_no[(n, c)] + pair
                            o = off(n, c)
                            if c == 0 and pair == 0:
                                pe.wait_ge(rows_in[n], 16 * G)
                            if u >= 2:
                                pe.wait_ge(sem["probs"], u - 1)
                            diagonal = c >= SUB * t
                            for j in (2 * pair, 2 * pair + 1):
                                mm = pe.matmul(ps[:, j, o:T], kb[0:SROWS, j, c * P:(c + 1) * P],
                                               qb[0:SROWS, n % QSLOTS, j, o:T], start=True, stop=not diagonal)
                                if diagonal:
                                    mm = pe.matmul(ps[:, j, o:o + P], k.identb[:, :], k.mask_kq[:, :],
                                                   start=False, stop=True)
                            mm.then_inc(sem["scores"], 1)
                        else:
                            c = st[2]
                            q = chunk_no[(n, c)]
                            o = off(n, c)
                            while seen_v <= c // SUB:
                                pe.wait_ge(v_in[seen_v], 16)
                                seen_v += 1
                            if c == 0 and n > 0:
                                pe.wait_ge(sem["out_sb"], n)
                            pe.wait_ge(sem["probs"], 2 * q + 2)
                            for j in range(G):
                                mm = pe.matmul(ps[32 * j:32 * j + 32, AV, o:T], vb[:, c, 32 * j:32 * j + 32],
                                               pb[:, 2 * (q % 2) + j // 2, j % 2, o:T],
                                               start=(c == 0), stop=(q == last_chunk[n]), tile_position=(0, 32 * j),
                                               skip_group_check=True)
                            mm.then_inc(sem["summed"], 1)

                @block.scalar
                def _(act):
                    def copy_out(n):
                        act.wait_ge(sem["summed"], last_chunk[n] + 1)
                        if n >= QSLOTS:
                            act.wait_ge(stored[n - QSLOTS], 16)
                        act.activation(ob[:, n % QSLOTS], ps[:, AV, :], ACT.Copy).then_inc(sem["out_sb"], 1)

                    for st in steps:
                        n = st[1]
                        if st[0] == "s":
                            c, pair = st[2:]
                            q = chunk_no[(n, c)]
                            o = off(n, c)
                            act.wait_ge(sem["scores"], 2 * q + pair + 1)
                            if q >= 2 and pair == 0:
                                act.wait_ge(sem["summed"], q - 1)
                            act.activation(pb[:, 2 * (q % 2) + pair, :, o:T], ps[:, 2 * pair:2 * pair + 2, o:T],
                                           ACT.Exp).then_inc(sem["probs"], 1)
                        elif st[0] == "a" and chunk_no[st[1:]] == last_chunk[n]:
                            copy_out(n)

                @block.vector
                def _(dve):
                    ch = Chain(dve, sem["dve"])
                    for i, u in enumerate(ring):
                        n = u[1]
                        t = TILES[n]
                        dve.wait_ge(sem["max_ps"], i + 1)
                        bank = RING + i % MAXSLOTS
                        if u[0] == "m":
                            s, b, j = u[2:]
                            width = T if b < t else (s + 1) * P
                            dve.tensor_reduce(mx[:, n % 2, j, s, b:b + 1], ps[:, bank, 0:width], AX, ALU.max)\
                               .then_inc(sem["max_used"], 1)
                            if (s, b, j) == (SUB - 1, t, G - 1):
                                dve.wait_ge(sem["max_used"], i + 1)
                                if n >= 2:
                                    dve.wait_ge(sem["turned"], n - 1)
                                ch.link(dve.tensor_reduce(nm[:, :, :], mx[:, n % 2, :, :, 0:t + 1], AX, ALU.max))
                                nms = nm[:, :, :].rearrange("p j s -> p s j")
                                ch.link(dve.tensor_scalar(cb[:, n % 2, :, :, 0], nms, -1.0, None, ALU.mult))
                                dve.scalar_tensor_tensor(out=cb[:, n % 2, :, :, 1], in0=nms, scalar=-1.0, in1=cb[:, n % 2, :, :, 0],
                                                         op0=ALU.mult, op1=ALU.subtract).then_inc(sem["neg_max"], 1)
                                dve.wait_ge(sem["neg_max"], n + 1)
                        else:
                            if n >= 2:
                                dve.wait_ge(rows_in[n - 2], 16 * G)
                            dve.tensor_copy(cr[:, n % 2, :], ps[0:2 * G, bank, :]).then_inc(sem["turned"], 1)
                            dve.wait_ge(sem["turned"], n + 1)
                            dve.engine_nop().then_inc(sem["max_used"], 1)
            nc.all_engine_barrier(sems_to_clear=cleared(sem))



FINISH_NORM, FINISH_APPLY, START_SCALE, START_ADD, START_APPLY, START_GATE, START_PICK, START_BIAS = 0, 1, 2, 4, 6, 9, 11, 13


def mix(nc, io, k, ps, scr):
    XP, TP, EP, LP = 0, 2, 4, 7
    EBANKS = 3
    UNITS = SUB * E // 2
    names = ["x_in", "o_in", "den_in", "dve", "pool", "on", "o_ps", "var", "rstd", "xn", "tn_ps", "tn", "gl_ps", "expo",
             "expd", "gate", "gt_ps", "gt", "bias_ps", "e_ps", "e_used", "now", "x1_now", "gate_now", "f_var", "f_rstd", "f_xn",
             "f_ps", "f_out", "hot", "l_ps"]
    with ExitStack() as ctx:
        sb = lambda n, shape, dt=F32: ctx.enter_context(nc.sbuf_tensor(n, shape, dt))
        wsem = stage_sems(ctx, nc, "mixw", ["in_", "zero", "lrow", "lt_ps", "lt", "den", "inv", "stored"])
        sem = loop_sems(k.loop_sems, names)
        wout, we, eb = sb("w_out", [P, DC, D]), sb("w_e", [P, DC, E, D]), sb("e_bias", [E, D])
        o, den = sb("o_c", [P, DC, T]), sb("den_c", [P, DC, T])
        x = sb("x_c", [P, SUB, D])
        x1, xt, gate = sb("x1_c", [P, SUB, D]), sb("xt_c", [P, DC, T]), sb("gate", [P, SUB, E])
        x1n, xtn, gaten = sb("x1_next", [P, SUB, D]), sb("xt_next", [P, DC, T]), sb("gate_next", [P, SUB, E])
        xn, fn = sb("xn_c", [P, SUB, D]), sb("fn_c", [P, SUB, D])
        st, mv, rstd = sb("st_c", [P, SUB, 6]), sb("mv_c", [P, SUB, 2]), sb("rstd_c", [P, SUB])
        fst, fmv, frstd = sb("fst_c", [P, SUB, 6]), sb("fmv_c", [P, SUB, 2]), sb("frstd_c", [P, SUB])
        lg, gm, gs = sb("lg", [P, SUB, E]), sb("gm", [P, SUB]), sb("gs", [P, SUB])
        more, ties = sb("more", [P, SUB, E, E]), sb("ties", [P, SUB, E, E])
        rank, ex = sb("rank", [P, SUB, E]), sb("ex", [P, SUB, E])
        gt = sb("gt", [E, T])
        hot, tok = sb("hot", [P, SUB, M]), k.tok
        lx = sb("lx", [M, D])
        inv = sb("inv_den", [P, T])
        with nc.Block() as block:
            @block.sync
            def _(sp):
                for i in range(NT):
                    sp.dma_start(inv[i * H:(i + 1) * H, :], scr.o.rearrange("(h r) n -> r h n", h=H)[DH][:, i * T:(i + 1) * T])\
                      .then_inc(wsem["den"], 16)
                sp.dma_start(wout[:], io["L0_attn_Wout"].rearrange("(c h) e n -> (h e) c n", c=DC)).then_inc(wsem["in_"], 16)
                for e in range(E):
                    sp.dma_start(we[:, :, e], io["L0_ffn_expert_w"][e].rearrange("(c p) n -> p c n", p=P)).then_inc(wsem["in_"], 16)
                sp.dma_start(eb[:], io["L0_ffn_expert_b"]).then_inc(wsem["in_"], 16)
                sp.wait_ge(wsem["inv"], 1)
                sp.dma_start(scr.r.rearrange("i h n -> (i h) n"), inv[:]).then_inc(wsem["stored"], 16)
                sp.wait_ge(wsem["stored"], 16)
                sp.wait_ge(wsem["in_"], 16 * (E + 2))

            @block.vector
            def _(dve):
                dve.wait_ge(wsem["den"], 16 * NT)
                dve.reciprocal(inv[:], inv[:]).then_inc(wsem["inv"], 1)
                dve.memset(hot[:], 0.0).then_inc(wsem["zero"], 1)

            @block.tensor
            def _(pe):
                pe.wait_ge(wsem["zero"], 1)
                pe.matmul(ps[0:M, LP, 0:D], hot[:, 0, :], hot[:].rearrange("p s m -> p (s m)"), start=True, stop=True).then_inc(wsem["lrow"], 1)
                pe.wait_ge(wsem["lrow"], 1)

        def half(ap, bank, s):
            return ap[:, bank + s // 2, (s % 2) * D:(s % 2 + 1) * D]

        def step(i, start, experts, finish):
            with nc.Block() as block:
                @block.sync
                def _(sp):
                    if start:
                        ov = scr.o.rearrange("(c h two e) (i n) -> i two c h e n", c=DC, two=2, e=DH, n=T)
                        rv = scr.r.rearrange("i (c h) n -> i c h n", c=DC)
                        for c in range(DC):
                            sp.dma_start(den[:, c], bc(rv[i + 1, c], 1, [H // DC, DH, T])).then_inc(sem["den_in"], 16)
                            sp.dma_start(o[:, c], ov[i + 1, 0, c]).then_inc(sem["o_in"], 16)
                        sp.dma_start(x[:], io["L0_attn_x"].rearrange("o (i s p) d -> (o i) p s d", s=SUB, p=P)[i + 1]).then_inc(sem["x_in"], 16)

                @block.tensor
                def _(pe):
                    def project_out():
                        pe.wait_ge(sem["on"], 1)
                        for s in range(SUB):
                            for c in range(DC):
                                mm = pe.matmul(half(ps, XP, s), o[:, c, s * P:(s + 1) * P], wout[:, c, :], start=(c == 0), stop=(c == DC - 1))
                            mm.then_inc(sem["o_ps"], 1)

                    def gate_logits():
                        pe.wait_ge(sem["tn"], 1)
                        for s in range(SUB):
                            for c in range(DC):
                                mm = pe.matmul(ps[:, XP, s * E:(s + 1) * E], xtn[:, c, s * P:(s + 1) * P], k.gate_w[:, c, :],
                                               start=(c == 0), stop=(c == DC - 1))
                        mm.then_inc(sem["gl_ps"], 1)

                    def gate_rows():
                        pe.wait_ge(sem["gate"], 1)
                        for s in range(SUB):
                            tr = pe.transpose(ps[0:E, XP + 1, s * P:(s + 1) * P], gaten[:, s, :], k.ident[:, :])
                        tr.then_inc(sem["gt_ps"], 1)

                    def gated_biases():
                        pe.wait_ge(sem["gt"], 1)
                        for s in range(SUB):
                            mm = pe.matmul(half(ps, XP, s), gt[:, s * P:(s + 1) * P], eb[:, :], start=True, stop=True)
                        mm.then_inc(sem["bias_ps"], 1)

                    def landmark_rows():
                        pe.wait_ge(sem["hot"], 1)
                        for s in range(SUB):
                            mm = pe.matmul(ps[0:M, LP, 0:D], hot[:, s, :], fn[:, s, :], start=False, stop=True, skip_group_check=True)
                        mm.then_inc(sem["l_ps"], 1)

                    for n in range(UNITS):
                        if experts:
                            s, e = n // (E // 2), 2 * (n % (E // 2))
                            if n % (E // 2) == 0:
                                pe.wait_ge(sem["now"], s + 1)
                            if n >= EBANKS:
                                pe.wait_ge(sem["e_used"], n - EBANKS + 1)
                            for c in range(DC):
                                mm = pe.matmul(ps[:, EP + n % EBANKS, :], xt[:, c, s * P:(s + 1) * P],
                                               we[:, c, e:e + 2, :].rearrange("p e n -> p (e n)"), start=(c == 0), stop=(c == DC - 1))
                            mm.then_inc(sem["e_ps"], 1)
                        if finish and n == FINISH_APPLY + 2:
                            transpose_tile(pe, ps, TP, fn, k.ident, sem["f_xn"], 0, sem["f_ps"])
                            landmark_rows()
                        if start and n == START_SCALE + 1:
                            project_out()
                        if start and n == START_APPLY + 1:
                            if finish:
                                pe.wait_ge(sem["f_out"], 1)
                            transpose_tile(pe, ps, TP, xn, k.ident, sem["xn"], 0, sem["tn_ps"])
                        if start and n == START_APPLY + 2:
                            gate_logits()
                        if start and n == START_PICK + 1:
                            gate_rows()
                        if start and n == START_PICK + 2:
                            gated_biases()

                @block.vector
                def _(dve):
                    ch = Chain(dve, sem["dve"])

                    def gate_ranks():
                        full = [P, SUB, E, E]
                        dve.wait_ge(sem["gl_ps"], 1)
                        ch.link(dve.tensor_tensor(lg[:], ps[:, XP, 0:SUB * E].rearrange("p (s e) -> p s e", s=SUB),
                                                  bc(k.gate_b[:, :], 1, [P, SUB, E]), ALU.add))
                        ch.step(dve.tensor_reduce(gm[:], lg[:], AX, ALU.max))
                        ch.step(dve.tensor_tensor(more[:], bc(lg[:], 2, full), bc(lg[:], 3, full), ALU.is_gt))
                        ch.step(dve.tensor_tensor(ties[:], bc(lg[:], 2, full), bc(lg[:], 3, full), ALU.is_equal))
                        ch.wait()
                        dve.tensor_tensor(lg[:], lg[:], bc(gm[:], 2, [P, SUB, E]), ALU.subtract).then_inc(sem["expd"], 1)
                        ch.link(dve.tensor_tensor(ties[:], ties[:], bc(k.before[:], 1, full), ALU.mult))
                        ch.step(dve.tensor_tensor(more[:], more[:], ties[:], ALU.add))

                    def gate_weights():
                        ch.wait()
                        ch.link(dve.tensor_reduce(rank[:], more[:], AX, ALU.add))
                        dve.wait_ge(sem["expo"], 1)
                        ch.link(dve.scalar_tensor_tensor(out=gaten[:], in0=rank[:], scalar=float(TOP), in1=ex[:], op0=ALU.is_lt, op1=ALU.mult))
                        ch.link(dve.tensor_reduce(gs[:], gaten[:], AX, ALU.add))
                        ch.link(dve.reciprocal(gs[:], gs[:]))
                        dve.tensor_tensor(gaten[:], gaten[:], bc(gs[:], 2, [P, SUB, E]), ALU.mult).then_inc(sem["gate"], 1)

                    if experts:
                        dve.tensor_copy(gate[:], gaten[:]).then_inc(sem["gate_now"], 1)
                    for n in range(UNITS):
                        if experts:
                            s, e = n // (E // 2), 2 * (n % (E // 2))
                            if n == 0:
                                dve.wait_ge(sem["gate_now"], 1)
                            if n == E // 2:
                                dve.wait_ge(sem["x1_now"], 1)
                            dve.wait_ge(sem["e_ps"], n + 1)
                            bank = ps[:, EP + n % EBANKS, :]
                            ch.link(dve.scalar_tensor_tensor(out=x1[:, s, :], in0=bank[:, 0:D], scalar=gate[:, s, e:e + 1],
                                                             in1=(x1n if n == 0 else x1)[:, s, :], op0=ALU.mult, op1=ALU.add))
                            to = k.x2[:, bass.ds(i * SUB + s, 1), :].rearrange("p o d -> p (o d)") if e == E - 2 else x1[:, s, :]
                            dve.scalar_tensor_tensor(out=to, in0=bank[:, D:2 * D], scalar=gate[:, s, e + 1:e + 2],
                                                     in1=x1[:, s, :], op0=ALU.mult, op1=ALU.add).then_inc(sem["e_used"], 1)
                            if not e == E - 2:
                                dve.wait_ge(sem["e_used"], n + 1)
                        if finish and n == FINISH_NORM:
                            for s in range(SUB):
                                ch.step(dve.bn_stats(fst[:, s, :], k.x2[:, bass.ds((i - 1) * SUB + s, 1), :].rearrange("p o d -> p (o d)")))
                            ch.wait()
                            for s in range(SUB):
                                dve.bn_aggr(fmv[:, s, :], fst[:, s, :]).then_inc(sem["f_var"], 1)
                            ch.link(dve.tensor_tensor(hot[:], bc(k.idx[:, :], 1, [P, SUB, M]), bc(tok[:], 2, [P, SUB, M]), ALU.is_equal))
                            dve.tensor_scalar(tok[:], tok[:], float(T), None, ALU.add).then_inc(sem["hot"], 1)
                        if finish and n == FINISH_APPLY:
                            dve.wait_ge(sem["f_rstd"], 1)
                            for s in range(SUB):
                                dve.tensor_scalar(fn[:, s, :], k.x2[:, bass.ds((i - 1) * SUB + s, 1), :].rearrange("p o d -> p (o d)"),
                                                  fmv[:, s, 0:1], frstd[:, s:s + 1], ALU.subtract, ALU.mult).then_inc(sem["f_xn"], 1)
                        if start and n == START_SCALE:
                            dve.wait_ge(sem["den_in"], 32)
                            dve.wait_ge(sem["o_in"], 32)
                            dve.tensor_tensor(o[:], o[:], den[:], ALU.mult).then_inc(sem["on"], 1)
                        if start and n == START_ADD:
                            dve.wait_ge(sem["x_in"], 16)
                            if experts:
                                dve.wait_ge(sem["x1_now"], 1)
                            for s in range(SUB):
                                dve.wait_ge(sem["o_ps"], 2 * (s // 2) + 2)
                                ch.step(dve.tensor_tensor(x1n[:, s, :], x[:, s, :], half(ps, XP, s), ALU.add))
                            ch.wait()
                            ln_stats(dve, ch, x1n, st, mv, sem["var"])
                        if start and n == START_APPLY:
                            ln_apply(dve, x1n, xn, mv, rstd, sem["rstd"], 1, sem["xn"])
                        if start and n == START_GATE:
                            gate_ranks()
                        if start and n == START_PICK:
                            gate_weights()
                        if start and n == START_BIAS:
                            dve.wait_ge(sem["bias_ps"], 1)
                            for s in range(SUB):
                                ch.step(dve.tensor_tensor(x1n[:, s, :], x1n[:, s, :], half(ps, XP, s), ALU.add))

                @block.gpsimd
                def _(pool):
                    ch = Chain(pool, sem["pool"])
                    if experts:
                        pool.tensor_copy(x1[:, 1:], x1n[:, 1:]).then_inc(sem["x1_now"], 1)
                    if finish:
                        ln_rstd(pool, ch, fmv, frstd, k.neghalf, sem["f_var"], SUB, sem["f_rstd"])
                    if start:
                        ln_rstd(pool, ch, mv, rstd, k.neghalf, sem["var"], SUB, sem["rstd"])

                @block.scalar
                def _(act):
                    if experts:
                        for s in range(SUB):
                            act.activation(xt[:, :, s * P:(s + 1) * P], xtn[:, :, s * P:(s + 1) * P], ACT.Copy).then_inc(sem["now"], 1)
                    if finish:
                        act.wait_ge(sem["f_ps"], 1)
                        act.activation(k.xn3t[:, :, bass.ds((i - 1) * T, T)], ps[:, TP:TP + DC, :], ACT.Copy).then_inc(sem["f_out"], 1)
                    if start:
                        act.wait_ge(sem["tn_ps"], 1)
                        if experts:
                            act.wait_ge(sem["now"], SUB)
                        act.activation(xtn[:], ps[:, TP:TP + DC, :], ACT.Copy).then_inc(sem["tn"], 1)
                        act.wait_ge(sem["expd"], 1)
                        act.activation(ex[:], lg[:], ACT.Exp).then_inc(sem["expo"], 1)
                        act.wait_ge(sem["gt_ps"], 1)
                        act.activation(gt[:], ps[0:E, XP + 1, :], ACT.Copy).then_inc(sem["gt"], 1)
            nc.all_engine_barrier(sems_to_clear=cleared(sem))

        step(-1, start=True, experts=False, finish=False)
        step(0, start=True, experts=True, finish=False)
        with nc.Fori(1, NT - 1) as i:
            step(i, start=True, experts=True, finish=True)
        step(NT - 1, start=False, experts=True, finish=True)
        step(NT, start=False, experts=False, finish=True)
        with nc.Block() as block:
            @block.vector
            def _(dve):
                dve.tensor_copy(lx[:], ps[0:M, LP, 0:D]).then_inc(wsem["lt"], 1)
                dve.wait_ge(wsem["lt_ps"], 1)
                dve.tensor_copy(k.lxt[:], ps[:, 0, 0:DC * M].rearrange("p (c m) -> p c m", c=DC)).then_inc(wsem["lt"], 1)

            @block.tensor
            def _(pe):
                pe.wait_ge(wsem["lt"], 1)
                for c in range(DC):
                    tr = pe.transpose(ps[:, 0, c * M:(c + 1) * M], lx[:, c * P:(c + 1) * P], k.ident[0:M, 0:M])
                tr.then_inc(wsem["lt_ps"], 1)



NROW, OROW = 64, 96
LROWS = OROW + 1


def landmark_operands(nc, io, k, ps, la, lk, scr):
    with ExitStack() as ctx:
        sb = lambda n, shape, dt=F32: ctx.enter_context(nc.sbuf_tensor(n, shape, dt))
        sem = stage_sems(ctx, nc, "lm", ["dve", "act", "l_ps", "lk", "sq", "n_ps", "ready", "w_ps", "w", "out"])
        sq, sql = sb("sq_la", [64, G, G * M]), sb("sq_lk", [64, G, M])
        wm = sb("wm", [M, H, M])
        laf = la[:].rearrange("p g j m -> p g (j m)")
        with nc.Block() as block:
            @block.tensor
            def _(pe):
                for c in range(DC):
                    for ic in range(DC):
                        mm = pe.matmul(ps[:, 0, c * M:(c + 1) * M], k.wk1[:, ic, c * P:(c + 1) * P], k.lxt[:, ic, :],
                                       start=(ic == 0), stop=(ic == DC - 1))
                mm.then_inc(sem["l_ps"], 1)
                pe.wait_ge(sem["sq"], 2)
                pe.matmul(ps[NROW:NROW + 32, 1, 0:G * M], k.sel[:, :], sql[:].rearrange("p g m -> p (g m)"), start=True, stop=True,
                          tile_position=(0, NROW)).then_inc(sem["n_ps"], 1)
                for b in range(2):
                    mm = pe.matmul(ps[OROW:OROW + 1, 2 + b, :], k.quarter[:, :], sq[:, 2 * b:2 * b + 2, :].rearrange("p g m -> p (g m)"),
                                   start=True, stop=True, tile_position=(0, OROW))
                mm.then_inc(sem["n_ps"], 1)
                pe.wait_ge(sem["ready"], 1)
                for g in range(G):
                    mm = pe.matmul(ps[0:M, 4 + g // 2, (g % 2) * D:(g % 2 + 1) * D], lk[0:LROWS, g, :], laf[0:LROWS, g],
                                   start=True, stop=True)
                mm.then_inc(sem["w_ps"], 1)

            @block.vector
            def _(dve):
                ch = Chain(dve, sem["dve"])
                ch.step(dve.memset(lk[OROW:LROWS], 1.0))
                for g in range(G):
                    ch.step(dve.tensor_copy(la[NROW:NROW + 32, g], k.blk1[NROW:NROW + 32]))
                dve.wait_ge(sem["l_ps"], 1)
                for g in range(G):
                    r, c = 64 * (g % 2), g // 2
                    ch.step(dve.tensor_scalar(lk[0:64, g, :], ps[r:r + 64, 0, c * M:(c + 1) * M], k.bk1[r:r + 64, c:c + 1], None, ALU.add))
                ch.wait()
                for g in range(G):
                    ch.step(dve.tensor_tensor(la[0:64, g], bc(lk[0:64, g, :], 1, [64, G, M]), k.blk2[:], ALU.mult))
                dve.tensor_tensor(sql[:], lk[0:64], lk[0:64], ALU.mult).then_inc(sem["sq"], 1)
                ch.wait()
                dve.tensor_tensor(sq[:], laf[0:64], laf[0:64], ALU.mult).then_inc(sem["sq"], 1)
                dve.wait_ge(sem["n_ps"], 2)
                ch.step(dve.tensor_copy(lk[NROW:NROW + 32], ps[NROW:NROW + 32, 1, 0:G * M].rearrange("p (g m) -> p g m", g=G)))
                ch.link(dve.tensor_copy(laf[OROW:LROWS].rearrange("p (b g) m -> p b (g m)", b=2), ps[OROW:LROWS, 2:4, :]))
                dve.engine_nop().then_inc(sem["ready"], 1)
                dve.wait_ge(sem["w_ps"], 1)
                dve.tensor_scalar(wm[:].rearrange("p (b h) m -> p b (h m)", b=2), ps[0:M, 4:6, :], 0.0, None, ALU.max).then_inc(sem["w"], 1)
                dve.wait_ge(sem["w"], 2)
                dve.tensor_tensor(wm[:], wm[:], bc(k.regi[:], 1, [M, H, M]), ALU.add).then_inc(sem["w"], 1)

            @block.scalar
            def _(act):
                act.wait_ge(sem["w"], 1)
                act.activation(wm[:], wm[:], ACT.Exp, scale=k.negt[0:M, 0:1]).then_inc(sem["w"], 1)

            @block.sync
            def _(sp):
                sp.wait_ge(sem["w"], 3)
                sp.dma_start(scr.w.rearrange("h a b -> a h b"), wm[:]).then_inc(sem["out"], 16)
                sp.wait_ge(sem["out"], 16)


def rows_of(k, i):
    return k.xn3t[:, :, bass.ds(i * T, T)]


def operand_project(pe, k, ps, w, rows, sem, PB):
    for c in range(DC):
        for ic in range(DC):
            mm = pe.matmul(ps[:, PB + c, :], w[:, ic, c * P:(c + 1) * P], rows[:, ic, :], start=(ic == 0), stop=(ic == DC - 1))
        mm.then_inc(sem["a_ps"], 1)


def operand_norms(pe, k, ps, sq, sem, NB):
    pe.wait_ge(sem["sq"], 1)
    for g in range(G):
        mm = pe.matmul(ps[32 * g:32 * g + 32, NB, :], k.sel[:, :], sq[:, g, :], start=True, stop=True,
                       tile_position=(0, 32 * g), skip_group_check=True)
    mm.then_inc(sem["an_ps"], 1)


def operand_act(act, ps, a, b, sq, sem, PB, NB):
    for g in range(G):
        r, c = 64 * (g % 2), g // 2
        act.wait_ge(sem["a_ps"], c + 1)
        act.activation(a[0:64, g, :], ps[r:r + 64, PB + c, :], ACT.Identity, bias=b[r:r + 64, c:c + 1]).then_inc(sem["a_in"], 1)
    act.wait_ge(sem["a_in"], G)
    act.activation(sq[:], a[0:64], ACT.Square).then_inc(sem["sq"], 1)
    act.wait_ge(sem["an_ps"], 1)
    for g in range(G):
        act.activation(a[NROW:NROW + 32, g, :], ps[32 * g:32 * g + 32, NB, :], ACT.Copy).then_inc(sem["an_in"], 1)


OPERAND = ["a_ps", "a_in", "sq", "an_ps", "an_in"]


KEY_STEPS = (("D0",), ("D1",), ("K0",), ("Z0", "D2"), ("D3",), ("Z1",), ("K1", "Z2"), ("V", "Z3", "N"))


def keys(nc, io, k, ps, scr, winv, zt, acc):
    KP, PV, CP, ZP = 0, 1, 2, 6
    SWEEPS = M // NT
    with ExitStack() as ctx:
        sb = lambda n, shape, dt=F32: ctx.enter_context(nc.sbuf_tensor(n, shape, dt))
        wsem = stage_sems(ctx, nc, "keysw", ["zero", "z_ps", "in_", "dve", "done", "out", "back"])
        sem = loop_sems(k.loop_sems, OPERAND + ["xt_in", "v_ps", "v", "c_ps", "clamp", "phi", "z_ps", "acc", "dve", "spread",
                                                "piv", "swept"])
        a, xt, sq = sb("a_keys", [P, G, T]), sb("xt_keys", [P, DC, T]), sb("sq_keys", [64, G, T])
        v = sb("v_e", [P, SUB, D])
        cl, phi = sb("cl_e", [P, 2, H * M]), sb("phi_e", [P, 2, H * M])
        w = sb("w_inv", [P, 8, M])
        u, spread = sb("u_inv", [P, 8, M]), sb("spread_now", [P, P])
        rd, sc, col = sb("rd_inv", [P, 1]), sb("sc_inv", [P, 8]), sb("col_inv", [P, M])
        own = k.own[:].rearrange("p (c j) -> p c j", j=8)
        with nc.Block() as block:
            @block.vector
            def _(dve):
                dve.memset(acc[:], 0.0).then_inc(wsem["zero"], 1)
                dve.memset(a[OROW:LROWS], 1.0).then_inc(wsem["zero"], 1)

            @block.gpsimd
            def _(pool):
                pool.memset(winv[:], 0.0).then_inc(wsem["zero"], 1)
                pool.wait_ge(wsem["zero"], 3)

            @block.sync
            def _(sp):
                sp.dma_start(w[:], scr.w.rearrange("h (c j) i -> (h c) j i", j=8)).then_inc(wsem["in_"], 16)
                sp.wait_ge(wsem["in_"], 16)

            @block.tensor
            def _(pe):
                pe.wait_ge(wsem["zero"], 3)
                for b in range(2):
                    mm = pe.matmul(ps[:, ZP + b, :], acc[:, 0:P], acc[:, 0:T], start=True, stop=True)
                mm.then_inc(wsem["z_ps"], 1)
                pe.wait_ge(wsem["z_ps"], 1)

        def step(i, start, features):
            with nc.Block() as block:
                @block.sync
                def _(sp):
                    if start:
                        sp.dma_start(xt[:], rows_of(k, i + 1)).then_inc(sem["xt_in"], 16)

                @block.tensor
                def _(pe):
                    def half_keys(c):
                        if c:
                            pe.wait_ge(sem["a_in"], 2)
                        for ic in range(DC):
                            mm = pe.matmul(ps[:, KP, :], k.wk1[:, ic, c * P:(c + 1) * P], rows_of(k, i + 1)[:, ic, :],
                                           start=(ic == 0), stop=(ic == DC - 1))
                        mm.then_inc(sem["a_ps"], 1)

                    def values():
                        pe.wait_ge(sem["xt_in"], 16)
                        if features:
                            pe.wait_ge(sem["clamp"], 3)
                        for s in range(SUB):
                            for ic in range(DC):
                                mm = pe.matmul(ps[:, CP + s // 2, (s % 2) * D:(s % 2 + 1) * D], xt[:, ic, s * P:(s + 1) * P],
                                               k.wv1[:, ic, :], start=(ic == 0), stop=(ic == DC - 1))
                        mm.then_inc(sem["v_ps"], 1)

                    def distances(s):
                        if s >= 2:
                            pe.wait_ge(sem["clamp"], s - 1)
                        for g in range(G):
                            mm = pe.matmul(ps[:, CP + 2 * (s % 2) + g // 2, (g % 2) * D:(g % 2 + 1) * D],
                                           a[0:LROWS, g, s * P:(s + 1) * P], k.la[0:LROWS, g].rearrange("p j m -> p (j m)"),
                                           start=True, stop=True)
                        mm.then_inc(sem["c_ps"], 1)

                    def products(s):
                        pe.wait_ge(sem["phi"], s + 1)
                        for b in range(2):
                            mm = pe.matmul(ps[:, ZP + b, :], v[:, s, b * P:(b + 1) * P], phi[:, s % 2, b * T:(b + 1) * T],
                                           start=False, stop=True, skip_group_check=True)
                        mm.then_inc(sem["z_ps"], 1)

                    for p in range(SWEEPS):
                        if features:
                            if p:
                                pe.wait_ge(sem["swept"], p)
                            else:
                                pe.wait_ge(sem["spread"], 1)
                            pe.matmul(ps[:, PV, 0:M], spread[:, :], w[:, p, :], start=True, stop=True).then_inc(sem["piv"], 1)
                        for piece in KEY_STEPS[p]:
                            if piece[0] == "D" and features:
                                distances(int(piece[1]))
                            if piece[0] == "Z" and features:
                                products(int(piece[1]))
                            if piece[0] == "K" and start:
                                half_keys(int(piece[1]))
                            if piece[0] == "V" and start:
                                values()
                            if piece[0] == "N" and start:
                                operand_norms(pe, k, ps, sq, sem, KP)

                @block.vector
                def _(dve):
                    ch = Chain(dve, sem["dve"])

                    def sweep(p):
                        pivot = i * SWEEPS + p
                        dve.wait_ge(sem["piv"], p + 1)
                        pc = ps[:, PV, 0:M]
                        ch.step(dve.reciprocal(rd[:], ps[:, PV, bass.ds(pivot, 1)]))
                        ch.step(dve.tensor_tensor(sc[:], w[:, :, bass.ds(pivot, 1)].rearrange("p j o -> p (j o)"),
                                                  own[:, bass.ds(pivot, 1), :].rearrange("p o j -> p (o j)"), ALU.subtract))
                        ch.step(dve.tensor_tensor(col[:], pc, k.unit[:, bass.ds(i * -SWEEPS + (M - 1 - p), M)], ALU.subtract))
                        ch.wait()
                        ch.link(dve.tensor_scalar(sc[:], sc[:], rd[:, 0:1], None, ALU.mult))
                        ch.link(dve.tensor_tensor(u[:], bc(sc[:], 2, [P, 8, M]), bc(col[:], 1, [P, 8, M]), ALU.mult))
                        dve.tensor_tensor(w[:], w[:], u[:], ALU.subtract).then_inc(sem["swept"], 1)
                        dve.wait_ge(sem["swept"], p + 1)

                    if features:
                        dve.tensor_copy(spread[:], k.spread[:, bass.ds(i, 1), :].rearrange("p o n -> p (o n)")).then_inc(sem["spread"], 1)
                    for p in range(SWEEPS):
                        if features:
                            sweep(p)
                    if start:
                        dve.wait_ge(sem["v_ps"], 1)
                        if features:
                            dve.wait_ge(sem["z_ps"], SUB)
                        dve.tensor_tensor(v[:], ps[:, CP:CP + 2, :].rearrange("p b (s n) -> p (b s) n", s=2), bc(k.bv1[:, :], 1, [P, SUB, D]),
                                          ALU.add).then_inc(sem["v"], 1)

                @block.scalar
                def _(act):
                    def shift(c):
                        act.wait_ge(sem["a_ps"], c + 1)
                        if features and c == 0:
                            act.wait_ge(sem["c_ps"], SUB)
                        for h in range(2):
                            act.activation(a[0:64, 2 * c + h, :], ps[64 * h:64 * h + 64, KP, :], ACT.Identity,
                                           bias=k.bk1[64 * h:64 * h + 64, c:c + 1]).then_inc(sem["a_in"], 1)

                    for s in range(SUB + 1):
                        if features:
                            if s < SUB:
                                act.wait_ge(sem["c_ps"], s + 1)
                                if s >= 2:
                                    act.wait_ge(sem["phi"], s - 1)
                                act.activation(cl[:, s % 2].rearrange("p (b n) -> p b n", b=2), ps[:, CP + 2 * (s % 2):CP + 2 * (s % 2) + 2, :],
                                               ACT.Relu).then_inc(sem["clamp"], 1)
                            if s == SUB - 1 and start:
                                shift(0)
                            if s > 0:
                                act.wait_ge(sem["clamp"], s)
                                if s > 2:
                                    act.wait_ge(sem["z_ps"], s - 2)
                                    act.wait_ge(sem["acc"], s - 2)
                                act.activation(phi[:, (s - 1) % 2], cl[:, (s - 1) % 2], ACT.Exp, scale=k.negt[:, 0:1]).then_inc(sem["phi"], 1)
                    if start:
                        if not features:
                            shift(0)
                        shift(1)
                        act.wait_ge(sem["a_in"], G)
                        act.activation(sq[:], a[0:64], ACT.Square).then_inc(sem["sq"], 1)
                        act.wait_ge(sem["an_ps"], 1)
                        for g in range(G):
                            act.activation(a[NROW:NROW + 32, g, :], ps[32 * g:32 * g + 32, KP, :], ACT.Copy).then_inc(sem["an_in"], 1)

                @block.gpsimd
                def _(pool):
                    for s in range(SUB):
                        if features:
                            pool.wait_ge(sem["phi"], s + 1)
                            pool.tensor_tensor(acc[:], acc[:], phi[:, s % 2], ALU.add).then_inc(sem["acc"], 1)
                            pool.wait_ge(sem["acc"], s + 1)
            nc.all_engine_barrier(sems_to_clear=cleared(sem))

        step(-1, start=True, features=False)
        with nc.Fori(0, NT - 1) as i:
            step(i, start=True, features=True)
        step(NT - 1, start=False, features=True)
        with nc.Block() as block:
            @block.vector
            def _(dve):
                dve.scalar_tensor_tensor(out=w[:], in0=own.rearrange("p i j -> p j i"), scalar=2.0, in1=w[:],
                                         op0=ALU.mult, op1=ALU.subtract).then_inc(wsem["done"], 1)

            @block.sync
            def _(sp):
                sp.wait_ge(wsem["done"], 1)
                sp.dma_start(scr.wi.rearrange("h (c j) i -> (h c) j i", j=8), w[:]).then_inc(wsem["out"], 16)
                sp.wait_ge(wsem["out"], 16)
                wv = scr.wi.rearrange("(r two) a b -> two a r b", two=2)
                for two in range(2):
                    sp.dma_start(winv[64 * two:64 * two + 64, :, 64 * two:64 * two + 64], wv[two]).then_inc(wsem["back"], 16)
                sp.wait_ge(wsem["back"], 32)


def solve(nc, io, k, ps, winv, zt, acc):
    with ExitStack() as ctx:
        sb = lambda n, shape, dt=F32: ctx.enter_context(nc.sbuf_tensor(n, shape, dt))
        sem = stage_sems(ctx, nc, "solve", ["zt", "s_ps", "z_ps", "z", "y_ps", "y"])
        z = sb("z_s", [P, PAIRS, 2 * DH + 2])
        with nc.Block() as block:
            @block.vector
            def _(dve):
                dve.tensor_tensor(zt[:].rearrange("p c (h m) -> p c h m", m=M), ps[:, 6:8, :].rearrange("p c (h m) -> p c h m", m=M),
                                  bc(k.headmask[:], 1, [P, DC, 8, M]), ALU.mult).then_inc(sem["zt"], 1)
                dve.wait_ge(sem["z_ps"], 1)
                for r in range(PAIRS):
                    o = 2 * DH * (r % 4)
                    dve.tensor_copy(z[:, r, 0:2 * DH], ps[:, r // 4, (r % 4) * P + o:(r % 4) * P + o + 2 * DH]).then_inc(sem["z"], 1)
                dve.wait_ge(sem["s_ps"], 1)
                dve.tensor_tensor(z[:, :, 2 * DH:], bc(ps[:, 2, 0:PAIRS], 2, [P, PAIRS, 2]), bc(k.half[:, :], 1, [P, PAIRS, 2]),
                                  ALU.mult).then_inc(sem["z"], 1)
                dve.wait_ge(sem["y_ps"], 1)
                yv = ps[:, 3, 0:PAIRS * 64].rearrange("p (r n) -> p r n", n=64)
                dve.tensor_copy(k.y[:, :, 0, :], yv[:, :, 0:2 * DH]).then_inc(sem["y"], 1)
                for a in range(2):
                    dve.tensor_copy(k.y[:, :, 1, a * DH:(a + 1) * DH], yv[:, :, 2 * DH + a:2 * DH + a + 1].broadcast_to([P, PAIRS, DH]))\
                       .then_inc(sem["y"], 1)

            @block.tensor
            def _(pe):
                for r in range(PAIRS):
                    mm = pe.matmul(ps[:, 2, r:r + 1], acc[:, r * P:(r + 1) * P], k.ones[:, :], start=True, stop=True)
                mm.then_inc(sem["s_ps"], 1)
                pe.wait_ge(sem["zt"], 1)
                for r in range(PAIRS):
                    tr = pe.transpose(ps[:, r // 4, (r % 4) * P:(r % 4 + 1) * P], zt[:, r // 4, (r % 4) * P:(r % 4 + 1) * P], k.ident[:, :])
                tr.then_inc(sem["z_ps"], 1)
                pe.wait_ge(sem["z"], PAIRS + 1)
                for r in range(PAIRS):
                    mm = pe.matmul(ps[:, 3, r * 64:r * 64 + 2 * DH + 2], winv[:, r, :], z[:, r, :], start=True, stop=True)
                mm.then_inc(sem["y_ps"], 1)


def landmarks(nc, io, k, ps, scr):
    with ExitStack() as ctx:
        sb = lambda n, shape, dt=F32: ctx.enter_context(nc.sbuf_tensor(n, shape, dt))
        winv = sb("winv", [P, PAIRS, P])
        zt, acc = sb("zt", [P, DC, T]), sb("acc", [P, H * M])
        with ExitStack() as inner:
            lk = inner.enter_context(nc.sbuf_tensor("lk", [P, G, M], F32))
            landmark_operands(nc, io, k, ps, k.la, lk, scr)
        keys(nc, io, k, ps, scr, winv, zt, acc)
        solve(nc, io, k, ps, winv, zt, acc)



OUT_PROJECT, WEIGH, START_QUERIES, OUT_NORM = 3, 3, 5, 5


def queries(nc, io, k, ps, out):
    BP, QP, CP, YP = 0, 2, 4, 6
    with ExitStack() as ctx:
        sb = lambda n, shape, dt=F32: ctx.enter_context(nc.sbuf_tensor(n, shape, dt))
        wsem = stage_sems(ctx, nc, "qryw", ["one"])
        sem = loop_sems(k.loop_sems, OPERAND + ["c_ps", "clamp", "phi", "n_ps", "on", "dve", "pool", "xb", "o_ps", "var",
                                             "rstd", "xn", "xt_ps", "xt", "f_ps", "res", "out"])
        a, sq = sb("a_q", [P, G, T]), sb("sq_q", [64, G, T])
        cl, phi = sb("cl_q", [P, 2, T]), sb("phi_q", [P, PAIRS, T])
        nr, ot = sb("nr_q", [P, DC, T]), sb("ot_q", [P, DC, T])
        xb, x3, xn, x4 = (sb(f"{n}_q", [P, SUB, D]) for n in ("xb", "x3", "xn", "x4"))
        st, mv, rstd = sb("st_q", [P, SUB, 6]), sb("mv_q", [P, SUB, 2]), sb("rstd_q", [P, SUB])
        xt4 = sb("xt4_q", [P, DC, T])
        with nc.Block() as block:
            @block.vector
            def _(dve):
                dve.memset(a[OROW:LROWS], 1.0).then_inc(wsem["one"], 1)
                dve.wait_ge(wsem["one"], 1)

        def half(bank, s):
            return ps[:, bank + s // 2, (s % 2) * D:(s % 2 + 1) * D]

        def step(i, start, features, output):
            with nc.Block() as block:
                @block.sync
                def _(sp):
                    if output:
                        sp.wait_ge(sem["res"], SUB)
                        sp.dma_start(out.rearrange("o (i s p) d -> (o i) p s d", s=SUB, p=P)[i - 1], x4[:]).then_inc(sem["out"], 16)
                        sp.wait_ge(sem["out"], 16)

                @block.tensor
                def _(pe):
                    def project_out():
                        for s in range(SUB):
                            for c in range(DC):
                                mm = pe.matmul(half(BP, s), ot[:, c, s * P:(s + 1) * P], k.wo1[:, c, :], start=(c == 0), stop=(c == DC - 1))
                            mm.then_inc(sem["o_ps"], 1)

                    def linear():
                        pe.wait_ge(sem["xt"], 1)
                        for s in range(SUB):
                            for c in range(DC):
                                mm = pe.matmul(half(BP, s), xt4[:, c, s * P:(s + 1) * P], k.wf[:, c, :], start=(c == 0), stop=(c == DC - 1))
                            mm.then_inc(sem["f_ps"], 1)

                    def weigh(c):
                        pe.wait_ge(sem["phi"], 4 * c + 4)
                        if c:
                            pe.wait_ge(sem["clamp"], PAIRS)
                        for w in range(2):
                            for r in range(4 * c, 4 * c + 4):
                                mm = pe.matmul(ps[32 * (r % 4):32 * (r % 4) + 32, (YP, CP)[c] + w, :], k.y[:, r, w, :], phi[:, r, :],
                                               start=True, stop=True, tile_position=(0, 32 * (r % 4)), skip_group_check=True)
                        mm.then_inc(sem["n_ps"], 1)

                    for r in range(PAIRS):
                        if features:
                            if r >= 2:
                                pe.wait_ge(sem["clamp"], r - 1)
                            pe.matmul(ps[:, CP + r % 2, :], k.la[0:LROWS, r // 2, 2 * (r % 2):2 * (r % 2) + 2].rearrange("p j m -> p (j m)"),
                                      a[0:LROWS, r // 2, :], start=True, stop=True).then_inc(sem["c_ps"], 1)
                        if output and r == OUT_PROJECT:
                            project_out()
                        if features and r == WEIGH:
                            weigh(0)
                        if start and r == START_QUERIES:
                            operand_project(pe, k, ps, k.wq1, rows_of(k, i + 1), sem, QP)
                    if output:
                        transpose_tile(pe, ps, BP, xn, k.ident, sem["xn"], 0, sem["xt_ps"])
                    if features:
                        weigh(1)
                    if output:
                        linear()
                    if start:
                        operand_norms(pe, k, ps, sq, sem, QP)

                @block.vector
                def _(dve):
                    ch = Chain(dve, sem["dve"])

                    def normalise(c):
                        dve.wait_ge(sem["n_ps"], c + 1)
                        ch.link(dve.tensor_scalar(nr[:, c], ps[:, (YP, CP)[c] + 1, :], NORM_MIN, None, ALU.max))
                        ch.link(dve.reciprocal(nr[:, c], nr[:, c]))
                        if output and c == 0:
                            dve.wait_ge(sem["o_ps"], SUB)
                        dve.tensor_tensor(ot[:, c], ps[:, (YP, CP)[c], :], nr[:, c], ALU.mult).then_inc(sem["on"], 1)

                    for r in range(PAIRS):
                        if features:
                            dve.wait_ge(sem["c_ps"], r + 1)
                            if r >= 2:
                                dve.wait_ge(sem["phi"], r - 1)
                            dve.tensor_scalar(cl[:, r % 2], ps[:, CP + r % 2, :], 0.0, None, ALU.max).then_inc(sem["clamp"], 1)
                        if output and r == OUT_PROJECT:
                            dve.wait_ge(sem["xb"], 1)
                            for s in range(SUB):
                                dve.wait_ge(sem["o_ps"], 2 * (s // 2) + 2)
                                ch.step(dve.tensor_tensor(x3[:, s, :], xb[:, s, :], half(BP, s), ALU.add))
                            ch.wait()
                            ln_stats(dve, ch, x3, st, mv, sem["var"])
                        if features and r == WEIGH:
                            normalise(0)
                        if output and r == OUT_NORM:
                            ln_apply(dve, x3, xn, mv, rstd, sem["rstd"], 1, sem["xn"])
                    if features:
                        normalise(1)
                    if output:
                        for s in range(SUB):
                            dve.wait_ge(sem["f_ps"], 2 * (s // 2) + 2)
                            dve.tensor_tensor(x4[:, s, :], x3[:, s, :], half(BP, s), ALU.add).then_inc(sem["res"], 1)

                @block.gpsimd
                def _(pool):
                    ch = Chain(pool, sem["pool"])
                    if output:
                        pool.tensor_tensor(xb[:], k.x2[:, bass.ds((i - 1) * SUB, SUB), :], bc(k.bo1[:, :], 1, [P, SUB, D]), ALU.add)\
                            .then_inc(sem["xb"], 1)
                        ln_rstd(pool, ch, mv, rstd, k.neghalf, sem["var"], SUB, sem["rstd"])

                @block.scalar
                def _(act):
                    for r in range(PAIRS):
                        if features:
                            act.wait_ge(sem["clamp"], r + 1)
                            act.activation(phi[:, r], cl[:, r % 2], ACT.Exp, scale=k.negt[:, 0:1]).then_inc(sem["phi"], 1)
                    if output:
                        act.wait_ge(sem["xt_ps"], 1)
                        act.activation(xt4[:], ps[:, BP:BP + 2, :], ACT.Copy).then_inc(sem["xt"], 1)
                    if start:
                        if features:
                            act.wait_ge(sem["c_ps"], PAIRS)
                        operand_act(act, ps, a, k.bq1, sq, sem, QP, QP)
            nc.all_engine_barrier(sems_to_clear=cleared(sem))

        step(-1, start=True, features=False, output=False)
        step(0, start=True, features=True, output=False)
        with nc.Fori(1, NT - 1) as i:
            step(i, start=True, features=True, output=True)
        step(NT - 1, start=False, features=True, output=True)
        step(NT, start=False, features=False, output=True)



class Names:
    pass


def build(nc, io, out, stages=("project", "attend", "mix", "landmarks", "queries")):
    scr = Names()
    scr.q = nc.dram_tensor("q_parts", (3, D, N), BF16, kind="Internal").ap()
    scr.k = nc.dram_tensor("k_parts", (3, D, N), BF16, kind="Internal").ap()
    scr.v = nc.dram_tensor("v_ones", (N, H * 2 * DH), F32, kind="Internal").ap()
    scr.o = nc.dram_tensor("attn_sums", (H * 2 * DH, N), F32, kind="Internal").ap()
    scr.r = nc.dram_tensor("weight_sums_inverse", (NT, H, T), F32, kind="Internal").ap()
    scr.w = nc.dram_tensor("kernel_matrix", (H, M, M), F32, kind="Internal").ap()
    scr.wi = nc.dram_tensor("kernel_inverse", (H, M, M), F32, kind="Internal").ap()
    with ExitStack() as ctx:
        sb = lambda n, shape, dt=F32: ctx.enter_context(nc.sbuf_tensor(n, shape, dt))
        ps = ctx.enter_context(nc.psum_tensor("ps", [P, 8, T], F32))
        k = Names()
        k.loop_sems = [ctx.enter_context(nc.semaphore(f"loop_{i}")) for i in range(LOOP_SEMS)]
        assert [s.num for s in k.loop_sems] == list(range(k.loop_sems[0].num, k.loop_sems[0].num + LOOP_SEMS))
        k.wq1, k.wk1, k.wv1, k.wo1, k.wf = (sb(n, [P, DC, D]) for n in ("wq1", "wk1", "wv1", "wo1", "wf"))
        k.gate_w = sb("gate_wt", [P, DC, E])
        k.gate_b = sb("gate_bias", [P, E])
        k.bq1, k.bk1 = sb("bq1", [P, DC]), sb("bk1", [P, DC])
        k.bv1, k.bo1 = sb("bv1", [P, D]), sb("bo1", [P, D])
        k.negt = sb("negt", [P, 1])
        k.ident, k.identb = sb("ident", [P, P]), sb("identb", [P, P], BF16)
        k.mask_kq, k.mask_qk = sb("mask_kq", [P, P], BF16), sb("mask_qk", [P, P], BF16)
        k.neghalf, k.ones = sb("neghalf", [P, SUB]), sb("ones", [P, 1])
        k.quarter = sb("quarter", [64, 1])
        k.half = sb("half", [P, 2])
        k.sel = sb("sel", [64, 32])
        k.blk2 = sb("blk2", [64, G, M])
        k.blk1 = sb("blk1", [P, G, M])
        k.headmask = sb("headmask", [P, 8, M])
        k.regi = sb("regi", [M, M])
        k.before = sb("before", [P, E, E])
        k.spread = sb("spread", [P, 8, P])
        k.unit = sb("unit", [P, 2 * M - 1])
        k.own = sb("own", [P, 8 * 8 * 8])
        k.idx, k.tok = sb("idx_f", [P, M]), sb("tok", [P, SUB])
        setup(nc, io, k, ps)
        if "project" in stages:
            project(nc, io, k, ps, scr)
        if "attend" in stages:
            attend(nc, io, k, ps, scr)
        if "mix" in stages:
            k.x2, k.xn3t = sb("x2", [P, N // P, D]), sb("xn3t", [P, DC, N])
            k.lxt = sb("lxt", [P, DC, M])
            mix(nc, io, k, ps, scr)
        if "landmarks" in stages:
            k.la, k.y = sb("la", [P, G, G, M]), sb("y", [P, PAIRS, 2, 32])
            landmarks(nc, io, k, ps, scr)
        if "queries" in stages:
            queries(nc, io, k, ps, out)
    return scr


_INS = ["L0_attn_x", "L0_attn_Wq", "L0_attn_Wk", "L0_attn_Wv", "L0_attn_Wout", "L0_ffn_gate_w", "L0_ffn_gate_b",
        "L0_ffn_expert_w", "L0_ffn_expert_b", "L1_attn_Wq", "L1_attn_bq", "L1_attn_Wk", "L1_attn_bk", "L1_attn_Wv",
        "L1_attn_bv", "L1_attn_Wo", "L1_attn_bo", "L1_attn_temperature", "L1_attn_landmark_idx", "L1_ffn_weight"]


def kernel(**inputs):
    import numpy as _np
    import concourse.bacc as _bacc
    from concourse import mybir as _mybir
    from concourse.bass_utils import run_bass_kernel_spmd as _run

    nc = _bacc.Bacc("TRN2", target_bir_lowering=False, num_devices=1)
    arrays, io = {}, {}
    for name in _INS:
        a = _np.ascontiguousarray(inputs[name])
        if a.ndim == 0:
            a = a.reshape(1)
        arrays[f"in_{name}"] = a
        io[name] = nc.dram_tensor(f"in_{name}", a.shape, _mybir.dt.from_np(a.dtype), kind="ExternalInput").ap()
    out = nc.dram_tensor("out_x", (1, N, D), F32, kind="ExternalOutput").ap()
    build(nc, io, out)
    r = _run(nc, [arrays], core_ids=[0])
    return r.results[0]["out_x"]
```

```python
from contextlib import ExitStack

import concourse.bass as bass
from concourse import mybir

F32 = mybir.dt.float32
BF16 = mybir.dt.bfloat16
I32 = mybir.dt.int32
ALU = mybir.AluOpType
ACT = mybir.ActivationFunctionType
AX = mybir.AxisListType.X

P = 128
N = 4096
D = 256
DC = D // P
H = 16
DH = D // H
T = 512
NT = N // T
SUB = T // P
G = 4
NG = H // G
E = 8
TOP = 2
M = 64
PAIRS = H // 2
LN_EPS = 1e-5
REG = 1e-6
NORM_MIN = 1e-10
BIG = 3.0e38
MASKED = -3.0e38


def stage_sems(ctx, nc, stage, names):
    return {n: ctx.enter_context(nc.semaphore(f"{stage}_{n}")) for n in names}


def loop_sems(pool, names):
    assert len(names) <= len(pool)
    return dict(zip(names, pool))


def cleared(sems):
    nums = [s.num for s in sems.values()]
    return range(min(nums), max(nums) + 1)


LOOP_SEMS = 54


class Chain:

    def __init__(self, eng, sem):
        self.eng, self.sem, self.n = eng, sem, 0

    def step(self, ins):
        ins.then_inc(self.sem, 1)
        self.n += 1

    def wait(self):
        self.eng.wait_ge(self.sem, self.n)

    def link(self, ins):
        self.step(ins)
        self.wait()


def bc(ap, axis, shape):
    return ap.unsqueeze(axis).broadcast_to(shape)



def ln_stats(dve, ch, x, st, mv, s_var):
    for s in range(SUB):
        ch.step(dve.bn_stats(st[:, s, :], x[:, s, :]))
    ch.wait()
    for s in range(SUB):
        dve.bn_aggr(mv[:, s, :], st[:, s, :]).then_inc(s_var, 1)


def ln_rstd(pool, ch, mv, rstd, neghalf, s_var, n_var, s_rstd):
    pool.wait_ge(s_var, n_var)
    ch.link(pool.tensor_scalar(rstd[:, :], mv[:, :, 1], LN_EPS, None, ALU.add))
    pool.tensor_tensor(rstd[:, :], rstd[:, :], neghalf[:, 0:SUB], ALU.pow).then_inc(s_rstd, 1)


def ln_apply(dve, x, xn, mv, rstd, s_rstd, n_rstd, s_xn):
    dve.wait_ge(s_rstd, n_rstd)
    for s in range(SUB):
        dve.tensor_scalar(xn[:, s, :], x[:, s, :], mv[:, s, 0:1], rstd[:, s:s + 1],
                          ALU.subtract, ALU.mult).then_inc(s_xn, 1)


def ln_offset(pool, ch, mv, rstd, off, s_rstd, n_rstd, s_off):
    pool.wait_ge(s_rstd, n_rstd)
    ch.link(pool.tensor_tensor(off[:, :], mv[:, :, 0], rstd[:, :], ALU.mult))
    pool.tensor_scalar(off[:, :], off[:, :], -1.0, None, ALU.mult).then_inc(s_off, 1)


def ln_affine(act, part, xn, rstd, off, s_off, n_off, s_xn):
    act.wait_ge(s_off, n_off)
    for s in range(SUB):
        act.activation(xn[:, s, :], part(s), ACT.Identity, bias=off[:, s:s + 1], scale=rstd[:, s:s + 1]).then_inc(s_xn, 1)


def transpose_tile(pe, ps, bank, xn, ident, s_xn, n_xn, s_ps):
    for s in range(SUB):
        pe.wait_ge(s_xn, n_xn + s + 1)
        for c in range(DC):
            last = pe.transpose(ps[:, bank + c, s * P:(s + 1) * P], xn[:, s, c * P:(c + 1) * P], ident[:, :])
    last.then_inc(s_ps, 1)



def setup(nc, io, k, ps):
    names = ["w_in", "sgn_in", "gate_in", "small_in", "pool", "dve", "id_ok", "tr_ps", "tr_sb", "sgn"]
    with ExitStack() as ctx:
        sem = stage_sems(ctx, nc, "setup", names)
        raw = ctx.enter_context(nc.sbuf_tensor("raw", [P, 5, DC, D], F32))
        sgn = ctx.enter_context(nc.sbuf_tensor("sgn", [P, DC, D], F32))
        neg = ctx.enter_context(nc.sbuf_tensor("neg", [P, DC, D], F32))
        graw = ctx.enter_context(nc.sbuf_tensor("graw", [E, D], F32))
        zeros = ctx.enter_context(nc.sbuf_tensor("zeros", [P, 8, P], F32))
        idx = ctx.enter_context(nc.sbuf_tensor("idx", [P, M], I32))
        under = ctx.enter_context(nc.sbuf_tensor("under", [P, M], F32))
        m8 = ctx.enter_context(nc.sbuf_tensor("m8", [P, 8], F32))
        i8 = ctx.enter_context(nc.sbuf_tensor("i8", [P, 8, 8], F32))
        weights = [("L1_attn_Wq", k.wq1), ("L1_attn_Wk", k.wk1), ("L1_attn_Wv", k.wv1), ("L1_attn_Wo", k.wo1),
                   ("L1_ffn_weight", k.wf)]
        with nc.Block() as block:
            @block.sync
            def _(sp):
                for i, (name, _) in enumerate(weights):
                    sp.dma_start(raw[:, i], io[name].rearrange("(c p) n -> p c n", p=P)).then_inc(sem["w_in"], 16)
                sp.dma_start(graw[:, :], io["L0_ffn_gate_w"]).then_inc(sem["gate_in"], 16)
                for tile, ap in ((k.bq1, io["L1_attn_bq"]), (k.bk1, io["L1_attn_bk"])):
                    sp.dma_start(tile[:, :], ap.rearrange("(c p) -> p c", p=P),
                                 allow_slow_non_contiguous=True).then_inc(sem["small_in"], 16)
                for tile, ap in ((k.bv1, io["L1_attn_bv"]), (k.bo1, io["L1_attn_bo"]), (k.gate_b, io["L0_ffn_gate_b"]),
                                 (idx, io["L1_attn_landmark_idx"]), (k.negt, io["L1_attn_temperature"])):
                    sp.dma_start(tile[:, :], ap.partition_broadcast(P)).then_inc(sem["small_in"], 16)

            @block.gpsimd
            def _(pool):
                ch = Chain(pool, sem["pool"])
                for tile, v in ((zeros, 0.0), (k.neghalf, -0.5), (k.ones, 1.0), (k.blk2, -2.0), (k.headmask, 1.0),
                                (k.sel, 1.0), (k.quarter, 0.25), (k.half, 0.0)):
                    ch.link(pool.memset(tile[:], v))
                ch.link(pool.memset(k.blk1[:], 0.0))
                ch.wait()
                ch.link(pool.memset(k.half[0:64, 0:1], 1.0))
                ch.link(pool.memset(k.half[64:128, 1:2], 1.0))
                z = zeros[:, 0, :]
                pool.affine_select(out=k.ident[:, :], in_=z, pattern=[[-1, P]], compare_op=ALU.not_equal, fill=1.0,
                                   base=0, channel_multiplier=1).then_inc(sem["id_ok"], 1)
                pool.wait_ge(sem["id_ok"], 1)
                ch.link(pool.affine_select(out=k.identb[:, :], in_=z, pattern=[[-1, P]], compare_op=ALU.not_equal,
                                           fill=1.0, base=0, channel_multiplier=1))
                ch.link(pool.affine_select(out=k.mask_kq[:, :], in_=z, pattern=[[1, P]], compare_op=ALU.is_ge,
                                           fill=MASKED, base=0, channel_multiplier=-1))
                ch.link(pool.affine_select(out=k.mask_qk[:, :], in_=z, pattern=[[-1, P]], compare_op=ALU.is_ge,
                                           fill=MASKED, base=0, channel_multiplier=1))
                for tile, pat, rows in ((k.sel, [[-DH, 32]], 64), (k.blk2, [[-DH, G], [0, M]], 64),
                                        (k.headmask, [[-DH, 8], [0, M]], P)):
                    ch.link(pool.affine_select(out=tile[:], in_=tile[:], pattern=pat, compare_op=ALU.is_ge,
                                               fill=0.0, base=0, channel_multiplier=1))
                    ch.link(pool.affine_select(out=tile[:], in_=tile[:], pattern=[[-s, n] for s, n in pat],
                                               compare_op=ALU.is_ge, fill=0.0, base=DH - 1, channel_multiplier=-1))
                ch.link(pool.affine_select(out=k.blk1[64:96], in_=k.blk1[64:96], pattern=[[-1, G], [0, M]],
                                           compare_op=ALU.not_equal, fill=1.0, base=0, channel_multiplier=1))
                ch.link(pool.affine_select(out=k.regi[:, :], in_=z[0:M, 0:M], pattern=[[-1, M]],
                                           compare_op=ALU.not_equal, fill=REG, base=0, channel_multiplier=1))
                ch.link(pool.affine_select(out=k.before[:, :, :], in_=zeros[:, 0, 0:64].rearrange("p (a b) -> p a b", a=8),
                                           pattern=[[-1, E], [1, E]], compare_op=ALU.is_ge, fill=1.0, base=0,
                                           channel_multiplier=0))
                ch.link(pool.affine_select(out=k.spread[:, :, :], in_=zeros[:, :, :].rearrange("p c (h r) -> p c h r", r=8),
                                           pattern=[[-1, 8], [-8, H], [0, 8]], compare_op=ALU.not_equal, fill=1.0,
                                           base=0, channel_multiplier=1))
                ch.link(pool.affine_select(out=i8[:, :, :], in_=zeros[:, 0, 0:64].rearrange("p (a b) -> p a b", a=8),
                                           pattern=[[-1, 8], [1, 8]], compare_op=ALU.not_equal, fill=1.0, base=0,
                                           channel_multiplier=0))
                ch.link(pool.affine_select(out=k.unit[:, :], in_=zeros[:, 0, 0:2 * M - 1], pattern=[[1, 2 * M - 1]],
                                           compare_op=ALU.not_equal, fill=1.0, base=1 - M, channel_multiplier=0))
                ch.link(pool.iota(k.tok[:, :], pattern=[[P, SUB]], base=0, channel_multiplier=1,
                                  allow_small_or_imprecise_dtypes=True))
                ch.wait()
                pool.engine_nop().then_inc(sem["id_ok"], 1)

            @block.tensor
            def _(pe):
                pe.wait_ge(sem["id_ok"], 1)
                pe.wait_ge(sem["w_in"], 80)
                for i in range(5):
                    src = sgn if i == 4 else raw[:, i]
                    if i == 4:
                        pe.wait_ge(sem["sgn"], 1)
                    if i >= 2:
                        pe.wait_ge(sem["tr_sb"], i - 1)
                    for oc in range(DC):
                        for ic in range(DC):
                            last = pe.transpose(ps[:, 2 * (i % 2) + ic, oc * P:(oc + 1) * P],
                                                src[:, oc, ic * P:(ic + 1) * P], k.ident[:, :])
                    last.then_inc(sem["tr_ps"], 1)
                pe.wait_ge(sem["gate_in"], 16)
                for ic in range(DC):
                    last = pe.transpose(ps[:, 4, ic * E:(ic + 1) * E], graw[:, ic * P:(ic + 1) * P],
                                        k.ident[0:E, 0:E])
                last.then_inc(sem["tr_ps"], 1)

            @block.vector
            def _(dve):
                ch = Chain(dve, sem["dve"])
                dve.wait_ge(sem["w_in"], 80)
                ch.step(dve.tensor_scalar(sgn[:], raw[:, 4], 0.0, None, ALU.is_gt))
                ch.step(dve.tensor_scalar(neg[:], raw[:, 4], 0.0, None, ALU.is_lt))
                ch.wait()
                dve.tensor_tensor(sgn[:], sgn[:], neg[:], ALU.subtract).then_inc(sem["sgn"], 1)
                for i, (_, dst) in enumerate(weights):
                    dve.wait_ge(sem["tr_ps"], i + 1)
                    b = 2 * (i % 2)
                    dve.tensor_copy(dst[:, :, :], ps[:, b:b + DC, 0:D]).then_inc(sem["tr_sb"], 1)
                dve.wait_ge(sem["tr_ps"], 6)
                ch.step(dve.tensor_copy(k.gate_w[:, :, :], ps[:, 4, 0:DC * E].rearrange("p (c e) -> p c e", c=DC)))
                dve.wait_ge(sem["small_in"], 16 * 7)
                ch.link(dve.tensor_copy(k.idx[:, :], idx[:, :]))
                ch.link(dve.tensor_scalar(under[:, :], k.idx[:, :], 0.0, float(N), ALU.is_lt, ALU.mult))
                ch.link(dve.tensor_tensor(k.idx[:, :], k.idx[:, :], under[:, :], ALU.add))
                ch.step(dve.tensor_scalar(k.idx[:, :], k.idx[:, :], 0.0, float(N - 1), ALU.max, ALU.min))
                ch.link(dve.reciprocal(k.negt[:, :], k.negt[:, :]))
                ch.step(dve.tensor_scalar(k.bounds[:, 0:1], k.negt[:, :], 0.0, BIG, ALU.is_lt, ALU.mult))
                ch.step(dve.tensor_scalar(k.bounds[:, 1:2], k.negt[:, :], 0.0, None, ALU.is_lt))
                ch.link(dve.tensor_scalar(k.negt[:, :], k.negt[:, :], -1.0, None, ALU.mult))
                ch.step(dve.tensor_scalar(k.bounds[:, 0:1], k.bounds[:, 0:1], 1.0, None, ALU.max))
                dve.wait_ge(sem["id_ok"], 2)
                ch.link(dve.tensor_reduce(m8[:, :], k.spread[:, :, :], AX, ALU.max))
                ch.step(dve.tensor_tensor(k.own[:, :].rearrange("p (a b c) -> p a b c", a=8, b=8),
                                          bc(bc(m8[:, :], 2, [P, 8, 8]), 3, [P, 8, 8, 8]),
                                          bc(i8[:, :, :], 1, [P, 8, 8, 8]), ALU.mult))



def project(nc, io, k, ps, scr):
    XP, QP, VP = 0, 2, 6
    names = ["x_in", "dve", "pool", "var", "rstd", "xn", "xt_ps", "xt", "qk_ps", "v_ps", "p1", "rest", "p2", "p3", "v",
             "q_out", "k_out", "v_out"]
    with ExitStack() as ctx:
        sb = lambda n, shape, dt=F32: ctx.enter_context(nc.sbuf_tensor(n, shape, dt))
        wsem = stage_sems(ctx, nc, "projw", ["in_", "ones"])
        sem = loop_sems(k.loop_sems, names)
        w = sb("w_qkv", [P, 3, DC, D])
        x = sb("x_a", [P, SUB, D])
        xn = sb("xn_a", [P, SUB, D])
        st = sb("st_a", [P, SUB, 6])
        mv = sb("mv_a", [P, SUB, 2])
        rstd = sb("rstd_a", [P, SUB])
        xt = sb("xt_a", [P, DC, T])
        part = sb("part", [P, 2, 3, DC, T], BF16)
        rest = sb("rest", [P, 4, T])
        v = sb("v_a", [P, SUB, H, 2 * DH])
        scale = (DH ** -0.5, 1.0)
        with nc.Block() as block:
            @block.sync
            def _(sp):
                for i, name in enumerate(("L0_attn_Wq", "L0_attn_Wk", "L0_attn_Wv")):
                    sp.dma_start(w[:, i], io[name].rearrange("(c p) h e -> p c (h e)", p=P)).then_inc(wsem["in_"], 16)
                sp.wait_ge(wsem["in_"], 48)

            @block.gpsimd
            def _(pool):
                pool.memset(v[:, :, :, DH:2 * DH], 1.0).then_inc(wsem["ones"], 1)
                pool.wait_ge(wsem["ones"], 1)

        def step(i, start, products, store):
            with nc.Block() as block:
                @block.sync
                def _(sp):
                    def store_parts(a, dst, done):
                        for n in range(3):
                            sp.dma_start(dst.rearrange("a (c p) (i n) -> i a p c n", c=DC, n=T)[i - 1, n], part[:, a, n]).then_inc(done, 16)

                    if store:
                        store_parts(0, scr.q, sem["q_out"])
                    if start:
                        sp.dma_start(x[:], io["L0_attn_x"].rearrange("o (i s p) d -> (o i) p s d", s=SUB, p=P)[i + 1]).then_inc(sem["x_in"], 16)
                    if store:
                        store_parts(1, scr.k, sem["k_out"])
                        sp.dma_start(scr.v.rearrange("(i s p) n -> i p s n", s=SUB, p=P)[i - 1],
                                     v[:].rearrange("p s h e -> p s (h e)")).then_inc(sem["v_out"], 16)
                        sp.wait_ge(sem["q_out"], 16 * 3)
                        sp.wait_ge(sem["k_out"], 16 * 3)
                        sp.wait_ge(sem["v_out"], 16)

                @block.vector
                def _(dve):
                    ch = Chain(dve, sem["dve"])

                    def remainder(o):
                        a, c = o // DC, o % DC
                        dve.wait_ge(sem["p1"], o + 1)
                        dve.scalar_tensor_tensor(out=rest[:, o, :], in0=ps[:, QP + o, :], scalar=scale[a], in1=part[:, a, 0, c, :],
                                                 op0=ALU.mult, op1=ALU.subtract).then_inc(sem["rest"], 1)

                    if products:
                        remainder(0)
                        remainder(1)
                    if start:
                        dve.wait_ge(sem["x_in"], 16)
                        ln_stats(dve, ch, x, st, mv, sem["var"])
                    if products:
                        remainder(2)
                    if start:
                        ln_apply(dve, x, xn, mv, rstd, sem["rstd"], 1, sem["xn"])
                    if products:
                        remainder(3)

                @block.gpsimd
                def _(pool):
                    ch = Chain(pool, sem["pool"])
                    for o in range(4):
                        if products:
                            a, c = o // DC, o % DC
                            pool.wait_ge(sem["p2"], o + 1)
                            pool.tensor_tensor(part[:, a, 2, c, :], rest[:, o, :], part[:, a, 1, c, :], ALU.subtract).then_inc(sem["p3"], 1)
                        if start and o == 1:
                            ln_rstd(pool, ch, mv, rstd, k.neghalf, sem["var"], SUB, sem["rstd"])

                @block.tensor
                def _(pe):
                    if products:
                        for o in range(4):
                            a, c = o // DC, o % DC
                            for ic in range(DC):
                                mm = pe.matmul(ps[:, QP + o, :], w[:, a, ic, c * P:(c + 1) * P], xt[:, ic, :],
                                               start=(ic == 0), stop=(ic == DC - 1))
                            mm.then_inc(sem["qk_ps"], 1)
                        for s in range(SUB):
                            for ic in range(DC):
                                mm = pe.matmul(ps[:, VP + s // 2, (s % 2) * D:(s % 2 + 1) * D], xt[:, ic, s * P:(s + 1) * P],
                                               w[:, 2, ic, :], start=(ic == 0), stop=(ic == DC - 1))
                        mm.then_inc(sem["v_ps"], 1)
                    if start:
                        transpose_tile(pe, ps, XP, xn, k.ident, sem["xn"], 0, sem["xt_ps"])

                @block.scalar
                def _(act):
                    def second(o):
                        a, c = o // DC, o % DC
                        act.wait_ge(sem["rest"], o + 1)
                        act.activation(part[:, a, 1, c, :], rest[:, o, :], ACT.Copy).then_inc(sem["p2"], 1)

                    if products:
                        for o in range(4):
                            a, c = o // DC, o % DC
                            act.wait_ge(sem["qk_ps"], o + 1)
                            if store and c == 0:
                                act.wait_ge(sem[("q_out", "k_out")[a]], 16 * 3)
                            act.activation(part[:, a, 0, c, :], ps[:, QP + o, :], ACT.Copy, scale=scale[a]).then_inc(sem["p1"], 1)
                            if o:
                                second(o - 1)
                        second(3)
                        act.wait_ge(sem["v_ps"], 1)
                        if store:
                            act.wait_ge(sem["v_out"], 16)
                        act.activation(v[:, :, :, 0:DH],
                                       ps[:, VP:VP + 2, :].rearrange("p b (s h e) -> p (b s) h e", s=2, e=DH), ACT.Copy).then_inc(sem["v"], 1)
                    if start:
                        act.wait_ge(sem["xt_ps"], 1)
                        act.activation(xt[:, :, :], ps[:, XP:XP + DC, :], ACT.Copy).then_inc(sem["xt"], 1)
            nc.all_engine_barrier(sems_to_clear=cleared(sem))

        step(-1, start=True, products=False, store=False)
        step(0, start=True, products=True, store=False)
        with nc.Fori(1, NT - 1) as i:
            step(i, start=True, products=True, store=True)
        step(NT - 1, start=False, products=True, store=True)
        step(NT, start=False, products=False, store=True)



TILES = [7, 0, 2, 6, 3, 1, 5, 4]
QSLOTS = 8
KROWS = 6 * DH
SROWS = KROWS + 2
QPARTS = (0, 0, 1, 1, 0, 2)
KPARTS = (0, 1, 0, 1, 2, 0)
MAXSLOTS = 3
OSLOTS = 4
AHEAD = 4
LEAD = 1


def tile(n):
    return TILES[n % len(TILES)]


def attend_schedule(first, end):
    HOP, ROWS_IN, LOAD, COPY = 0.15, 2.5, 2.5, 0.6
    never = 1e9
    chunks = [(n, c) for n, t in enumerate(TILES) for c in range(SUB * (t + 1))]
    last = [chunks.index((n, SUB * (t + 1) - 1)) for n, t in enumerate(TILES)]
    maxima = [(n, s, b, j) for n in range(first, end) for s in range(SUB) for b in range(tile(n) + 1) for j in range(G)]
    order = []
    pe = act = dve = copied = 0.0
    exp_end, scores_end, summed, ring_end, max_end = [], [], [], [], {}
    rows = {n: 0.0 for n in range(first)}
    at = {"a": 0, "t": first, "s": 0, "m": 0}

    def width(n, c):
        return T - P * max(0, c - SUB * TILES[n])

    def ring_free():
        return ring_end[-MAXSLOTS] + HOP if len(ring_end) >= MAXSLOTS else 0.0

    while at["s"] < 2 * len(chunks) or at["a"] < len(chunks) or at["t"] < end:
        ready = {}
        if at["a"] < len(chunks) and at["s"] >= 2 * at["a"] + 2:
            ready["a"] = exp_end[2 * at["a"] + 1] + HOP
            if chunks[at["a"]][1] == 0:
                ready["a"] = max(ready["a"], copied + HOP)
        if at["t"] in max_end:
            ready["t"] = max(max_end[at["t"]] + HOP, ring_free())
        if at["s"] < 2 * len(chunks):
            q = at["s"] // 2
            n, c = chunks[q]
            if at["a"] >= q - 1 and (c > 0 or n in rows):
                ready["s"] = max(rows[n], exp_end[at["s"] - 2] + HOP if at["s"] >= 2 else 0.0)
        if at["m"] < len(maxima):
            n = maxima[at["m"]][0]
            load = scores_end[2 * last[n - QSLOTS] + 1] + LOAD if n >= QSLOTS and len(scores_end) > 2 * last[n - QSLOTS] + 1 else \
                never if n >= QSLOTS else 0.0
            if load < never:
                ready["m"] = max(load, ring_free())
        behind = at["m"] * 2 * len(chunks) < (at["s"] + AHEAD) * G * len(chunks)
        kind = min(ready, key=lambda x: (max(pe, ready[x]), ("tmas" if behind else "tasm").index(x)))
        start = max(pe, ready[kind])
        i = at[kind]
        at[kind] += 1
        if kind == "a":
            n, c = chunks[i]
            pe = start + width(n, c) * 4 / 2400
            summed.append(pe)
            if i == last[n]:
                act = copied = max(act, pe + HOP) + COPY
            order.append(("a", n, c))
        elif kind == "t":
            pe = start + 0.24
            dve = max(dve, pe + HOP) + 0.62
            ring_end.append(dve)
            rows[i] = dve + ROWS_IN
            order.append(("t", i))
        elif kind == "s":
            q = i // 2
            n, c = chunks[q]
            pe = start + 2 * width(n, c) / 2400 + (0.11 if c >= SUB * TILES[n] else 0.0)
            scores_end.append(pe)
            act = max(act, pe + HOP, summed[q - 2] + HOP if q >= 2 else 0.0) + 2 * width(n, c) / 1200 + 0.1
            exp_end.append(act)
            order.append(("s", n, c, i % 2))
        else:
            n, s, b, j = maxima[i]
            w = T if b < tile(n) else (s + 1) * P
            pe = start + w / 2400 + (0.06 if b == tile(n) else 0.0)
            dve = max(dve, pe + HOP) + w / 960 + 0.08
            ring_end.append(dve)
            if (s, b, j) == (SUB - 1, tile(n), G - 1):
                dve += 0.45
                max_end[n] = dve
            order.append(("m", n, s, b, j))
    return order


def attend(nc, io, k, ps, scr):
    NTL = len(TILES)
    chunks = [(n, c) for n, t in enumerate(TILES) for c in range(SUB * (t + 1))]
    chunk_no = {nc_: i for i, nc_ in enumerate(chunks)}
    last_chunk = [chunk_no[(n, SUB * (t + 1) - 1)] for n, t in enumerate(TILES)]
    LT = max(TILES[:LEAD]) + 1

    def off(n, c):
        return max(0, c - SUB * TILES[n]) * P

    names = [f"k_in{i}" for i in range(NT)] + [f"v_in{i}" for i in range(NT)] + [f"q_in{n}" for n in range(NTL)] + \
            [f"rows_in{n}" for n in range(NTL)] + [f"stored{n}" for n in range(NTL)] + \
            ["lead_in", "scores", "probs", "summed", "max_ps", "max_used", "neg_max", "turned", "out_sb", "dve", "ones"]
    with ExitStack() as ctx:
        sb = lambda n, shape, dt=F32: ctx.enter_context(nc.sbuf_tensor(n, shape, dt))
        sem = loop_sems(k.loop_sems, names)
        k_in, v_in = [sem[f"k_in{i}"] for i in range(NT)], [sem[f"v_in{i}"] for i in range(NT)]
        q_in, rows_in, stored = ([sem[f"{x}{n}"] for n in range(NTL)] for x in ("q_in", "rows_in", "stored"))
        kb = sb("kb", [P, G, N], BF16)
        kl = sb("kb_next", [P, G, LT * T], BF16)
        qb = sb("qb", [P, QSLOTS, G, T], BF16)
        vb = sb("vb", [P, N // P, G * 2 * DH])
        pb = sb("pb", [P, 4, 2, T])
        mx = sb("mx", [P, 2, G, SUB, NT])
        nm = sb("nm", [P, G, SUB])
        cb = sb("cb", [P, 2, SUB, G, 2], BF16)
        cr = sb("cr", [2 * G, 2, T], BF16)
        ob = sb("ob", [P, OSLOTS, T])
        AV, RING = 4, 5

        def group(g, steps, first, end):
            ring = [st for st in steps if st[0] in "mt"]
            ring_no = {u: i for i, u in enumerate(ring)}
            whole = any(st[0] == "s" for st in steps)
            with nc.Block() as block:
                @block.sync
                def _(sp):
                    qv = scr.q.rearrange("a (g j d) n -> a g d j n", g=NG, j=G)
                    kv = scr.k.rearrange("a (g j d) n -> a g d j n", g=NG, j=G)
                    vv = scr.v.rearrange("(c p) (g m) -> g p c m", p=P, g=NG)
                    ov = scr.o.rearrange("(g r) n -> g r n", g=NG)

                    def load_q(n):
                        if n >= QSLOTS and whole:
                            sp.wait_ge(sem["scores"], 2 * (last_chunk[n - QSLOTS] + 1))
                        for r, a in enumerate(QPARTS):
                            sp.dma_start(qb[r * DH:(r + 1) * DH, n % QSLOTS],
                                         qv[a, g + n // NTL][:, :, tile(n) * T:(tile(n) + 1) * T]).then_inc(q_in[n % NTL], 16)

                    def load_k(i):
                        for r, a in enumerate(KPARTS):
                            sp.dma_start(kb[r * DH:(r + 1) * DH, :, i * T:(i + 1) * T],
                                         kv[a, g][:, :, i * T:(i + 1) * T]).then_inc(k_in[i], 16)

                    def load_lead():
                        for r, a in enumerate(KPARTS):
                            sp.dma_start(kl[r * DH:(r + 1) * DH], kv[a, g + 1][:, :, 0:LT * T]).then_inc(sem["lead_in"], 16)

                    def load_v(i):
                        sp.dma_start(vb[:, i * SUB:(i + 1) * SUB], vv[g][:, i * SUB:(i + 1) * SUB]).then_inc(v_in[i], 16)

                    def store(n):
                        sp.wait_ge(sem["out_sb"], n + 1)
                        sp.dma_start(ov[g][:, TILES[n] * T:(TILES[n] + 1) * T], ob[:, n % OSLOTS]).then_inc(stored[n], 16)

                    def send_rows(n):
                        sp.wait_ge(sem["turned"], n - first + 1)
                        for j in range(G):
                            sp.dma_start(qb[KROWS:SROWS, n % QSLOTS, j], cr[2 * j:2 * j + 2, n % 2]).then_inc(rows_in[n % NTL], 16)

                    if whole:
                        load_k(0)
                        load_v(0)
                        load_q(LEAD)
                        for i in range(1, NT):
                            load_k(i)
                            load_v(i)
                            if i < QSLOTS - LEAD:
                                load_q(LEAD + i)
                        if end > NTL:
                            load_lead()
                        for n in range(NTL):
                            for m in range(max(first, n + LEAD), min(end, n + LEAD + 1)):
                                send_rows(m)
                            if n + QSLOTS < end:
                                load_q(n + QSLOTS)
                            store(n)
                        for n in range(NTL):
                            sp.wait_ge(stored[n], 16)
                    else:
                        load_lead()
                        for n in range(first, end):
                            load_q(n)
                        for n in range(first, end):
                            send_rows(n)
                    for n in range(max(first, NTL), end):
                        sp.wait_ge(rows_in[n % NTL], 16 * G)

                @block.tensor
                def _(pe):
                    def ring_bank(u):
                        i = ring_no[u]
                        if i >= MAXSLOTS:
                            pe.wait_ge(sem["max_used"], i - MAXSLOTS + 1)
                        return RING + i % MAXSLOTS

                    seen_k = seen_v = 0
                    for st in steps:
                        n = st[1]
                        t = tile(n)
                        if st[0] == "m":
                            s, b, j = st[2:]
                            if (s, b, j) == (0, 0, 0):
                                pe.wait_ge(q_in[n % NTL], 16 * len(QPARTS))
                                if n == NTL:
                                    pe.wait_ge(sem["lead_in"], 16 * len(KPARTS))
                            while n < NTL and seen_k <= b:
                                pe.wait_ge(k_in[seen_k], 16 * len(KPARTS))
                                seen_k += 1
                            keys = kb if n < NTL else kl
                            width = T if b < t else (s + 1) * P
                            bank = ring_bank(st)
                            mm = pe.matmul(ps[:, bank, 0:width], qb[0:KROWS, n % QSLOTS, j, s * P:(s + 1) * P],
                                           keys[0:KROWS, j, b * T:b * T + width], start=True, stop=(b < t))
                            if b == t:
                                mm = pe.matmul(ps[:, bank, s * P:width], k.identb[:, :], k.mask_qk[:, :],
                                               start=False, stop=True)
                            mm.then_inc(sem["max_ps"], 1)
                        elif st[0] == "t":
                            pe.wait_ge(sem["neg_max"], n - first + 1)
                            bank = ring_bank(st)
                            for s in range(SUB):
                                mm = pe.matmul(ps[0:2 * G, bank, s * P:(s + 1) * P], cb[:, n % 2, s, :, :].rearrange("p j a -> p (j a)"),
                                               k.identb[:, :], start=True, stop=True)
                            mm.then_inc(sem["max_ps"], 1)
                        elif st[0] == "s":
                            c, pair = st[2:]
                            u = 2 * chunk_no[(n, c)] + pair
                            o = off(n, c)
                            if c == 0 and pair == 0 and n >= first:
                                pe.wait_ge(rows_in[n], 16 * G)
                            while seen_k <= c // SUB:
                                pe.wait_ge(k_in[seen_k], 16 * len(KPARTS))
                                seen_k += 1
                            if u >= 2:
                                pe.wait_ge(sem["probs"], u - 1)
                            diagonal = c >= SUB * t
                            for j in (2 * pair, 2 * pair + 1):
                                mm = pe.matmul(ps[:, j, o:T], kb[0:SROWS, j, c * P:(c + 1) * P],
                                               qb[0:SROWS, n % QSLOTS, j, o:T], start=True, stop=not diagonal)
                                if diagonal:
                                    mm = pe.matmul(ps[:, j, o:o + P], k.identb[:, :], k.mask_kq[:, :],
                                                   start=False, stop=True)
                            mm.then_inc(sem["scores"], 1)
                        else:
                            c = st[2]
                            q = chunk_no[(n, c)]
                            o = off(n, c)
                            while seen_v <= c // SUB:
                                pe.wait_ge(v_in[seen_v], 16)
                                seen_v += 1
                            if c == 0 and n > 0:
                                pe.wait_ge(sem["out_sb"], n)
                            pe.wait_ge(sem["probs"], 2 * q + 2)
                            for j in range(G):
                                mm = pe.matmul(ps[32 * j:32 * j + 32, AV, o:T], vb[:, c, 32 * j:32 * j + 32],
                                               pb[:, 2 * (q % 2) + j // 2, j % 2, o:T],
                                               start=(c == 0), stop=(q == last_chunk[n]), tile_position=(0, 32 * j),
                                               skip_group_check=True)
                            mm.then_inc(sem["summed"], 1)

                @block.scalar
                def _(act):
                    def copy_out(n):
                        act.wait_ge(sem["summed"], last_chunk[n] + 1)
                        if n >= OSLOTS:
                            act.wait_ge(stored[n - OSLOTS], 16)
                        act.activation(ob[:, n % OSLOTS], ps[:, AV, :], ACT.Copy).then_inc(sem["out_sb"], 1)

                    for st in steps:
                        n = st[1]
                        if st[0] == "s":
                            c, pair = st[2:]
                            q = chunk_no[(n, c)]
                            o = off(n, c)
                            act.wait_ge(sem["scores"], 2 * q + pair + 1)
                            if q >= 2 and pair == 0:
                                act.wait_ge(sem["summed"], q - 1)
                            act.activation(pb[:, 2 * (q % 2) + pair, :, o:T], ps[:, 2 * pair:2 * pair + 2, o:T],
                                           ACT.Exp).then_inc(sem["probs"], 1)
                        elif st[0] == "a" and chunk_no[st[1:]] == last_chunk[n]:
                            copy_out(n)

                @block.vector
                def _(dve):
                    ch = Chain(dve, sem["dve"])
                    for i, u in enumerate(ring):
                        n = u[1]
                        t = tile(n)
                        dve.wait_ge(sem["max_ps"], i + 1)
                        bank = RING + i % MAXSLOTS
                        if u[0] == "m":
                            s, b, j = u[2:]
                            width = T if b < t else (s + 1) * P
                            dve.tensor_reduce(mx[:, n % 2, j, s, b:b + 1], ps[:, bank, 0:width], AX, ALU.max)\
                               .then_inc(sem["max_used"], 1)
                            if (s, b, j) == (SUB - 1, t, G - 1):
                                dve.wait_ge(sem["max_used"], i + 1)
                                if n >= first + 2:
                                    dve.wait_ge(sem["turned"], n - first - 1)
                                ch.link(dve.tensor_reduce(nm[:, :, :], mx[:, n % 2, :, :, 0:t + 1], AX, ALU.max))
                                nms = nm[:, :, :].rearrange("p j s -> p s j")
                                ch.link(dve.tensor_scalar(cb[:, n % 2, :, :, 0], nms, -1.0, None, ALU.mult))
                                dve.scalar_tensor_tensor(out=cb[:, n % 2, :, :, 1], in0=nms, scalar=-1.0, in1=cb[:, n % 2, :, :, 0],
                                                         op0=ALU.mult, op1=ALU.subtract).then_inc(sem["neg_max"], 1)
                                dve.wait_ge(sem["neg_max"], n - first + 1)
                        else:
                            if n >= first + 2:
                                dve.wait_ge(rows_in[(n - 2) % NTL], 16 * G)
                            dve.tensor_copy(cr[:, n % 2, :], ps[0:2 * G, bank, :]).then_inc(sem["turned"], 1)
                            dve.wait_ge(sem["turned"], n - first + 1)
                            dve.engine_nop().then_inc(sem["max_used"], 1)

                @block.gpsimd
                def _(pool):
                    if not whole:
                        pool.memset(kb[KROWS:SROWS, :, :], 1.0).then_inc(sem["ones"], 1)
                        pool.wait_ge(sem["ones"], 1)
            nc.all_engine_barrier(sems_to_clear=cleared(sem))

        lead_only = [st for st in attend_schedule(LEAD, NTL + LEAD) if st[0] in "mt" and st[1] >= NTL]
        group(-1, lead_only, NTL, NTL + LEAD)
        with nc.Fori(0, NG - 1) as g:
            group(g, attend_schedule(LEAD, NTL + LEAD), LEAD, NTL + LEAD)
        group(NG - 1, attend_schedule(LEAD, NTL), LEAD, NTL)



FINISH_NORM, FINISH_HOT, FINISH_TURN, START_OUT, START_ADD, START_TURN, START_GATE, START_PICK, START_ROWS, START_BIAS = 0, 1, 5, 4, 5, 8, 10, 11, 13, 14


def mix(nc, io, k, ps, scr):
    XP, TP, EP, LP = 0, 2, 4, 7
    EBANKS = 3
    UNITS = SUB * E // 2
    names = ["x_in", "o_in", "den_in", "dve", "pool", "on", "o_ps", "var", "rstd", "xn", "tn_ps", "tn", "gl_ps", "expo",
             "expd", "gate", "gt_ps", "gt", "bias_ps", "e_ps", "e_used", "now", "x1_now", "gate_now", "f_var", "f_rstd", "f_xn",
             "f_ps", "f_out", "hot", "l_ps", "off", "f_off"]
    with ExitStack() as ctx:
        sb = lambda n, shape, dt=F32: ctx.enter_context(nc.sbuf_tensor(n, shape, dt))
        wsem = stage_sems(ctx, nc, "mixw", ["in_", "zero", "lrow", "lt_ps", "lt", "den", "inv", "stored"])
        sem = loop_sems(k.loop_sems, names)
        wout, we, eb = sb("w_out", [P, DC, D]), sb("w_e", [P, DC, E, D]), sb("e_bias", [E, D])
        o, den = sb("o_c", [P, DC, T]), sb("den_c", [P, DC, T])
        x = sb("x_c", [P, SUB, D])
        x1, xt, gate = sb("x1_c", [P, SUB, D]), sb("xt_c", [P, DC, T]), sb("gate", [P, SUB, E])
        x1n, xtn, gaten = sb("x1_next", [P, SUB, D]), sb("xt_next", [P, DC, T]), sb("gate_next", [P, SUB, E])
        xn, fn = sb("xn_c", [P, SUB, D]), sb("fn_c", [P, SUB, D])
        st, mv, rstd = sb("st_c", [P, SUB, 6]), sb("mv_c", [P, SUB, 2]), sb("rstd_c", [P, SUB])
        fst, fmv, frstd = sb("fst_c", [P, SUB, 6]), sb("fmv_c", [P, SUB, 2]), sb("frstd_c", [P, SUB])
        off, foff = sb("off_c", [P, SUB]), sb("foff_c", [P, SUB])
        lg, gm, gs = sb("lg", [P, SUB, E]), sb("gm", [P, SUB]), sb("gs", [P, SUB])
        more, ties = sb("more", [P, SUB, E, E]), sb("ties", [P, SUB, E, E])
        rank, ex = sb("rank", [P, SUB, E]), sb("ex", [P, SUB, E])
        gt = sb("gt", [E, T])
        hot, tok = sb("hot", [P, SUB, M]), k.tok
        lx = sb("lx", [M, D])
        inv = sb("inv_den", [P, T])
        with nc.Block() as block:
            @block.sync
            def _(sp):
                for i in range(NT):
                    sp.dma_start(inv[i * H:(i + 1) * H, :], scr.o.rearrange("(h r) n -> r h n", h=H)[DH][:, i * T:(i + 1) * T])\
                      .then_inc(wsem["den"], 16)
                sp.dma_start(wout[:], io["L0_attn_Wout"].rearrange("(c h) e n -> (h e) c n", c=DC)).then_inc(wsem["in_"], 16)
                for e in range(E):
                    sp.dma_start(we[:, :, e], io["L0_ffn_expert_w"][e].rearrange("(c p) n -> p c n", p=P)).then_inc(wsem["in_"], 16)
                sp.dma_start(eb[:], io["L0_ffn_expert_b"]).then_inc(wsem["in_"], 16)
                sp.wait_ge(wsem["inv"], 1)
                sp.dma_start(scr.r.rearrange("i h n -> (i h) n"), inv[:]).then_inc(wsem["stored"], 16)
                sp.wait_ge(wsem["stored"], 16)
                sp.wait_ge(wsem["in_"], 16 * (E + 2))

            @block.vector
            def _(dve):
                dve.wait_ge(wsem["den"], 16 * NT)
                dve.reciprocal(inv[:], inv[:]).then_inc(wsem["inv"], 1)
                dve.memset(hot[:], 0.0).then_inc(wsem["zero"], 1)

            @block.tensor
            def _(pe):
                pe.wait_ge(wsem["zero"], 1)
                pe.matmul(ps[0:M, LP, 0:D], hot[:, 0, :], hot[:].rearrange("p s m -> p (s m)"), start=True, stop=True).then_inc(wsem["lrow"], 1)
                pe.wait_ge(wsem["lrow"], 1)

        def half(ap, bank, s):
            return ap[:, bank + s // 2, (s % 2) * D:(s % 2 + 1) * D]

        def step(i, start, experts, finish):
            with nc.Block() as block:
                @block.sync
                def _(sp):
                    if start:
                        ov = scr.o.rearrange("(c h two e) (i n) -> i two c h e n", c=DC, two=2, e=DH, n=T)
                        rv = scr.r.rearrange("i (c h) n -> i c h n", c=DC)
                        for c in range(DC):
                            sp.dma_start(den[:, c], bc(rv[i + 1, c], 1, [H // DC, DH, T])).then_inc(sem["den_in"], 16)
                            sp.dma_start(o[:, c], ov[i + 1, 0, c]).then_inc(sem["o_in"], 16)
                        sp.dma_start(x[:], io["L0_attn_x"].rearrange("o (i s p) d -> (o i) p s d", s=SUB, p=P)[i + 1]).then_inc(sem["x_in"], 16)

                @block.tensor
                def _(pe):
                    def project_out():
                        pe.wait_ge(sem["on"], DC)
                        for s in range(SUB):
                            for c in range(DC):
                                mm = pe.matmul(half(ps, XP, s), o[:, c, s * P:(s + 1) * P], wout[:, c, :], start=(c == 0), stop=(c == DC - 1))
                            mm.then_inc(sem["o_ps"], 1)

                    def gate_logits():
                        pe.wait_ge(sem["tn"], 1)
                        for s in range(SUB):
                            for c in range(DC):
                                mm = pe.matmul(ps[:, XP, s * E:(s + 1) * E], xtn[:, c, s * P:(s + 1) * P], k.gate_w[:, c, :],
                                               start=(c == 0), stop=(c == DC - 1))
                        mm.then_inc(sem["gl_ps"], 1)

                    def gate_rows():
                        pe.wait_ge(sem["gate"], 1)
                        for s in range(SUB):
                            tr = pe.transpose(ps[0:E, XP + 1, s * P:(s + 1) * P], gaten[:, s, :], k.ident[:, :])
                        tr.then_inc(sem["gt_ps"], 1)

                    def gated_biases():
                        pe.wait_ge(sem["gt"], 1)
                        for s in range(SUB):
                            mm = pe.matmul(half(ps, XP, s), gt[:, s * P:(s + 1) * P], eb[:, :], start=True, stop=True)
                        mm.then_inc(sem["bias_ps"], 1)

                    def landmark_rows():
                        pe.wait_ge(sem["hot"], 1)
                        for s in range(SUB):
                            mm = pe.matmul(ps[0:M, LP, 0:D], hot[:, s, :], fn[:, s, :], start=False, stop=True, skip_group_check=True)
                        mm.then_inc(sem["l_ps"], 1)

                    for n in range(UNITS):
                        if experts:
                            s, e = n // (E // 2), 2 * (n % (E // 2))
                            if n % (E // 2) == 0:
                                pe.wait_ge(sem["now"], s + 1)
                            if n >= EBANKS:
                                pe.wait_ge(sem["e_used"], n - EBANKS + 1)
                            for c in range(DC):
                                mm = pe.matmul(ps[:, EP + n % EBANKS, :], xt[:, c, s * P:(s + 1) * P],
                                               we[:, c, e:e + 2, :].rearrange("p e n -> p (e n)"), start=(c == 0), stop=(c == DC - 1))
                            mm.then_inc(sem["e_ps"], 1)
                        if finish and n == FINISH_TURN:
                            transpose_tile(pe, ps, TP, fn, k.ident, sem["f_xn"], 0, sem["f_ps"])
                            landmark_rows()
                        if start and n == START_OUT:
                            project_out()
                        if start and n == START_TURN:
                            if finish:
                                pe.wait_ge(sem["f_out"], 1)
                            transpose_tile(pe, ps, TP, xn, k.ident, sem["xn"], 0, sem["tn_ps"])
                        if start and n == START_TURN + 1:
                            gate_logits()
                        if start and n == START_ROWS:
                            gate_rows()
                        if start and n == START_ROWS + 1:
                            gated_biases()

                @block.vector
                def _(dve):
                    ch = Chain(dve, sem["dve"])

                    def gate_ranks():
                        full = [P, SUB, E, E]
                        dve.wait_ge(sem["gl_ps"], 1)
                        ch.link(dve.tensor_tensor(lg[:], ps[:, XP, 0:SUB * E].rearrange("p (s e) -> p s e", s=SUB),
                                                  bc(k.gate_b[:, :], 1, [P, SUB, E]), ALU.add))
                        ch.step(dve.tensor_reduce(gm[:], lg[:], AX, ALU.max))
                        ch.step(dve.tensor_tensor(more[:], bc(lg[:], 2, full), bc(lg[:], 3, full), ALU.is_gt))
                        ch.step(dve.tensor_tensor(ties[:], bc(lg[:], 2, full), bc(lg[:], 3, full), ALU.is_equal))
                        ch.wait()
                        dve.tensor_tensor(lg[:], lg[:], bc(gm[:], 2, [P, SUB, E]), ALU.subtract).then_inc(sem["expd"], 1)
                        ch.link(dve.tensor_tensor(ties[:], ties[:], bc(k.before[:], 1, full), ALU.mult))
                        ch.step(dve.tensor_tensor(more[:], more[:], ties[:], ALU.add))

                    def gate_weights():
                        ch.wait()
                        ch.link(dve.tensor_reduce(rank[:], more[:], AX, ALU.add))
                        dve.wait_ge(sem["expo"], 1)
                        ch.link(dve.scalar_tensor_tensor(out=gaten[:], in0=rank[:], scalar=float(TOP), in1=ex[:], op0=ALU.is_lt, op1=ALU.mult))
                        ch.link(dve.tensor_reduce(gs[:], gaten[:], AX, ALU.add))
                        ch.link(dve.reciprocal(gs[:], gs[:]))
                        dve.tensor_tensor(gaten[:], gaten[:], bc(gs[:], 2, [P, SUB, E]), ALU.mult).then_inc(sem["gate"], 1)

                    if experts:
                        dve.tensor_copy(gate[:], gaten[:]).then_inc(sem["gate_now"], 1)
                    for n in range(UNITS):
                        if experts:
                            s, e = n // (E // 2), 2 * (n % (E // 2))
                            if n == 0:
                                dve.wait_ge(sem["gate_now"], 1)
                            if n == E // 2:
                                dve.wait_ge(sem["x1_now"], 1)
                            dve.wait_ge(sem["e_ps"], n + 1)
                            bank = ps[:, EP + n % EBANKS, :]
                            ch.link(dve.scalar_tensor_tensor(out=x1[:, s, :], in0=bank[:, 0:D], scalar=gate[:, s, e:e + 1],
                                                             in1=(x1n if n == 0 else x1)[:, s, :], op0=ALU.mult, op1=ALU.add))
                            to = k.x2[:, bass.ds(i * SUB + s, 1), :].rearrange("p o d -> p (o d)") if e == E - 2 else x1[:, s, :]
                            dve.scalar_tensor_tensor(out=to, in0=bank[:, D:2 * D], scalar=gate[:, s, e + 1:e + 2],
                                                     in1=x1[:, s, :], op0=ALU.mult, op1=ALU.add).then_inc(sem["e_used"], 1)
                            if not e == E - 2:
                                dve.wait_ge(sem["e_used"], n + 1)
                        if finish and n == FINISH_NORM:
                            for s in range(SUB):
                                ch.step(dve.bn_stats(fst[:, s, :], k.x2[:, bass.ds((i - 1) * SUB + s, 1), :].rearrange("p o d -> p (o d)")))
                            ch.wait()
                            for s in range(SUB):
                                dve.bn_aggr(fmv[:, s, :], fst[:, s, :]).then_inc(sem["f_var"], 1)
                        if finish and n == FINISH_HOT:
                            ch.link(dve.tensor_tensor(hot[:], bc(k.idx[:, :], 1, [P, SUB, M]), bc(tok[:], 2, [P, SUB, M]), ALU.is_equal))
                            dve.tensor_scalar(tok[:], tok[:], float(T), None, ALU.add).then_inc(sem["hot"], 1)
                        if start and n == START_ADD:
                            dve.wait_ge(sem["x_in"], 16)
                            if experts:
                                dve.wait_ge(sem["x1_now"], 1)
                            for s in range(SUB):
                                dve.wait_ge(sem["o_ps"], 2 * (s // 2) + 2)
                                ch.step(dve.tensor_tensor(x1n[:, s, :], x[:, s, :], half(ps, XP, s), ALU.add))
                            ch.wait()
                            ln_stats(dve, ch, x1n, st, mv, sem["var"])
                        if start and n == START_GATE:
                            gate_ranks()
                        if start and n == START_PICK:
                            gate_weights()
                        if start and n == START_BIAS:
                            dve.wait_ge(sem["bias_ps"], 1)
                            for s in range(SUB):
                                ch.step(dve.tensor_tensor(x1n[:, s, :], x1n[:, s, :], half(ps, XP, s), ALU.add))

                @block.gpsimd
                def _(pool):
                    ch = Chain(pool, sem["pool"])
                    if experts:
                        pool.tensor_copy(x1[:, 1:], x1n[:, 1:]).then_inc(sem["x1_now"], 1)
                    if finish:
                        ln_rstd(pool, ch, fmv, frstd, k.neghalf, sem["f_var"], SUB, sem["f_rstd"])
                        ln_offset(pool, ch, fmv, frstd, foff, sem["f_rstd"], 1, sem["f_off"])
                    if start:
                        for c in range(DC):
                            if c == 0:
                                pool.wait_ge(sem["den_in"], 16 * DC)
                                pool.wait_ge(sem["o_in"], 16 * DC)
                            pool.tensor_tensor(o[:, c], o[:, c], den[:, c], ALU.mult).then_inc(sem["on"], 1)
                        ln_rstd(pool, ch, mv, rstd, k.neghalf, sem["var"], SUB, sem["rstd"])
                        ln_offset(pool, ch, mv, rstd, off, sem["rstd"], 1, sem["off"])

                @block.scalar
                def _(act):
                    if experts:
                        for s in range(SUB):
                            act.activation(xt[:, :, s * P:(s + 1) * P], xtn[:, :, s * P:(s + 1) * P], ACT.Copy).then_inc(sem["now"], 1)
                    if finish:
                        ln_affine(act, lambda s: k.x2[:, bass.ds((i - 1) * SUB + s, 1), :].rearrange("p o d -> p (o d)"),
                                  fn, frstd, foff, sem["f_off"], 1, sem["f_xn"])
                        act.wait_ge(sem["f_ps"], 1)
                        act.activation(k.xn3t[:, :, bass.ds((i - 1) * T, T)], ps[:, TP:TP + DC, :], ACT.Copy).then_inc(sem["f_out"], 1)
                    if start:
                        ln_affine(act, lambda s: x1n[:, s, :], xn, rstd, off, sem["off"], 1, sem["xn"])
                        act.wait_ge(sem["tn_ps"], 1)
                        if experts:
                            act.wait_ge(sem["now"], SUB)
                        act.activation(xtn[:], ps[:, TP:TP + DC, :], ACT.Copy).then_inc(sem["tn"], 1)
                        act.wait_ge(sem["expd"], 1)
                        act.activation(ex[:], lg[:], ACT.Exp).then_inc(sem["expo"], 1)
                        act.wait_ge(sem["gt_ps"], 1)
                        act.activation(gt[:], ps[0:E, XP + 1, :], ACT.Copy).then_inc(sem["gt"], 1)
            nc.all_engine_barrier(sems_to_clear=cleared(sem))

        step(-1, start=True, experts=False, finish=False)
        step(0, start=True, experts=True, finish=False)
        with nc.Fori(1, NT - 1) as i:
            step(i, start=True, experts=True, finish=True)
        step(NT - 1, start=False, experts=True, finish=True)
        step(NT, start=False, experts=False, finish=True)
        with nc.Block() as block:
            @block.vector
            def _(dve):
                dve.tensor_copy(lx[:], ps[0:M, LP, 0:D]).then_inc(wsem["lt"], 1)
                dve.wait_ge(wsem["lt_ps"], 1)
                dve.tensor_copy(k.lxt[:], ps[:, 0, 0:DC * M].rearrange("p (c m) -> p c m", c=DC)).then_inc(wsem["lt"], 1)

            @block.tensor
            def _(pe):
                pe.wait_ge(wsem["lt"], 1)
                for c in range(DC):
                    tr = pe.transpose(ps[:, 0, c * M:(c + 1) * M], lx[:, c * P:(c + 1) * P], k.ident[0:M, 0:M])
                tr.then_inc(wsem["lt_ps"], 1)



NROW, OROW = 64, 96
LROWS = OROW + 1


def landmark_operands(nc, io, k, ps, la, lk, scr):
    with ExitStack() as ctx:
        sb = lambda n, shape, dt=F32: ctx.enter_context(nc.sbuf_tensor(n, shape, dt))
        sem = stage_sems(ctx, nc, "lm", ["dve", "act", "l_ps", "lk", "sq", "n_ps", "ready", "w_ps", "w", "out"])
        sq, sql = sb("sq_la", [64, G, G * M]), sb("sq_lk", [64, G, M])
        wm = sb("wm", [M, H, M])
        laf = la[:].rearrange("p g j m -> p g (j m)")
        with nc.Block() as block:
            @block.tensor
            def _(pe):
                for c in range(DC):
                    for ic in range(DC):
                        mm = pe.matmul(ps[:, 0, c * M:(c + 1) * M], k.wk1[:, ic, c * P:(c + 1) * P], k.lxt[:, ic, :],
                                       start=(ic == 0), stop=(ic == DC - 1))
                mm.then_inc(sem["l_ps"], 1)
                pe.wait_ge(sem["sq"], 2)
                pe.matmul(ps[NROW:NROW + 32, 1, 0:G * M], k.sel[:, :], sql[:].rearrange("p g m -> p (g m)"), start=True, stop=True,
                          tile_position=(0, NROW)).then_inc(sem["n_ps"], 1)
                for b in range(2):
                    mm = pe.matmul(ps[OROW:OROW + 1, 2 + b, :], k.quarter[:, :], sq[:, 2 * b:2 * b + 2, :].rearrange("p g m -> p (g m)"),
                                   start=True, stop=True, tile_position=(0, OROW))
                mm.then_inc(sem["n_ps"], 1)
                pe.wait_ge(sem["ready"], 1)
                for g in range(G):
                    mm = pe.matmul(ps[0:M, 4 + g // 2, (g % 2) * D:(g % 2 + 1) * D], lk[0:LROWS, g, :], laf[0:LROWS, g],
                                   start=True, stop=True)
                mm.then_inc(sem["w_ps"], 1)

            @block.vector
            def _(dve):
                ch = Chain(dve, sem["dve"])
                ch.step(dve.memset(lk[OROW:LROWS], 1.0))
                for g in range(G):
                    ch.step(dve.tensor_copy(la[NROW:NROW + 32, g], k.blk1[NROW:NROW + 32]))
                dve.wait_ge(sem["l_ps"], 1)
                for g in range(G):
                    r, c = 64 * (g % 2), g // 2
                    ch.step(dve.tensor_scalar(lk[0:64, g, :], ps[r:r + 64, 0, c * M:(c + 1) * M], k.bk1[r:r + 64, c:c + 1], None, ALU.add))
                ch.wait()
                for g in range(G):
                    ch.step(dve.tensor_tensor(la[0:64, g], bc(lk[0:64, g, :], 1, [64, G, M]), k.blk2[:], ALU.mult))
                dve.tensor_tensor(sql[:], lk[0:64], lk[0:64], ALU.mult).then_inc(sem["sq"], 1)
                ch.wait()
                dve.tensor_tensor(sq[:], laf[0:64], laf[0:64], ALU.mult).then_inc(sem["sq"], 1)
                dve.wait_ge(sem["n_ps"], 2)
                ch.step(dve.tensor_copy(lk[NROW:NROW + 32], ps[NROW:NROW + 32, 1, 0:G * M].rearrange("p (g m) -> p g m", g=G)))
                ch.link(dve.tensor_copy(laf[OROW:LROWS].rearrange("p (b g) m -> p b (g m)", b=2), ps[OROW:LROWS, 2:4, :]))
                dve.engine_nop().then_inc(sem["ready"], 1)
                dve.wait_ge(sem["w_ps"], 1)
                dve.tensor_scalar(wm[:].rearrange("p (b h) m -> p b (h m)", b=2), ps[0:M, 4:6, :], 0.0, None, ALU.max).then_inc(sem["w"], 1)
                dve.wait_ge(sem["w"], 2)
                dve.tensor_tensor(wm[:], wm[:], bc(k.regi[:], 1, [M, H, M]), ALU.add).then_inc(sem["w"], 1)

            @block.scalar
            def _(act):
                act.wait_ge(sem["w"], 1)
                act.activation(wm[:], wm[:], ACT.Exp, scale=k.negt[0:M, 0:1]).then_inc(sem["w"], 1)

            @block.sync
            def _(sp):
                sp.wait_ge(sem["w"], 3)
                sp.dma_start(scr.w.rearrange("h a b -> a h b"), wm[:]).then_inc(sem["out"], 16)
                sp.wait_ge(sem["out"], 16)


def rows_of(k, i):
    return k.xn3t[:, :, bass.ds(i * T, T)]


def operand_project(pe, k, ps, w, rows, sem, PB):
    for c in range(DC):
        for ic in range(DC):
            mm = pe.matmul(ps[:, PB + c, :], w[:, ic, c * P:(c + 1) * P], rows[:, ic, :], start=(ic == 0), stop=(ic == DC - 1))
        mm.then_inc(sem["a_ps"], 1)


def operand_norms(pe, k, ps, sq, sem, NB):
    pe.wait_ge(sem["sq"], 1)
    for g in range(G):
        mm = pe.matmul(ps[32 * g:32 * g + 32, NB, :], k.sel[:, :], sq[:, g, :], start=True, stop=True,
                       tile_position=(0, 32 * g), skip_group_check=True)
    mm.then_inc(sem["an_ps"], 1)


def operand_act(act, ps, a, b, sq, sem, PB, NB):
    for g in range(G):
        r, c = 64 * (g % 2), g // 2
        act.wait_ge(sem["a_ps"], c + 1)
        act.activation(a[0:64, g, :], ps[r:r + 64, PB + c, :], ACT.Identity, bias=b[r:r + 64, c:c + 1]).then_inc(sem["a_in"], 1)
    act.wait_ge(sem["a_in"], G)
    act.activation(sq[:], a[0:64], ACT.Square).then_inc(sem["sq"], 1)
    act.wait_ge(sem["an_ps"], 1)
    for g in range(G):
        act.activation(a[NROW:NROW + 32, g, :], ps[32 * g:32 * g + 32, NB, :], ACT.Copy).then_inc(sem["an_in"], 1)


OPERAND = ["a_ps", "a_in", "sq", "an_ps", "an_in"]


KEY_STEPS = (("D0",), ("D1",), ("D2",), ("K0", "Z0"), ("D3",), ("Z1", "K1"), ("Z2", "V"), ("Z3", "N"))


def keys(nc, io, k, ps, scr, winv, zt, acc):
    KP, PV, CP, ZP = 0, 1, 2, 6
    SWEEPS = M // NT
    with ExitStack() as ctx:
        sb = lambda n, shape, dt=F32: ctx.enter_context(nc.sbuf_tensor(n, shape, dt))
        wsem = stage_sems(ctx, nc, "keysw", ["zero", "z_ps", "in_", "dve", "done", "out", "back"])
        sem = loop_sems(k.loop_sems, OPERAND + ["xt_in", "v_ps", "v", "c_ps", "clamp", "phi", "z_ps", "acc", "dve", "spread",
                                                "piv", "swept"])
        a, xt, sq = sb("a_keys", [P, G, T]), sb("xt_keys", [P, DC, T]), sb("sq_keys", [64, G, T])
        v = sb("v_e", [P, SUB, D])
        cl, phi = sb("cl_e", [P, 2, H * M]), sb("phi_e", [P, 2, H * M])
        w = sb("w_inv", [P, 8, M])
        u, spread = sb("u_inv", [P, 8, M]), sb("spread_now", [P, P])
        rd, sc, col = sb("rd_inv", [P, 1]), sb("sc_inv", [P, 8]), sb("col_inv", [P, M])
        own = k.own[:].rearrange("p (c j) -> p c j", j=8)
        with nc.Block() as block:
            @block.vector
            def _(dve):
                dve.memset(acc[:], 0.0).then_inc(wsem["zero"], 1)
                dve.memset(a[OROW:LROWS], 1.0).then_inc(wsem["zero"], 1)

            @block.gpsimd
            def _(pool):
                pool.memset(winv[:], 0.0).then_inc(wsem["zero"], 1)
                pool.wait_ge(wsem["zero"], 3)

            @block.sync
            def _(sp):
                sp.dma_start(w[:], scr.w.rearrange("h (c j) i -> (h c) j i", j=8)).then_inc(wsem["in_"], 16)
                sp.wait_ge(wsem["in_"], 16)

            @block.tensor
            def _(pe):
                pe.wait_ge(wsem["zero"], 3)
                pe.matmul(ps[:, ZP, :], acc[:, 0:P], acc[:, 0:T], start=True, stop=True).then_inc(wsem["z_ps"], 1)
                pe.wait_ge(wsem["z_ps"], 1)

        def step(i, start, features):
            with nc.Block() as block:
                @block.sync
                def _(sp):
                    if start:
                        sp.dma_start(xt[:], rows_of(k, i + 1)).then_inc(sem["xt_in"], 16)

                @block.tensor
                def _(pe):
                    def half_keys(c):
                        if c:
                            pe.wait_ge(sem["a_in"], 2)
                        for ic in range(DC):
                            mm = pe.matmul(ps[:, KP, :], k.wk1[:, ic, c * P:(c + 1) * P], rows_of(k, i + 1)[:, ic, :],
                                           start=(ic == 0), stop=(ic == DC - 1))
                        mm.then_inc(sem["a_ps"], 1)

                    def values():
                        pe.wait_ge(sem["xt_in"], 16)
                        if features:
                            pe.wait_ge(sem["clamp"], 3)
                        for s in range(SUB):
                            for ic in range(DC):
                                mm = pe.matmul(ps[:, CP + s // 2, (s % 2) * D:(s % 2 + 1) * D], xt[:, ic, s * P:(s + 1) * P],
                                               k.wv1[:, ic, :], start=(ic == 0), stop=(ic == DC - 1))
                        mm.then_inc(sem["v_ps"], 1)

                    def distances(s):
                        if s >= 2:
                            pe.wait_ge(sem["clamp"], s - 1)
                        for g in range(G):
                            mm = pe.matmul(ps[:, CP + 2 * (s % 2) + g // 2, (g % 2) * D:(g % 2 + 1) * D],
                                           a[0:LROWS, g, s * P:(s + 1) * P], k.la[0:LROWS, g].rearrange("p j m -> p (j m)"),
                                           start=True, stop=True)
                        mm.then_inc(sem["c_ps"], 1)

                    def products(s):
                        pe.wait_ge(sem["phi"], s + 1)
                        for r in range(PAIRS):
                            mm = pe.matmul(ps[32 * (r % 4):32 * (r % 4) + 32, ZP, r // 4 * P:(r // 4 + 1) * P], v[:, s, 32 * r:32 * r + 32],
                                           phi[:, s % 2, r * P:(r + 1) * P], start=False, stop=True, tile_position=(0, 32 * (r % 4)),
                                           skip_group_check=True)
                        mm.then_inc(sem["z_ps"], 1)

                    for p in range(SWEEPS):
                        if features:
                            if p:
                                pe.wait_ge(sem["swept"], p)
                            else:
                                pe.wait_ge(sem["spread"], 1)
                            pe.matmul(ps[:, PV, 0:M], spread[:, :], w[:, p, :], start=True, stop=True).then_inc(sem["piv"], 1)
                        for piece in KEY_STEPS[p]:
                            if piece[0] == "D" and features:
                                distances(int(piece[1]))
                            if piece[0] == "Z" and features:
                                products(int(piece[1]))
                            if piece[0] == "K" and start:
                                half_keys(int(piece[1]))
                            if piece[0] == "V" and start:
                                values()
                            if piece[0] == "N" and start:
                                operand_norms(pe, k, ps, sq, sem, KP)

                @block.vector
                def _(dve):
                    ch = Chain(dve, sem["dve"])

                    def sweep(p):
                        pivot = i * SWEEPS + p
                        dve.wait_ge(sem["piv"], p + 1)
                        pc = ps[:, PV, 0:M]
                        ch.step(dve.reciprocal(rd[:], ps[:, PV, bass.ds(pivot, 1)]))
                        ch.step(dve.tensor_tensor(sc[:], w[:, :, bass.ds(pivot, 1)].rearrange("p j o -> p (j o)"),
                                                  own[:, bass.ds(pivot, 1), :].rearrange("p o j -> p (o j)"), ALU.subtract))
                        ch.step(dve.tensor_tensor(col[:], pc, k.unit[:, bass.ds(i * -SWEEPS + (M - 1 - p), M)], ALU.subtract))
                        ch.wait()
                        ch.link(dve.tensor_scalar(sc[:], sc[:], rd[:, 0:1], None, ALU.mult))
                        ch.link(dve.tensor_tensor(u[:], bc(sc[:], 2, [P, 8, M]), bc(col[:], 1, [P, 8, M]), ALU.mult))
                        dve.tensor_tensor(w[:], w[:], u[:], ALU.subtract).then_inc(sem["swept"], 1)
                        dve.wait_ge(sem["swept"], p + 1)

                    if features:
                        dve.tensor_copy(spread[:], k.spread[:, bass.ds(i, 1), :].rearrange("p o n -> p (o n)")).then_inc(sem["spread"], 1)
                    for p in range(SWEEPS):
                        if features:
                            sweep(p)
                    if start:
                        dve.wait_ge(sem["v_ps"], 1)
                        if features:
                            dve.wait_ge(sem["z_ps"], SUB)
                        dve.tensor_tensor(v[:], ps[:, CP:CP + 2, :].rearrange("p b (s n) -> p (b s) n", s=2), bc(k.bv1[:, :], 1, [P, SUB, D]),
                                          ALU.add).then_inc(sem["v"], 1)

                @block.scalar
                def _(act):
                    def shift(c):
                        act.wait_ge(sem["a_ps"], c + 1)
                        if features and c == 0:
                            act.wait_ge(sem["c_ps"], SUB)
                        for h in range(2):
                            act.activation(a[0:64, 2 * c + h, :], ps[64 * h:64 * h + 64, KP, :], ACT.Identity,
                                           bias=k.bk1[64 * h:64 * h + 64, c:c + 1]).then_inc(sem["a_in"], 1)

                    for s in range(SUB + 1):
                        if features:
                            if s < SUB:
                                act.wait_ge(sem["c_ps"], s + 1)
                                if s >= 2:
                                    act.wait_ge(sem["phi"], s - 1)
                                act.activation(cl[:, s % 2].rearrange("p (b n) -> p b n", b=2), ps[:, CP + 2 * (s % 2):CP + 2 * (s % 2) + 2, :],
                                               ACT.Relu).then_inc(sem["clamp"], 1)
                            if s == SUB - 1 and start:
                                shift(0)
                            if s > 0:
                                act.wait_ge(sem["clamp"], s)
                                if s > 2:
                                    act.wait_ge(sem["z_ps"], s - 2)
                                    act.wait_ge(sem["acc"], s - 2)
                                act.activation(phi[:, (s - 1) % 2], cl[:, (s - 1) % 2], ACT.Exp, scale=k.negt[:, 0:1]).then_inc(sem["phi"], 1)
                    if start:
                        if not features:
                            shift(0)
                        shift(1)
                        act.wait_ge(sem["a_in"], G)
                        act.activation(sq[:], a[0:64], ACT.Square).then_inc(sem["sq"], 1)
                        act.wait_ge(sem["an_ps"], 1)
                        for g in range(G):
                            act.activation(a[NROW:NROW + 32, g, :], ps[32 * g:32 * g + 32, KP, :], ACT.Copy).then_inc(sem["an_in"], 1)

                @block.gpsimd
                def _(pool):
                    for s in range(SUB):
                        if features:
                            pool.wait_ge(sem["phi"], s + 1)
                            pool.tensor_tensor(acc[:], acc[:], phi[:, s % 2], ALU.add).then_inc(sem["acc"], 1)
                            pool.wait_ge(sem["acc"], s + 1)
            nc.all_engine_barrier(sems_to_clear=cleared(sem))

        step(-1, start=True, features=False)
        with nc.Fori(0, NT - 1) as i:
            step(i, start=True, features=True)
        step(NT - 1, start=False, features=True)
        with nc.Block() as block:
            @block.vector
            def _(dve):
                dve.scalar_tensor_tensor(out=w[:], in0=own.rearrange("p i j -> p j i"), scalar=2.0, in1=w[:],
                                         op0=ALU.mult, op1=ALU.subtract).then_inc(wsem["done"], 1)

            @block.sync
            def _(sp):
                sp.wait_ge(wsem["done"], 1)
                sp.dma_start(scr.wi.rearrange("h (c j) i -> (h c) j i", j=8), w[:]).then_inc(wsem["out"], 16)
                sp.wait_ge(wsem["out"], 16)
                wv = scr.wi.rearrange("(r two) a b -> two a r b", two=2)
                for two in range(2):
                    sp.dma_start(winv[64 * two:64 * two + 64, :, 64 * two:64 * two + 64], wv[two]).then_inc(wsem["back"], 16)
                sp.wait_ge(wsem["back"], 32)


def solve(nc, io, k, ps, winv, zt, acc):
    with ExitStack() as ctx:
        sb = lambda n, shape, dt=F32: ctx.enter_context(nc.sbuf_tensor(n, shape, dt))
        sem = stage_sems(ctx, nc, "solve", ["own", "zt", "s_ps", "z_ps", "z", "y_ps", "y"])
        own = sb("own_s", [P, 2, M])
        z = sb("z_s", [P, PAIRS, 2 * DH + 2])
        with nc.Block() as block:
            @block.vector
            def _(dve):
                dve.tensor_reduce(own[:], k.headmask[:].rearrange("p (q a) m -> p a m q", a=2), AX, ALU.add).then_inc(sem["own"], 1)
                dve.wait_ge(sem["own"], 1)
                dve.tensor_tensor(zt[:].rearrange("p c (a m) -> p c a m", m=M), ps[:, 6, 0:2 * P].rearrange("p (c a m) -> p c a m", c=2, m=M),
                                  bc(own[:], 1, [P, 2, 2, M]), ALU.mult).then_inc(sem["zt"], 1)
                dve.wait_ge(sem["z_ps"], 1)
                dve.tensor_copy(z[:, :, 0:2 * DH], ps[:, 0, 0:2 * P].rearrange("p (r n) -> p r n", n=2 * DH)).then_inc(sem["z"], 1)
                dve.wait_ge(sem["s_ps"], 1)
                dve.tensor_tensor(z[:, :, 2 * DH:], bc(ps[:, 2, 0:PAIRS], 2, [P, PAIRS, 2]), bc(k.half[:, :], 1, [P, PAIRS, 2]),
                                  ALU.mult).then_inc(sem["z"], 1)
                dve.wait_ge(sem["y_ps"], 1)
                yv = ps[:, 3, 0:PAIRS * 64].rearrange("p (r n) -> p r n", n=64)
                dve.tensor_copy(k.y[:, :, 0, :], yv[:, :, 0:2 * DH]).then_inc(sem["y"], 1)
                for a in range(2):
                    dve.tensor_copy(k.y[:, :, 1, a * DH:(a + 1) * DH], yv[:, :, 2 * DH + a:2 * DH + a + 1].broadcast_to([P, PAIRS, DH]))\
                       .then_inc(sem["y"], 1)

            @block.tensor
            def _(pe):
                for r in range(PAIRS):
                    mm = pe.matmul(ps[:, 2, r:r + 1], acc[:, r * P:(r + 1) * P], k.ones[:, :], start=True, stop=True)
                mm.then_inc(sem["s_ps"], 1)
                pe.wait_ge(sem["zt"], 1)
                for c in range(2):
                    tr = pe.transpose(ps[:, 0, c * P:(c + 1) * P], zt[:, c, :], k.ident[:, :])
                tr.then_inc(sem["z_ps"], 1)
                pe.wait_ge(sem["z"], 2)
                for r in range(PAIRS):
                    mm = pe.matmul(ps[:, 3, r * 64:r * 64 + 2 * DH + 2], winv[:, r, :], z[:, r, :], start=True, stop=True)
                mm.then_inc(sem["y_ps"], 1)


def landmarks(nc, io, k, ps, scr):
    with ExitStack() as ctx:
        sb = lambda n, shape, dt=F32: ctx.enter_context(nc.sbuf_tensor(n, shape, dt))
        winv = sb("winv", [P, PAIRS, P])
        zt, acc = sb("zt", [P, 2, P]), sb("acc", [P, H * M])
        with ExitStack() as inner:
            lk = inner.enter_context(nc.sbuf_tensor("lk", [P, G, M], F32))
            landmark_operands(nc, io, k, ps, k.la, lk, scr)
        keys(nc, io, k, ps, scr, winv, zt, acc)
        solve(nc, io, k, ps, winv, zt, acc)



OUT_PROJECT, WEIGH, START_QUERIES, OUT_NORM = 3, 3, 5, 5


def queries(nc, io, k, ps, out):
    BP, QP, CP, YP = 0, 2, 4, 6
    with ExitStack() as ctx:
        sb = lambda n, shape, dt=F32: ctx.enter_context(nc.sbuf_tensor(n, shape, dt))
        wsem = stage_sems(ctx, nc, "qryw", ["one"])
        sem = loop_sems(k.loop_sems, OPERAND + ["c_ps", "exp", "phi", "n_ps", "on", "dve", "pool", "xb", "o_ps", "var",
                                             "rstd", "xn", "xt_ps", "xt", "f_ps", "res", "out", "off"])
        a, sq = sb("a_q", [P, G, T]), sb("sq_q", [64, G, T])
        phi = sb("phi_q", [P, PAIRS, T])
        nr, ot = sb("nr_q", [P, DC, T]), sb("ot_q", [P, DC, T])
        xb, x3, xn, x4 = (sb(f"{n}_q", [P, SUB, D]) for n in ("xb", "x3", "xn", "x4"))
        st, mv, rstd = sb("st_q", [P, SUB, 6]), sb("mv_q", [P, SUB, 2]), sb("rstd_q", [P, SUB])
        off = sb("off_q", [P, SUB])
        xt4 = sb("xt4_q", [P, DC, T])
        with nc.Block() as block:
            @block.vector
            def _(dve):
                dve.memset(a[OROW:LROWS], 1.0).then_inc(wsem["one"], 1)
                dve.wait_ge(wsem["one"], 1)

        def half(bank, s):
            return ps[:, bank + s // 2, (s % 2) * D:(s % 2 + 1) * D]

        def step(i, start, features, output, store):
            with nc.Block() as block:
                @block.sync
                def _(sp):
                    if store:
                        sp.dma_start(out.rearrange("o (i s p) d -> (o i) p s d", s=SUB, p=P)[i - 2], x4[:]).then_inc(sem["out"], 16)
                        sp.wait_ge(sem["out"], 16)

                @block.tensor
                def _(pe):
                    def project_out():
                        for s in range(SUB):
                            for c in range(DC):
                                mm = pe.matmul(half(BP, s), ot[:, c, s * P:(s + 1) * P], k.wo1[:, c, :], start=(c == 0), stop=(c == DC - 1))
                            mm.then_inc(sem["o_ps"], 1)

                    def linear():
                        pe.wait_ge(sem["xt"], 1)
                        for s in range(SUB):
                            for c in range(DC):
                                mm = pe.matmul(half(BP, s), xt4[:, c, s * P:(s + 1) * P], k.wf[:, c, :], start=(c == 0), stop=(c == DC - 1))
                            mm.then_inc(sem["f_ps"], 1)

                    def weigh(c):
                        pe.wait_ge(sem["phi"], 4 * c + 4)
                        for w in range(2):
                            for r in range(4 * c, 4 * c + 4):
                                mm = pe.matmul(ps[32 * (r % 4):32 * (r % 4) + 32, (YP, CP)[c] + w, :], k.y[:, r, w, :], phi[:, r, :],
                                               start=True, stop=True, tile_position=(0, 32 * (r % 4)), skip_group_check=True)
                        mm.then_inc(sem["n_ps"], 1)

                    for r in range(PAIRS):
                        if features:
                            if r >= 2:
                                pe.wait_ge(sem["exp"], r - 1)
                            pe.matmul(ps[:, CP + r % 2, :], k.la[0:LROWS, r // 2, 2 * (r % 2):2 * (r % 2) + 2].rearrange("p j m -> p (j m)"),
                                      a[0:LROWS, r // 2, :], start=True, stop=True).then_inc(sem["c_ps"], 1)
                        if output and r == OUT_PROJECT:
                            project_out()
                        if features and r == WEIGH:
                            weigh(0)
                        if start and r == START_QUERIES:
                            operand_project(pe, k, ps, k.wq1, rows_of(k, i + 1), sem, QP)
                    if output:
                        transpose_tile(pe, ps, BP, xn, k.ident, sem["xn"], 0, sem["xt_ps"])
                    if features:
                        weigh(1)
                    if output:
                        linear()
                    if start:
                        operand_norms(pe, k, ps, sq, sem, QP)

                @block.vector
                def _(dve):
                    ch = Chain(dve, sem["dve"])

                    def normalise(c):
                        dve.wait_ge(sem["n_ps"], c + 1)
                        ch.link(dve.tensor_scalar(nr[:, c], ps[:, (YP, CP)[c] + 1, :], NORM_MIN, None, ALU.max))
                        ch.link(dve.reciprocal(nr[:, c], nr[:, c]))
                        if output and c == 0:
                            dve.wait_ge(sem["o_ps"], SUB)
                        dve.tensor_tensor(ot[:, c], ps[:, (YP, CP)[c], :], nr[:, c], ALU.mult).then_inc(sem["on"], 1)

                    for r in range(PAIRS):
                        if features:
                            dve.wait_ge(sem["exp"], r + 1)
                            dve.tensor_scalar(phi[:, r], phi[:, r], k.bounds[:, 0:1], k.bounds[:, 1:2], ALU.min, ALU.max).then_inc(sem["phi"], 1)
                        if output and r == OUT_PROJECT:
                            dve.wait_ge(sem["xb"], 1)
                            for s in range(SUB):
                                dve.wait_ge(sem["o_ps"], 2 * (s // 2) + 2)
                                ch.step(dve.tensor_tensor(x3[:, s, :], xb[:, s, :], half(BP, s), ALU.add))
                            ch.wait()
                            ln_stats(dve, ch, x3, st, mv, sem["var"])
                        if features and r == WEIGH:
                            normalise(0)
                    if features:
                        normalise(1)
                    if output:
                        if store:
                            dve.wait_ge(sem["out"], 16)
                        for s in range(SUB):
                            dve.wait_ge(sem["f_ps"], 2 * (s // 2) + 2)
                            dve.tensor_tensor(x4[:, s, :], x3[:, s, :], half(BP, s), ALU.add).then_inc(sem["res"], 1)

                @block.gpsimd
                def _(pool):
                    ch = Chain(pool, sem["pool"])
                    if output:
                        pool.tensor_tensor(xb[:], k.x2[:, bass.ds((i - 1) * SUB, SUB), :], bc(k.bo1[:, :], 1, [P, SUB, D]), ALU.add)\
                            .then_inc(sem["xb"], 1)
                        ln_rstd(pool, ch, mv, rstd, k.neghalf, sem["var"], SUB, sem["rstd"])
                        ln_offset(pool, ch, mv, rstd, off, sem["rstd"], 1, sem["off"])

                @block.scalar
                def _(act):
                    for r in range(PAIRS):
                        if features:
                            act.wait_ge(sem["c_ps"], r + 1)
                            act.activation(phi[:, r], ps[:, CP + r % 2, :], ACT.Exp, scale=k.negt[:, 0:1]).then_inc(sem["exp"], 1)
                        if output and r == OUT_NORM:
                            ln_affine(act, lambda s: x3[:, s, :], xn, rstd, off, sem["off"], 1, sem["xn"])
                    if output:
                        act.wait_ge(sem["xt_ps"], 1)
                        act.activation(xt4[:], ps[:, BP:BP + 2, :], ACT.Copy).then_inc(sem["xt"], 1)
                    if start:
                        if features:
                            act.wait_ge(sem["c_ps"], PAIRS)
                        operand_act(act, ps, a, k.bq1, sq, sem, QP, QP)
            nc.all_engine_barrier(sems_to_clear=cleared(sem))

        step(-1, start=True, features=False, output=False, store=False)
        step(0, start=True, features=True, output=False, store=False)
        step(1, start=True, features=True, output=True, store=False)
        with nc.Fori(2, NT - 1) as i:
            step(i, start=True, features=True, output=True, store=True)
        step(NT - 1, start=False, features=True, output=True, store=True)
        step(NT, start=False, features=False, output=True, store=True)
        step(NT + 1, start=False, features=False, output=False, store=True)



class Names:
    pass


def build(nc, io, out, stages=("project", "attend", "mix", "landmarks", "queries")):
    scr = Names()
    scr.q = nc.dram_tensor("q_parts", (3, D, N), BF16, kind="Internal").ap()
    scr.k = nc.dram_tensor("k_parts", (3, D, N), BF16, kind="Internal").ap()
    scr.v = nc.dram_tensor("v_ones", (N, H * 2 * DH), F32, kind="Internal").ap()
    scr.o = nc.dram_tensor("attn_sums", (H * 2 * DH, N), F32, kind="Internal").ap()
    scr.r = nc.dram_tensor("weight_sums_inverse", (NT, H, T), F32, kind="Internal").ap()
    scr.w = nc.dram_tensor("kernel_matrix", (H, M, M), F32, kind="Internal").ap()
    scr.wi = nc.dram_tensor("kernel_inverse", (H, M, M), F32, kind="Internal").ap()
    with ExitStack() as ctx:
        sb = lambda n, shape, dt=F32: ctx.enter_context(nc.sbuf_tensor(n, shape, dt))
        ps = ctx.enter_context(nc.psum_tensor("ps", [P, 8, T], F32))
        k = Names()
        k.loop_sems = [ctx.enter_context(nc.semaphore(f"loop_{i}")) for i in range(LOOP_SEMS)]
        assert [s.num for s in k.loop_sems] == list(range(k.loop_sems[0].num, k.loop_sems[0].num + LOOP_SEMS))
        k.wq1, k.wk1, k.wv1, k.wo1, k.wf = (sb(n, [P, DC, D]) for n in ("wq1", "wk1", "wv1", "wo1", "wf"))
        k.gate_w = sb("gate_wt", [P, DC, E])
        k.gate_b = sb("gate_bias", [P, E])
        k.bq1, k.bk1 = sb("bq1", [P, DC]), sb("bk1", [P, DC])
        k.bv1, k.bo1 = sb("bv1", [P, D]), sb("bo1", [P, D])
        k.negt = sb("negt", [P, 1])
        k.bounds = sb("bounds", [P, 2])
        k.ident, k.identb = sb("ident", [P, P]), sb("identb", [P, P], BF16)
        k.mask_kq, k.mask_qk = sb("mask_kq", [P, P], BF16), sb("mask_qk", [P, P], BF16)
        k.neghalf, k.ones = sb("neghalf", [P, SUB]), sb("ones", [P, 1])
        k.quarter = sb("quarter", [64, 1])
        k.half = sb("half", [P, 2])
        k.sel = sb("sel", [64, 32])
        k.blk2 = sb("blk2", [64, G, M])
        k.blk1 = sb("blk1", [P, G, M])
        k.headmask = sb("headmask", [P, 8, M])
        k.regi = sb("regi", [M, M])
        k.before = sb("before", [P, E, E])
        k.spread = sb("spread", [P, 8, P])
        k.unit = sb("unit", [P, 2 * M - 1])
        k.own = sb("own", [P, 8 * 8 * 8])
        k.idx, k.tok = sb("idx_f", [P, M]), sb("tok", [P, SUB])
        setup(nc, io, k, ps)
        if "project" in stages:
            project(nc, io, k, ps, scr)
        if "attend" in stages:
            attend(nc, io, k, ps, scr)
        if "mix" in stages:
            k.x2, k.xn3t = sb("x2", [P, N // P, D]), sb("xn3t", [P, DC, N])
            k.lxt = sb("lxt", [P, DC, M])
            mix(nc, io, k, ps, scr)
        if "landmarks" in stages:
            k.la, k.y = sb("la", [P, G, G, M]), sb("y", [P, PAIRS, 2, 32])
            landmarks(nc, io, k, ps, scr)
        if "queries" in stages:
            queries(nc, io, k, ps, out)
    return scr


_INS = ["L0_attn_x", "L0_attn_Wq", "L0_attn_Wk", "L0_attn_Wv", "L0_attn_Wout", "L0_ffn_gate_w", "L0_ffn_gate_b",
        "L0_ffn_expert_w", "L0_ffn_expert_b", "L1_attn_Wq", "L1_attn_bq", "L1_attn_Wk", "L1_attn_bk", "L1_attn_Wv",
        "L1_attn_bv", "L1_attn_Wo", "L1_attn_bo", "L1_attn_temperature", "L1_attn_landmark_idx", "L1_ffn_weight"]


def kernel(**inputs):
    import numpy as _np
    import concourse.bacc as _bacc
    from concourse import mybir as _mybir
    from concourse.bass_utils import run_bass_kernel_spmd as _run

    nc = _bacc.Bacc("TRN2", target_bir_lowering=False, num_devices=1)
    arrays, io = {}, {}
    for name in _INS:
        a = _np.ascontiguousarray(inputs[name])
        if a.ndim == 0:
            a = a.reshape(1)
        arrays[f"in_{name}"] = a
        io[name] = nc.dram_tensor(f"in_{name}", a.shape, _mybir.dt.from_np(a.dtype), kind="ExternalInput").ap()
    out = nc.dram_tensor("out_x", (1, N, D), F32, kind="ExternalOutput").ap()
    build(nc, io, out)
    r = _run(nc, [arrays], core_ids=[0])
    return r.results[0]["out_x"]
```
